# Optimizing a Trainium2 kernel written in Bass

```python
import numpy as np
import jax
import jax.numpy as jnp

def _softmax(x, axis=-1):
    return jax.nn.softmax(x, axis=axis)

def _gelu(x):
    return jax.nn.gelu(x, approximate=True)

def _silu(x):
    return jax.nn.silu(x)

def _sigmoid(x):
    return jax.nn.sigmoid(x)

def _layernorm(x, axis=-1, eps=1e-05):
    m = jnp.mean(x, axis=axis, keepdims=True)
    v = jnp.var(x, axis=axis, keepdims=True)
    return (x - m) / jnp.sqrt(v + eps)

def _scatter_add(tgt, idx, src, axis=0):
    return tgt.at[idx].add(src)

def _segment_sum(src, seg, n):
    return jax.ops.segment_sum(src, seg, n)
kernel_name = 'mk_xattn_ffn_d1_seqx_r4_1d759d'

def setup_inputs(seed: int=0):
    np.random.seed(seed)
    _w = jnp.asarray

    def _rec_inputs():
        import jax
        import jax.numpy as jnp
        _rk = jax.random.key(seed)
        x = 7.22e-05 + 1 * jax.random.normal(jax.random.fold_in(_rk, 1), (8, 512, 256), jnp.float32)
        _lenS = 512 - jax.random.randint(jax.random.fold_in(_rk, 7), (8,), 0, max(1, 512 // 4) + 1, jnp.int32)
        _lenS2 = 1601 - jax.random.randint(jax.random.fold_in(_rk, 8), (8,), 0, max(1, 1601 // 4) + 1, jnp.int32)
        _ctx_1024P = jax.random.normal(jax.random.fold_in(_rk, 11), (8, 16, 256), jnp.float32)
        _ctx_1024c = jax.random.dirichlet(jax.random.fold_in(_rk, 511), 0.3 * jnp.ones((16,), jnp.float32), (8, 1601))
        _ctx_1024t = jnp.einsum('bsk,bkd->bsd', _ctx_1024c, _ctx_1024P)
        _ctx_1024t = _ctx_1024t * jax.lax.rsqrt(jnp.mean(jnp.square(_ctx_1024t)) + 1e-12) * 0.953939
        ctx_1024 = 4.13588e-05 + 0.999923 * (_ctx_1024t + 0.3 * jax.random.normal(jax.random.fold_in(_rk, 611), (8, 1601, 256), jnp.float32))
        _validS = jnp.arange(512)[None, :] < _lenS[:, None]
        _validS2 = jnp.arange(1601)[None, :] < _lenS2[:, None]
        _causal = jnp.tril(jnp.ones((512, 512), dtype=bool))
        mask_Bx1xSxS2_bf1 = jnp.ones((8, 1, 512, 1601), dtype=bool)
        return (x, ctx_1024, mask_Bx1xSxS2_bf1)
    x, ctx_1024, mask_Bx1xSxS2_bf1 = _rec_inputs()

    def _L0_xattn_setup():
        import jax, jax.numpy as jnp
        import numpy as np
        D_MODEL = 256
        NUM_HEADS = 16
        D_K = D_MODEL // NUM_HEADS
        B, S = (4, 512)

        def _split_heads(x):
            b, s, _ = x.shape
            return x.reshape(b, s, NUM_HEADS, D_K).transpose(0, 2, 1, 3)
        key = jax.random.key(seed)
        ks = jax.random.split(key, 11)
        scale = 1.0 / np.sqrt(D_MODEL)
        inp = {'query': jax.random.normal(ks[0], (B, S, D_MODEL), dtype=jnp.float32), 'key': jax.random.normal(ks[1], (B, S, D_MODEL), dtype=jnp.float32), 'value': jax.random.normal(ks[2], (B, S, D_MODEL), dtype=jnp.float32), 'mask': jnp.ones((B, 1, S, S), dtype=bool), 'W_q': jax.random.normal(ks[3], (D_MODEL, D_MODEL), dtype=jnp.float32) * scale, 'b_q': jax.random.normal(ks[4], (D_MODEL,), dtype=jnp.float32) * 0.01, 'W_k': jax.random.normal(ks[5], (D_MODEL, D_MODEL), dtype=jnp.float32) * scale, 'b_k': jax.random.normal(ks[6], (D_MODEL,), dtype=jnp.float32) * 0.01, 'W_v': jax.random.normal(ks[7], (D_MODEL, D_MODEL), dtype=jnp.float32) * scale, 'b_v': jax.random.normal(ks[8], (D_MODEL,), dtype=jnp.float32) * 0.01, 'W_o': jax.random.normal(ks[9], (D_MODEL, D_MODEL), dtype=jnp.float32) * scale, 'b_o': jax.random.normal(ks[10], (D_MODEL,), dtype=jnp.float32) * 0.01}
        return inp
    _L0_xattn_all = _L0_xattn_setup()
    _L0_xattn_in = {k: v for k, v in _L0_xattn_all.items() if k in ('W_q', 'b_q', 'W_k', 'b_k', 'W_v', 'b_v', 'W_o', 'b_o')}
    del _L0_xattn_all

    def _L0_ffn_setup():
        import jax, jax.numpy as jnp
        import numpy as np
        DIM = 256
        HEADS = 16
        HD = DIM // HEADS
        M = 64
        E = 4
        K = 2
        HID = 512
        MID = 512
        LB = 0.01
        EPS = 1.1920929e-07

        def _rms(x, w):
            return x * jax.lax.rsqrt(jnp.mean(x * x, axis=-1, keepdims=True) + EPS) * w

        def _gelu(x):
            return jax.nn.gelu(x, approximate=False)
        key = jax.random.key(seed)
        ks = jax.random.split(key, 20)
        d = DIM
        w = lambda k, s: jax.random.normal(k, s, jnp.float32) * 0.02
        return {'x': jax.random.normal(ks[0], (4, 256, d), jnp.float32), 'n1_w': jnp.ones((d,), jnp.float32), 'n2_w': jnp.ones((d,), jnp.float32), 'wq': w(ks[1], (d, d)), 'wk': w(ks[2], (d, d)), 'wv': w(ks[3], (d, d)), 'wo': w(ks[4], (d, d)), 'qn_w': jnp.ones((HD,), jnp.float32), 'kn_w': jnp.ones((HD,), jnp.float32), 'gate_w': w(ks[5], (E, d)), 'e0_up': w(ks[6], (HID, d)), 'e0_down': w(ks[7], (d, HID)), 'e1_w1': w(ks[8], (HID, d)), 'e1_w2': w(ks[9], (HID, d)), 'e1_down': w(ks[10], (d, HID)), 'e2_l1': w(ks[11], (MID, d)), 'e2_l2': w(ks[12], (HID, MID)), 'e2_l3': w(ks[13], (MID, HID)), 'e2_l4': w(ks[14], (d, MID)), 'e3_down': w(ks[15], (d, d)), 'e3_up': w(ks[16], (HID, d)), 'e3_out': w(ks[17], (d, HID))}
    _L0_ffn_all = _L0_ffn_setup()
    _L0_ffn_in = {k: v for k, v in _L0_ffn_all.items() if k in ('n1_w', 'n2_w', 'wq', 'wk', 'wv', 'wo', 'qn_w', 'kn_w', 'gate_w', 'e0_up', 'e0_down', 'e1_w1', 'e1_w2', 'e1_down', 'e2_l1', 'e2_l2', 'e2_l3', 'e2_l4', 'e3_down', 'e3_up', 'e3_out')}
    del _L0_ffn_all
    return {'x': x, 'ctx_1024': ctx_1024, 'mask_Bx1xSxS2_bf1': mask_Bx1xSxS2_bf1, 'L0_xattn_W_q': _L0_xattn_in['W_q'], 'L0_xattn_b_q': _L0_xattn_in['b_q'], 'L0_xattn_W_k': _L0_xattn_in['W_k'], 'L0_xattn_b_k': _L0_xattn_in['b_k'], 'L0_xattn_W_v': _L0_xattn_in['W_v'], 'L0_xattn_b_v': _L0_xattn_in['b_v'], 'L0_xattn_W_o': _L0_xattn_in['W_o'], 'L0_xattn_b_o': _L0_xattn_in['b_o'], 'L0_ffn_n1_w': _L0_ffn_in['n1_w'], 'L0_ffn_n2_w': _L0_ffn_in['n2_w'], 'L0_ffn_wq': _L0_ffn_in['wq'], 'L0_ffn_wk': _L0_ffn_in['wk'], 'L0_ffn_wv': _L0_ffn_in['wv'], 'L0_ffn_wo': _L0_ffn_in['wo'], 'L0_ffn_qn_w': _L0_ffn_in['qn_w'], 'L0_ffn_kn_w': _L0_ffn_in['kn_w'], 'L0_ffn_gate_w': _L0_ffn_in['gate_w'], 'L0_ffn_e0_up': _L0_ffn_in['e0_up'], 'L0_ffn_e0_down': _L0_ffn_in['e0_down'], 'L0_ffn_e1_w1': _L0_ffn_in['e1_w1'], 'L0_ffn_e1_w2': _L0_ffn_in['e1_w2'], 'L0_ffn_e1_down': _L0_ffn_in['e1_down'], 'L0_ffn_e2_l1': _L0_ffn_in['e2_l1'], 'L0_ffn_e2_l2': _L0_ffn_in['e2_l2'], 'L0_ffn_e2_l3': _L0_ffn_in['e2_l3'], 'L0_ffn_e2_l4': _L0_ffn_in['e2_l4'], 'L0_ffn_e3_down': _L0_ffn_in['e3_down'], 'L0_ffn_e3_up': _L0_ffn_in['e3_up'], 'L0_ffn_e3_out': _L0_ffn_in['e3_out']}

def reference(x, ctx_1024, mask_Bx1xSxS2_bf1, L0_xattn_W_q, L0_xattn_b_q, L0_xattn_W_k, L0_xattn_b_k, L0_xattn_W_v, L0_xattn_b_v, L0_xattn_W_o, L0_xattn_b_o, L0_ffn_n1_w, L0_ffn_n2_w, L0_ffn_wq, L0_ffn_wk, L0_ffn_wv, L0_ffn_wo, L0_ffn_qn_w, L0_ffn_kn_w, L0_ffn_gate_w, L0_ffn_e0_up, L0_ffn_e0_down, L0_ffn_e1_w1, L0_ffn_e1_w2, L0_ffn_e1_down, L0_ffn_e2_l1, L0_ffn_e2_l2, L0_ffn_e2_l3, L0_ffn_e2_l4, L0_ffn_e3_down, L0_ffn_e3_up, L0_ffn_e3_out):
    import jax
    import jax.numpy as jnp

    def _L0_xattn_ref(query, key, value, mask, W_q, b_q, W_k, b_k, W_v, b_v, W_o, b_o):
        import jax, jax.numpy as jnp
        import numpy as np
        D_MODEL = 256
        NUM_HEADS = 16
        D_K = D_MODEL // NUM_HEADS
        B, S = (4, 512)

        def _split_heads(x):
            b, s, _ = x.shape
            return x.reshape(b, s, NUM_HEADS, D_K).transpose(0, 2, 1, 3)
        q = _split_heads(query @ W_q.T + b_q)
        k = _split_heads(key @ W_k.T + b_k)
        v = _split_heads(value @ W_v.T + b_v)
        scores = jnp.einsum('bhqd,bhkd->bhqk', q, k) / jnp.sqrt(jnp.float32(D_K))
        scores = jnp.where(mask, scores, jnp.float32(-1000000000.0))
        attn = jax.nn.softmax(scores, axis=-1)
        out = jnp.einsum('bhqk,bhkd->bhqd', attn, v)
        out = out.transpose(0, 2, 1, 3).reshape(query.shape[0], -1, NUM_HEADS * D_K)
        return out @ W_o.T + b_o

    def _L0_ffn_ref(x, n1_w, n2_w, wq, wk, wv, wo, qn_w, kn_w, gate_w, e0_up, e0_down, e1_w1, e1_w2, e1_down, e2_l1, e2_l2, e2_l3, e2_l4, e3_down, e3_up, e3_out):
        import jax, jax.numpy as jnp
        import numpy as np
        DIM = 256
        HEADS = 16
        HD = DIM // HEADS
        M = 64
        E = 4
        K = 2
        HID = 512
        MID = 512
        LB = 0.01
        EPS = 1.1920929e-07

        def _rms(x, w):
            return x * jax.lax.rsqrt(jnp.mean(x * x, axis=-1, keepdims=True) + EPS) * w

        def _gelu(x):
            return jax.nn.gelu(x, approximate=False)
        B, T, C = x.shape
        h = _rms(x, n1_w)
        heads = lambda w_: (h @ w_.T).reshape(B, T, HEADS, HD).transpose(0, 2, 1, 3)
        q = _rms(heads(wq), qn_w)
        k = _rms(heads(wk), kn_w)
        v = heads(wv)
        scores = jnp.einsum('bhqd,bhkd->bhqk', q, k) * HD ** (-0.5)
        causal = jnp.tril(jnp.ones((T, T), bool))
        scores = jnp.where(causal[None, None], scores, -jnp.inf)
        attn = jax.nn.softmax(scores, axis=-1)
        ao = jnp.einsum('bhqk,bhkd->bhqd', attn, v).transpose(0, 2, 1, 3).reshape(B, T, C) @ wo.T
        ao = ao.at[:, :, :M].set(0.0)
        x = x + ao
        xf = _rms(x, n2_w).reshape(-1, C)
        N = xf.shape[0]
        logits = jnp.nan_to_num(xf @ gate_w.T)
        probs = jax.nn.softmax(logits, axis=-1)
        topv, topi = jax.lax.top_k(probs, K)
        topv = topv / (topv.sum(-1, keepdims=True) + 1e-08)
        wts = jnp.zeros((N, E), x.dtype).at[jnp.arange(N)[:, None], topi].add(topv)
        o0 = _gelu(xf @ e0_up.T) @ e0_down.T
        o1 = jax.nn.silu(xf @ e1_w1.T) * (xf @ e1_w2.T) @ e1_down.T
        o2 = _gelu(_gelu(_gelu(xf @ e2_l1.T) @ e2_l2.T) @ e2_l3.T) @ e2_l4.T
        o3 = _gelu(_gelu(xf @ e3_down.T) @ e3_up.T) @ e3_out.T
        moe = wts[:, 0:1] * o0 + wts[:, 1:2] * o1 + wts[:, 2:3] * o2 + wts[:, 3:4] * o3
        moe = moe.reshape(B, T, C).at[:, :, :M].set(0.0)
        return x + moe
    x = x + _L0_xattn_ref(_layernorm(x, axis=-1), ctx_1024, ctx_1024, mask_Bx1xSxS2_bf1, L0_xattn_W_q, L0_xattn_b_q, L0_xattn_W_k, L0_xattn_b_k, L0_xattn_W_v, L0_xattn_b_v, L0_xattn_W_o, L0_xattn_b_o)
    x = x + _L0_ffn_ref(_layernorm(x, axis=-1), L0_ffn_n1_w, L0_ffn_n2_w, L0_ffn_wq, L0_ffn_wk, L0_ffn_wv, L0_ffn_wo, L0_ffn_qn_w, L0_ffn_kn_w, L0_ffn_gate_w, L0_ffn_e0_up, L0_ffn_e0_down, L0_ffn_e1_w1, L0_ffn_e1_w2, L0_ffn_e1_down, L0_ffn_e2_l1, L0_ffn_e2_l2, L0_ffn_e2_l3, L0_ffn_e2_l4, L0_ffn_e3_down, L0_ffn_e3_up, L0_ffn_e3_out)
    return x

_drawn_inputs = setup_inputs


def setup_inputs(seed=0):
    import zlib

    import numpy as np

    out = dict(_drawn_inputs(seed))
    spreads = {'L0_ffn_n1_w': (1.0, 0.6),
     'L0_ffn_n2_w': (1.0, 0.6),
     'L0_ffn_qn_w': (1.0, 0.6),
     'L0_ffn_kn_w': (1.0, 0.6)}
    factors = {'L0_xattn_b_q': 8.0,
     'L0_xattn_b_k': 8.0,
     'L0_xattn_b_v': 6.764,
     'L0_xattn_b_o': 6.221,
     'L0_ffn_wq': 8.0,
     'L0_ffn_wk': 8.0,
     'L0_ffn_wv': 2.685,
     'L0_ffn_wo': 2.786,
     'L0_ffn_gate_w': 6.15,
     'L0_ffn_e0_up': 4.867,
     'L0_ffn_e0_down': 4.788,
     'L0_ffn_e1_w1': 8.0,
     'L0_ffn_e1_w2': 8.0,
     'L0_ffn_e1_down': 8.0,
     'L0_ffn_e2_l1': 8.0,
     'L0_ffn_e2_l2': 8.0,
     'L0_ffn_e2_l3': 8.0,
     'L0_ffn_e2_l4': 8.0,
     'L0_ffn_e3_down': 8.0,
     'L0_ffn_e3_up': 8.0,
     'L0_ffn_e3_out': 8.0}
    for name, (base, spread) in spreads.items():
        noise = np.random.default_rng([zlib.crc32(name.encode()), seed]).standard_normal(out[name].shape)
        drawn = base * np.exp(spread * noise) if base else spread * noise
        out[name] = jnp.asarray(drawn.astype(out[name].dtype))
    for name, factor in factors.items():
        out[name] = (out[name] * factor).astype(out[name].dtype)
    return out
```

```python
from contextlib import ExitStack

import concourse.bass as bass
from concourse import mybir

F32 = mybir.dt.float32
BF16 = mybir.dt.bfloat16
I32 = mybir.dt.int32
ALU = mybir.AluOpType
ACT = mybir.ActivationFunctionType
AX = mybir.AxisListType

P = 128
B, S, D = 8, 512, 256
KEYS = 1601
H, DK = 16, 16
HG = 4
NG = H // HG
TT = S // P
KT = D // P
NKT = -(-KEYS // P)
HID = 512
HT = HID // P
ZERO_COLS = 64
DOUT = D - ZERO_COLS
PARTS = 96
ROWS = PARTS + 3
VW = DK + 1
BIG = float(2 ** 30)
LN_EPS = 1e-5
RMS_EPS = 1.1920929e-07
FLT_MAX = 3.4028234e38
CHUNKS = []
for _c in range(4):
    _lo = sum(w for _, w in CHUNKS)
    CHUNKS.append((_lo, -(-(KEYS - _lo) // (4 - _c))))
NCH = len(CHUNKS)

Q_BLOCKS = ((0, 2, 4), (1, 5), (3,))
K_BLOCKS = ((0, 1, 3), (2, 5), (4,))

FFN_W = {}
_at = 0
for _name, _kt, _w in (("e0_up", KT, HID), ("e0_down", HT, DOUT),
                       ("e1_w1", KT, HID), ("e1_w2", KT, HID), ("e1_down", HT, DOUT),
                       ("e2_l1", KT, HID), ("e2_l2", HT, HID), ("e2_l3", HT, HID), ("e2_l4", HT, DOUT),
                       ("e3_down", KT, D), ("e3_up", KT, HID), ("e3_out", HT, DOUT)):
    FFN_W[_name] = (_at, _kt, _w)
    _at += _kt * _w
FFN_WORDS = _at
EXPERT_AT = [FFN_W[n][0] for n in ("e0_up", "e1_w1", "e2_l1", "e3_down")] + [FFN_WORDS]

CROSS_PER_STEP = 6
SELF_PER_STEP = 6


def cross_side_work(g, j):
    units = [(hh, tt, c) for hh in range(HG) for tt in range(TT) for c in range(NCH)]
    work = []
    if g + 1 < NG:
        work += [("max",) + u for u in units[CROSS_PER_STEP * j:CROSS_PER_STEP * (j + 1)]]
        if j == NKT - 2:
            work.append(("negate",))
        if j == NKT - 1:
            work.append(("rows",))
    if j == 4 and g > 0:
        work.insert(0, ("natural",))
    return work


def self_side_work(g, j):
    units = [(hh, tt) for hh in range(HG) for tt in range(TT)]
    work = []
    if g + 1 < NG:
        work += [("max",) + u for u in units[SELF_PER_STEP * j:SELF_PER_STEP * (j + 1)]]
        if j == 2:
            work.append(("negate",))
        if j == 3:
            work.append(("rows",))
    if j == 1 and g > 0:
        work.insert(0, ("natural",))
    return work


M_PREP = TT + NKT + H // 2 + HG * TT * NCH + 2
M_CROSS = (NG - 1) * (HG * TT * NCH + 2) + NG + KT + TT
M_SELF = 2 * TT + 2 * (H // 2) + NG * (HG * TT + 2) + NG + KT + TT
M_FFN = 1 + HT + 4 * TT
M_USES = M_PREP + M_CROSS + M_SELF + M_FFN
S_PREP = KT + KT * NCH
S_CROSS = NG * NKT * HG
S_SELF = KT + NG * TT * HG
S_FFN = KT + HT + HT + 3 * HT + KT + HT
S_USES = S_PREP + S_CROSS + S_SELF + S_FFN
N_M, N_S = 3, 4
assert M_USES % N_M == 0 and S_USES % N_S == 0
PV_STEPS = NG * NKT + NG * TT


def apart(eng, sem):
    eng.sem_inc(sem, 1)


class Ring:

    def __init__(self, eng, banks, full, free, uses, b):
        self.eng, self.banks, self.full, self.free = eng, banks, full, free
        self.base, self.n = b * uses, 0

    def acquire(self):
        self.eng.wait_ge(self.free, self.base + (self.n + 1))
        self.n += 1
        return self.banks[(self.n - 1) % len(self.banks)]

    def take(self):
        self.eng.wait_ge(self.full, self.base + (self.n + 1))
        self.n += 1
        return self.banks[(self.n - 1) % len(self.banks)]

    def wait_released(self, n):
        self.eng.wait_ge(self.free, self.base + (n + len(self.banks)))


class Chain:

    def __init__(self, eng, sem, per_batch, b):
        self.eng, self.sem, self.per, self.base, self.n = eng, sem, per_batch, b * per_batch, 0

    def step(self, ins):
        self.n += 1
        ins.then_inc(self.sem, 1)

    def settle(self):
        self.eng.wait_ge(self.sem, self.base + self.n)

    def __call__(self, ins):
        self.step(ins)
        self.settle()

    def end(self):
        assert self.n == self.per, (self.n, self.per)


DVE_STEPS = 209
POOL_STEPS = 26


def xattn_ffn_kernel(nc, x, ctx_t, mask, w_cross, w_self, rows, bias_k, gate_t, ffn_w, ones, out):
    with ExitStack() as ctx:
        def sb(name, shape, dt=F32):
            return ctx.enter_context(nc.sbuf_tensor(name, shape, dt))

        def sem(name):
            return ctx.enter_context(nc.semaphore(name))

        cross_w = sb("cross_w", [P, 4, KT, D])
        wq, wk, wv, wo = (cross_w[:, i] for i in range(4))
        self_w = sb("self_w", [P, KT, 3 * D + DOUT])
        row_c = sb("row_c", [P, 5 * D + 2 * D])
        bq, bv, bo, n1w, n2w = (row_c[:, i * D:(i + 1) * D] for i in range(5))
        qkw = row_c[:, 5 * D:7 * D]
        bk = sb("bk", [P, KT])
        gate_w = sb("gate_w", [P, KT, 4])
        identf = sb("identf", [P, P])
        identb = sb("identb", [P, P], BF16)
        causal_q = sb("causal_q", [P, S], BF16)
        causal_k = sb("causal_k", [P, P], BF16)
        half = sb("half", [P, 2 * TT * H])

        region1 = sb("region1", [P, max(FFN_WORDS, H * KEYS // 2)])
        region2 = sb("region2", [P, 2 * H * S // 2])
        region3 = sb("region3", [P, TT * KEYS], BF16)
        region4 = sb("region4", [P, 2 * HG * S])
        region5 = sb("region5", [P, KT * KEYS])
        k_stack = region1[:, 0:H * KEYS // 2].bitcast(BF16).rearrange("p (h n) -> p h n", h=H)
        fw = region1
        q_stack = region2[:, 0:H * S // 2].bitcast(BF16).rearrange("p (h n) -> p h n", h=H)
        ks_stack = region2[:, H * S // 2:H * S].bitcast(BF16).rearrange("p (h n) -> p h n", h=H)
        v_aug = region2[:, H * S // 2:H * S // 2 + NKT * H * VW].rearrange("p (j h c) -> p j h c", j=NKT, h=H)
        hidden = region2[:, 0:3 * HT * S].rearrange("p (i t n) -> p i t n", i=3, t=HT)
        mask_b = region3[:].rearrange("p (t n) -> p t n", t=TT)
        k_nat = region3[:, 0:TT * H * PARTS].rearrange("p (t h c) -> p t h c", t=TT, h=H)
        probs = region4[:].rearrange("p (s h n) -> p s h n", s=2, h=HG)
        squares = region4[:, 0:2 * TT * D].rearrange("p (t n) -> p t n", t=TT)
        kf = region4[:, 0:KEYS]
        HK = -(-KEYS // 2)
        k_part = [region4[:, KEYS + i * HK:KEYS + (i + 1) * HK].bitcast(BF16)[:, 0:KEYS] for i in range(3)]
        ctx_sb = region5[:].rearrange("p (t n) -> p t n", t=KT)
        o_t = region5[:, 0:S]
        o_nat = region5[:, S:S + TT * D].rearrange("p (t n) -> p t n", t=TT)
        o_natT = region5[:, S + TT * D:S + TT * D + KT * S].rearrange("p (t n) -> p t n", t=KT)

        q_nat = sb("q_nat", [P, TT, H, PARTS], BF16)
        x_in = sb("x_in", [P, TT, D])
        nat = sb("nat", [P, TT, D])
        natT = sb("natT", [P, KT, S])
        qk = sb("qk", [P, TT, 2 * D])
        x1 = sb("x1", [P, TT, D])
        x2 = sb("x2", [P, TT, D])
        acc = sb("acc", [P, TT, D])
        vs = sb("vs", [P, TT, H, VW])
        junk = sb("junk", [P, 2, S], BF16)
        stats = sb("stats", [P, TT, 6])
        mv = sb("mv", [P, TT, 2])
        ms = sb("ms", [P, 2 * TT * H])
        rs = sb("rs", [P, 2 * TT * H])
        mx = sb("mx", [P, HG * TT, NCH])
        neg = sb("neg", [P, HG * TT])
        neg_nat = sb("neg_nat", [P, HG * TT, 3], BF16)
        rden = sb("rden", [P, TT, HG])
        mask_sum = sb("mask_sum", [P, TT])
        mask_any = sb("mask_any", [P, 3])
        row_live = sb("row_live", [P, TT])
        masked_i = sb("masked_i", [1, 1], I32)
        big_c = sb("big_c", [P, 1])
        lg = sb("lg", [P, TT, 4])
        lt = sb("lt", [P, TT, 4])
        rank = sb("rank", [P, TT, 4])
        l1 = sb("l1", [P, TT])

        banks = [ctx.enter_context(nc.psum_tensor(f"bank{i}", [P, 512], F32)) for i in range(8)]
        s_banks = [t[:] for t in banks[0:N_S]]
        m_banks = [t[:] for t in banks[N_S:N_S + N_M]]
        pv = banks[7][:]

        const_dma = sem("const_dma")
        x_dma, ctx_dma, mask_dma = sem("x_dma"), sem("ctx_dma"), sem("mask_dma")
        kst_dma = sem("kst_dma")
        ks_ones_dma = sem("ks_ones_dma")
        expert_dma = [sem(f"expert{e}_dma") for e in range(4)]
        out_dma = sem("out_dma")
        pool_setup, dve_setup = sem("pool_setup"), sem("dve_setup")
        s_full, s_free = sem("s_full"), sem("s_free")
        m_full, m_free = sem("m_full"), sem("m_free")
        pv_done = sem("pv_done")
        pv_copied = sem("pv_copied")
        dve_steps, pool_steps = sem("dve_steps"), sem("pool_steps")
        act_mask = sem("act_mask")
        nat_ready = sem("nat_ready")
        ms_ready, rs_ready = sem("ms_ready"), sem("rs_ready")
        live_ready = sem("live_ready")
        flag_ready = sem("flag_ready")
        kcast, ksub = sem("kcast"), sem("ksub")
        q_parts = sem("q_parts")
        k_parts = sem("k_parts")
        ks_nat_ready = sem("ks_nat_ready")
        neg_ready = sem("neg_ready")
        x1_done = sem("x1_done")
        gate_in, gate_exp = sem("gate_in"), sem("gate_exp")
        waits_apart = sem("waits_apart")
        stored = sem("stored")
        out_ready = sem("out_ready")

        block = ctx.enter_context(nc.Block())

        M_VDONE = TT + NKT
        M_QST = M_VDONE + H // 2
        M_CROSS_END = M_PREP + M_CROSS
        M_CROSS_PV_END = M_CROSS_END - TT - KT
        M_SELF_AT = M_CROSS_END
        S_SELF_AT = S_PREP + S_CROSS
        S_FFN_AT = S_SELF_AT + S_SELF

        @block.sync
        def _(sp):
            sp.dma_start(cross_w[:], w_cross).then_inc(const_dma, 16)
            sp.dma_start(row_c[:], rows).then_inc(const_dma, 16)
            sp.dma_start(bk[:], bias_k).then_inc(const_dma, 16)
            sp.dma_start(self_w[:], w_self).then_inc(const_dma, 16)
            sp.dma_start(gate_w[:], gate_t).then_inc(const_dma, 16)
            with sp.Fori(0, B) as b:
                sp.wait_ge(x1_done, b + 1)
                sp.dma_start(x_in[:], x[b]).then_inc(x_dma, 16)
                sp.wait_ge(m_free, b * M_USES + N_M)
                sp.dma_start(ctx_sb, ctx_t[b]).then_inc(ctx_dma, 16)
                sp.dma_start(k_stack[PARTS:ROWS, :, :], ones).then_inc(kst_dma, 16)
                for t in range(KT):
                    for part in range(3):
                        sp.wait_ge(kcast, b * (3 * KT) + (3 * t + part + 1))
                        for hh in range(P // DK):
                            for blk in K_BLOCKS[part]:
                                sp.dma_start(k_stack[blk * DK:(blk + 1) * DK, t * (P // DK) + hh, :],
                                             k_part[part][hh * DK:(hh + 1) * DK, :]).then_inc(kst_dma, 16)
                sp.wait_ge(m_free, b * M_USES + (M_CROSS_PV_END + N_M))
                sp.dma_start(ks_stack[PARTS:ROWS, :, :],
                             ones[:, 0:H * S].rearrange("p (h n) -> p h n", h=H)).then_inc(ks_ones_dma, 16)
                for e in range(4):
                    sp.dma_start(fw[:, EXPERT_AT[e]:EXPERT_AT[e + 1]],
                                 ffn_w[:, EXPERT_AT[e]:EXPERT_AT[e + 1]]).then_inc(expert_dma[e], 16)
                sp.wait_ge(out_ready, (b + 1) * 1)
                sp.dma_start(out[b], acc[:]).then_inc(out_dma, 16)
                sp.wait_ge(out_dma, 16 * b + 16)
                sp.sem_inc(stored, 1)

        KST_INCS = 16 * (1 + 6 * H)

        @block.gpsimd
        def _(pool):
            setup = [0]

            def once(ins):
                setup[0] += 1
                ins.then_inc(pool_setup, 1)
                pool.wait_ge(pool_setup, setup[0])

            once(pool.memset(identf[:], 0.0))
            once(pool.affine_select(out=identf[:], in_=identf[:], compare_op=ALU.not_equal, fill=1.0,
                                    base=0, pattern=[[-1, P]], channel_multiplier=1))
            once(pool.tensor_copy(identb[:], identf[:]))
            once(pool.memset(causal_q[:], 0.0))
            once(pool.affine_select(out=causal_q[:, S - P:S], in_=causal_q[:, S - P:S], compare_op=ALU.is_ge,
                                    fill=-BIG, base=0, pattern=[[-1, P]], channel_multiplier=1))
            once(pool.memset(causal_k[:], 0.0))
            once(pool.affine_select(out=causal_k[:], in_=causal_k[:], compare_op=ALU.is_ge,
                                    fill=-BIG, base=0, pattern=[[1, P]], channel_multiplier=-1))
            once(pool.memset(half[:], -0.5))
            once(pool.memset(big_c[:], -BIG))
            once(pool.memset(vs[:, :, :, DK:VW], 1.0))
            pool.sem_inc(x1_done, 1)
            pool.sem_inc(stored, 1)
            with pool.Fori(0, B) as b:
                chain = Chain(pool, pool_steps, POOL_STEPS, b)
                roots = [0]

                def root(width):
                    roots[0] += 1
                    pool.wait_ge(ms_ready, b * 5 + roots[0])
                    pool.tensor_tensor(rs[:, 0:width], ms[:, 0:width], half[:, 0:width], ALU.pow)\
                        .then_inc(rs_ready, 1)

                pool.wait_ge(m_free, b * M_USES + N_M)
                pool.dma_start(mask_b, mask[b]).then_inc(mask_dma, 16)
                chain(pool.memset(v_aug[:, :, :, DK:VW], 1.0))
                root(TT)
                pool.wait_ge(live_ready, b + 1)
                apart(pool, waits_apart)
                chain(pool.partition_all_reduce(mask_any[:, 1:2], mask_any[:, 0:1], P, bass.bass_isa.ReduceOp.max))
                apart(pool, waits_apart)
                chain(pool.tensor_scalar(mask_any[:, 2:3], mask_any[:, 1:2], 1.0 / BIG, 1.0, ALU.mult, ALU.min))
                apart(pool, waits_apart)
                pool.tensor_copy(masked_i[:], mask_any[0:1, 2:3]).then_inc(flag_ready, 1)
                for t in range(KT):
                    for part in range(3):
                        if part == 0:
                            pool.wait_ge(s_free, b * S_USES + (KT + NCH * (t + 1) + N_S))
                        else:
                            pool.wait_ge(ksub, b * (2 * KT) + (2 * t + part))
                        if t > 0:
                            pool.wait_ge(kst_dma, b * KST_INCS + 16 * (1 + 6 * (H // 2)))
                        apart(pool, waits_apart)
                        pool.tensor_copy(k_part[part], kf).then_inc(kcast, 1)
                root(TT)
                root(TT)
                root(2 * TT * H)
                pool.wait_ge(ks_nat_ready, b + 1)
                ks = qk[:, :, D:2 * D].rearrange("p t (h c) -> p t h c", c=DK)

                def kb(i):
                    return k_nat[:, :, :, i * DK:(i + 1) * DK]

                for part, blocks in enumerate(K_BLOCKS):
                    apart(pool, waits_apart)
                    for tt in range(TT):
                        chain.step(pool.tensor_copy(kb(blocks[0])[:, tt], ks[:, tt]))
                    chain.settle()
                    if part < 2:
                        for tt in range(TT):
                            chain.step(pool.tensor_tensor(ks[:, tt], ks[:, tt], kb(blocks[0])[:, tt], ALU.subtract))
                        chain.settle()
                apart(pool, waits_apart)
                for blocks in K_BLOCKS:
                    for i in blocks[1:]:
                        chain.step(pool.tensor_copy(kb(i), kb(blocks[0])))
                chain.settle()
                pool.sem_inc(k_parts, 1)
                root(TT)
                chain.end()

        @block.tensor
        def _(pe):
            mm, tr = pe.matmul, pe.transpose
            pe.wait_ge(pool_setup, 10)
            pe.wait_ge(const_dma, 16 * 5)
            pe.wait_ge(dve_setup, 3)
            with pe.Fori(0, B) as b:
                sr = Ring(pe, s_banks, s_full, s_free, S_USES, b)
                mr = Ring(pe, m_banks, m_full, m_free, M_USES, b)
                pv_step, on_n = [0], [0]

                def transpose_nat(stage):
                    pe.wait_ge(nat_ready, b * 3 + stage)
                    for kt in range(KT):
                        bank = sr.acquire()
                        for tt in range(TT):
                            last = tr(bank[:, tt * P:(tt + 1) * P], nat[:, tt, kt * P:(kt + 1) * P], identf[:])
                        last.then_inc(s_full, 1)
                    sr.wait_released(sr.n)

                def stack(src):
                    for pair in range(H // 2):
                        bank = mr.acquire().bitcast(BF16)
                        for i in range(2):
                            for tt in range(TT):
                                at = i * S + tt * P
                                last = tr(bank[0:PARTS, at:at + P], src[:, tt, 2 * pair + i, :], identb[:])
                        last.then_inc(m_full, 1)

                def max_rows():
                    neg_n[0] += 1
                    pe.wait_ge(neg_ready, b * (2 * NG) + neg_n[0])
                    for pair in range(2):
                        bank = mr.acquire().bitcast(BF16)
                        for i in range(2):
                            for tt in range(TT):
                                at = i * S + tt * P
                                last = tr(bank[PARTS:ROWS, at:at + P], neg_nat[:, (2 * pair + i) * TT + tt, :], identb[:])
                        last.then_inc(m_full, 1)

                def natural(n):
                    pe.wait_ge(pv_copied, b * (2 * NG) + n + 1)
                    bank = mr.acquire()
                    for tt in range(TT):
                        last = tr(bank[:, tt * P:(tt + 1) * P], o_t[:, tt * P:(tt + 1) * P], identf[:])
                    last.then_inc(m_full, 1)

                def project_out(n, w, width):
                    natural(n)
                    mr.wait_released(mr.n)
                    for kt in range(KT):
                        bank = mr.acquire()
                        for tt in range(TT):
                            last = tr(bank[:, tt * P:(tt + 1) * P], o_nat[:, tt, kt * P:(kt + 1) * P], identf[:])
                        last.then_inc(m_full, 1)
                    mr.wait_released(mr.n)
                    for tt in range(TT):
                        bank = mr.acquire()
                        for kt in range(KT):
                            last = mm(bank[:, 0:width], o_natT[:, kt, tt * P:(tt + 1) * P], w[:, kt, :],
                                      start=kt == 0, stop=kt == KT - 1)
                        last.then_inc(m_full, 1)

                def max_chunk(g, hh, tt, c):
                    h, (lo, w) = HG * g + hh, CHUNKS[c]
                    bank = mr.acquire()
                    mm(bank[:, 0:w], q_stack[0:PARTS, h, tt * P:(tt + 1) * P], k_stack[0:PARTS, h, lo:lo + w],
                       start=True, stop=True).then_inc(m_full, 1)

                def products(v_of, rows, j, tiles, lo, ring_n):
                    sr.wait_released(ring_n)
                    if j == 0:
                        pe.wait_ge(pv_copied, b * (2 * NG) + group[0] + 1)
                    slot = pv_step[0] % 2
                    for hh in range(HG):
                        last = mm(pv[32 * hh:32 * hh + VW, lo:S], v_of(j, hh),
                                  probs[0:rows, slot, hh, 0:S - lo], start=j == 0, stop=j == tiles - 1)
                    last.then_inc(pv_done, 1)
                    pv_step[0] += 1

                group = [0]
                neg_n = [0]

                transpose_nat(1)
                pe.wait_ge(ctx_dma, 16 * b + 16)
                for t in range(KT):
                    for lo, w in CHUNKS:
                        bank = sr.acquire()
                        for kt in range(KT):
                            last = mm(bank[:, 0:w], wk[:, kt, t * P:(t + 1) * P], ctx_sb[:, kt, lo:lo + w],
                                      start=kt == 0, stop=kt == KT - 1)
                        last.then_inc(s_full, 1)
                    if t == 0:
                        for tt in range(TT):
                            bank = mr.acquire()
                            for kt in range(KT):
                                last = mm(bank[:, 0:D], natT[:, kt, tt * P:(tt + 1) * P], wq[:, kt, :],
                                          start=kt == 0, stop=kt == KT - 1)
                            last.then_inc(m_full, 1)
                        for j in range(NKT):
                            r = min(P, KEYS - P * j)
                            bank = mr.acquire()
                            for kt in range(KT):
                                last = mm(bank[0:r, 0:D], ctx_sb[:, kt, j * P:j * P + r], wv[:, kt, :],
                                          start=kt == 0, stop=kt == KT - 1)
                            last.then_inc(m_full, 1)
                pe.wait_ge(q_parts, b * 2 + 1)
                stack(q_nat)
                mr.wait_released(mr.n)
                pe.wait_ge(kst_dma, b * KST_INCS + KST_INCS)
                for hh in range(HG):
                    for tt in range(TT):
                        for c in range(NCH):
                            max_chunk(0, hh, tt, c)
                max_rows()

                at_m, at_s = mr.n, sr.n

                def cross_attention(masked):
                    mr.n, sr.n = at_m, at_s
                    pv_step[0], group[0], neg_n[0] = 0, 0, 1
                    for g in range(NG):
                        mr.wait_released(mr.n)
                        for j in range(NKT):
                            r = min(P, KEYS - P * j)
                            for hh in range(HG):
                                h = HG * g + hh
                                bank = sr.acquire()
                                if masked:
                                    for tt in range(TT):
                                        mm(bank[0:r, tt * P:(tt + 1) * P], mask_b[:, tt, j * P:j * P + r], identb[:],
                                           start=tt == 0, stop=False, skip_group_check=True)
                                mm(bank[0:r, :], k_stack[0:ROWS, h, j * P:j * P + r], q_stack[0:ROWS, h, :],
                                   start=not masked, stop=True, skip_group_check=masked).then_inc(s_full, 1)
                            for work in cross_side_work(g, j):
                                if work[0] == "max":
                                    max_chunk(g + 1, *work[1:])
                                elif work[0] == "natural":
                                    natural(g)
                                elif work[0] == "rows":
                                    max_rows()
                            if j > 0:
                                products(lambda j, hh: v_aug[:, j, HG * g + hh, :], P, j - 1, NKT, 0, sr.n - HG)
                        r = KEYS - P * (NKT - 1)
                        products(lambda j, hh: v_aug[0:r, j, HG * g + hh, :], r, NKT - 1, NKT, 0, sr.n)
                        group[0] += 1

                pe.wait_ge(flag_ready, b + 1)
                apart(pe, waits_apart)
                masked = pe.value_load(masked_i[:])
                with pe.If(masked):
                    cross_attention(True)
                with pe.Else():
                    cross_attention(False)
                project_out(NG, wo, D)
                assert mr.n == M_CROSS_END and sr.n == S_SELF_AT

                transpose_nat(2)
                for tt in range(TT):
                    bank = mr.acquire()
                    for kt in range(KT):
                        last = mm(bank[:, :], natT[:, kt, tt * P:(tt + 1) * P], self_w[:, kt, 0:2 * D],
                                  start=kt == 0, stop=kt == KT - 1)
                    last.then_inc(m_full, 1)
                for tt in range(TT):
                    bank = mr.acquire()
                    for kt in range(KT):
                        last = mm(bank[:, 0:D], natT[:, kt, tt * P:(tt + 1) * P], self_w[:, kt, 2 * D:3 * D],
                                  start=kt == 0, stop=kt == KT - 1)
                    last.then_inc(m_full, 1)
                pe.wait_ge(q_parts, b * 2 + 2)
                stack(q_nat)
                pe.wait_ge(k_parts, b + 1)
                stack(k_nat)
                mr.wait_released(mr.n)
                pe.wait_ge(ks_ones_dma, 16 * b + 16)

                def self_max(g, hh, tt):
                    w = P * (tt + 1)
                    bank = mr.acquire()
                    mm(bank[:, 0:w], q_stack[0:PARTS, HG * g + hh, tt * P:(tt + 1) * P],
                       ks_stack[0:PARTS, HG * g + hh, 0:w], start=True, stop=True).then_inc(m_full, 1)

                for hh in range(HG):
                    for tt in range(TT):
                        self_max(0, hh, tt)
                max_rows()
                for g in range(NG):
                    mr.wait_released(mr.n)
                    for j in range(TT):
                        lo = P * j
                        for hh in range(HG):
                            h = HG * g + hh
                            bank = sr.acquire()
                            mm(bank[:, 0:S - lo], ks_stack[0:ROWS, h, lo:lo + P], q_stack[0:ROWS, h, lo:S],
                               start=True, stop=False)
                            mm(bank[:, 0:P], identb[:], causal_k[:], start=False, stop=True).then_inc(s_full, 1)
                        for work in self_side_work(g, j):
                            if work[0] == "max":
                                self_max(g + 1, *work[1:])
                            elif work[0] == "natural":
                                natural(NG + g)
                            elif work[0] == "rows":
                                max_rows()
                        if j > 0:
                            products(lambda j, hh: vs[:, j, HG * g + hh, :], P, j - 1, TT, lo - P, sr.n - HG)
                    products(lambda j, hh: vs[:, j, HG * g + hh, :], P, TT - 1, TT, S - P, sr.n)
                    group[0] += 1
                project_out(2 * NG, self_w[:, :, 3 * D:3 * D + DOUT], DOUT)
                assert sr.n == S_FFN_AT

                transpose_nat(3)
                bank = mr.acquire()
                for tt in range(TT):
                    for kt in range(KT):
                        last = mm(bank[:, 4 * tt:4 * tt + 4], natT[:, kt, tt * P:(tt + 1) * P], gate_w[:, kt, :],
                                  start=kt == 0, stop=kt == KT - 1)
                last.then_inc(m_full, 1)

                def layer(name, src, ring, full):
                    at, kts, w = FFN_W[name]
                    for t in range(w // P):
                        bank = ring.acquire()
                        for kt in range(kts):
                            last = mm(bank[:, :], fw[:, at + kt * w + t * P:at + kt * w + (t + 1) * P], src[:, kt, :],
                                      start=kt == 0, stop=kt == kts - 1)
                        last.then_inc(full, 1)

                def down(name, src):
                    at, kts, w = FFN_W[name]
                    for tt in range(TT):
                        bank = mr.acquire()
                        for kt in range(kts):
                            last = mm(bank[:, 0:w], src[:, kt, tt * P:(tt + 1) * P], fw[:, at + kt * w:at + (kt + 1) * w],
                                      start=kt == 0, stop=kt == kts - 1)
                        last.then_inc(m_full, 1)

                h0, h1, h2 = (hidden[:, i] for i in range(3))
                pe.wait_ge(expert_dma[0], 16 * b + 16)
                layer("e0_up", natT, sr, s_full)
                pe.wait_ge(expert_dma[1], 16 * b + 16)
                layer("e1_w1", natT, sr, s_full)
                layer("e1_w2", natT, mr, m_full)
                sr.wait_released(sr.n - HT)
                down("e0_down", h0)
                pe.wait_ge(expert_dma[2], 16 * b + 16)
                layer("e2_l1", natT, sr, s_full)
                mr.wait_released(mr.n - TT)
                down("e1_down", h1)
                sr.wait_released(sr.n)
                layer("e2_l2", h0, sr, s_full)
                pe.wait_ge(expert_dma[3], 16 * b + 16)
                sr.wait_released(sr.n)
                layer("e2_l3", h1, sr, s_full)
                layer("e3_down", natT, sr, s_full)
                sr.wait_released(sr.n - KT)
                down("e2_l4", h0)
                sr.wait_released(sr.n)
                layer("e3_up", h2, sr, s_full)
                sr.wait_released(sr.n)
                down("e3_out", h1)
                assert mr.n == M_USES and sr.n == S_USES, (mr.n, M_USES, sr.n, S_USES)

        @block.scalar
        def _(act):
            act.wait_ge(pool_setup, 10)
            act.wait_ge(const_dma, 16 * 5)
            act.sem_inc(s_free, N_S)
            with act.Fori(0, B) as b:
                sr = Ring(act, s_banks, s_full, s_free, S_USES, b)
                pv_step = [0]

                def empty(dst, func, width=S, bias=0.0):
                    bank = sr.take()
                    act.activation(dst, bank[:, 0:width], func, bias=bias).then_inc(s_free, 1)

                def exps(rows, lo):
                    act.wait_ge(pv_done, b * PV_STEPS + (pv_step[0] + 1))
                    for hh in range(HG):
                        bank = sr.take()
                        act.activation(probs[0:rows, pv_step[0] % 2, hh, 0:S - lo], bank[0:rows, 0:S - lo],
                                       ACT.Exp).then_inc(s_free, 1)
                    pv_step[0] += 1

                for kt in range(KT):
                    empty(natT[:, kt, :], ACT.Copy)
                act.wait_ge(mask_dma, 16 * b + 16)
                for tt in range(TT):
                    act.activation(mask_b[:, tt, :], mask_b[:, tt, :], ACT.Identity, bias=big_c[:], scale=BIG,
                                   accum_out=mask_sum[:, tt:tt + 1]).then_inc(act_mask, 1)
                act.wait_ge(pv_done, b * PV_STEPS + 2)
                for t in range(KT):
                    if t > 0:
                        act.wait_ge(kcast, b * (3 * KT) + 3 * t)
                    for lo, w in CHUNKS:
                        empty(kf[:, lo:lo + w], ACT.Identity, w, bk[:, t:t + 1])
                for g in range(NG):
                    for j in range(NKT):
                        exps(min(P, KEYS - P * j), 0)
                for kt in range(KT):
                    empty(natT[:, kt, :], ACT.Copy)
                for g in range(NG):
                    for j in range(TT):
                        exps(P, P * j)
                for kt in range(KT):
                    empty(natT[:, kt, :], ACT.Copy)
                act.wait_ge(gate_in, b + 1)
                act.activation(lg[:], lg[:], ACT.Exp).then_inc(gate_exp, 1)
                h0, h1, h2 = (hidden[:, i] for i in range(3))
                for t in range(HT):
                    empty(h0[:, t, :], ACT.Gelu)
                for t in range(HT):
                    empty(h1[:, t, :], ACT.Silu)
                for t in range(HT):
                    empty(h0[:, t, :], ACT.Gelu)
                for t in range(HT):
                    empty(h1[:, t, :], ACT.Gelu)
                for t in range(HT):
                    empty(h0[:, t, :], ACT.Gelu)
                for t in range(KT):
                    empty(h2[:, t, :], ACT.Gelu)
                for t in range(HT):
                    empty(h1[:, t, :], ACT.Gelu)
                assert sr.n == S_USES

        @block.vector
        def _(dve):
            dve.wait_ge(const_dma, 16 * 5)
            dve.tensor_scalar(qkw[:, 0:D], qkw[:, 0:D], DK ** -0.5, None, ALU.mult).then_inc(dve_setup, 1)
            dve.memset(pv, 0.0).then_inc(dve_setup, 1)
            dve.memset(mx[:], -FLT_MAX).then_inc(dve_setup, 1)
            dve.wait_ge(dve_setup, 3)
            dve.sem_inc(m_free, N_M)
            dve.sem_inc(pv_copied, 1)
            dve.sem_inc(pv_done, 2)
            with dve.Fori(0, B) as b:
                v = Chain(dve, dve_steps, DVE_STEPS, b)
                mr = Ring(dve, m_banks, m_full, m_free, M_USES, b)
                roots, nats = [0], [0]

                def root(ins):
                    roots[0] += 1
                    ins.then_inc(ms_ready, 1)
                    dve.wait_ge(rs_ready, b * 5 + roots[0])

                def layer_norm(src, dst, last_sem):
                    for tt in range(TT):
                        v.step(dve.bn_stats(stats[:, tt, :], src[:, tt, :]))
                    v.settle()
                    apart(dve, waits_apart)
                    for tt in range(TT):
                        v.step(dve.bn_aggr(mv[:, tt, :], stats[:, tt, :]))
                    v.settle()
                    root(dve.tensor_scalar(ms[:, 0:TT], mv[:, :, 1], LN_EPS, None, ALU.add))
                    for tt in range(TT):
                        ins = dve.tensor_scalar(dst[:, tt, :], src[:, tt, :], mv[:, tt, 0:1], rs[:, tt:tt + 1],
                                                ALU.subtract, ALU.mult)
                        if tt == TT - 1 and last_sem is not None:
                            ins.then_inc(last_sem, 1)
                        else:
                            v.step(ins)
                    v.settle()

                def rms_norm(src, w):
                    for tt in range(TT):
                        v(dve.tensor_tensor_reduce(junk[:, 0, 0:D], src[:, tt, :], src[:, tt, :], 1.0, 0.0,
                                                   ALU.mult, ALU.add, ms[:, TT + tt:TT + tt + 1]))
                    root(dve.tensor_scalar(ms[:, 0:TT], ms[:, TT:2 * TT], 1.0 / D, RMS_EPS, ALU.mult, ALU.add))
                    for tt in range(TT):
                        ins = dve.scalar_tensor_tensor(nat[:, tt, :], src[:, tt, :], rs[:, tt:tt + 1], w,
                                                       ALU.mult, ALU.mult)
                        ins.then_inc(nat_ready, 1) if tt == TT - 1 else v.step(ins)
                    v.settle()

                def split_q():
                    q = qk[:, :, 0:D].rearrange("p t (h c) -> p t h c", c=DK)

                    def qb(i):
                        return q_nat[:, :, :, i * DK:(i + 1) * DK]

                    for part, blocks in enumerate(Q_BLOCKS):
                        for tt in range(TT):
                            v.step(dve.tensor_copy(qb(blocks[0])[:, tt], q[:, tt]))
                        v.settle()
                        if part < 2:
                            for tt in range(TT):
                                v.step(dve.tensor_tensor(q[:, tt], q[:, tt], qb(blocks[0])[:, tt], ALU.subtract))
                            v.settle()
                    for i, src in ((2, 0), (4, 0)):
                        v.step(dve.tensor_copy(qb(i), qb(src)))
                    v.settle()
                    dve.tensor_copy(qb(5), qb(1)).then_inc(q_parts, 1)

                def unstack(dst):
                    for pair in range(H // 2):
                        bank = mr.take().bitcast(BF16)
                        dve.tensor_copy(dst[0:PARTS, 2 * pair:2 * pair + 2, :],
                                        bank[0:PARTS, :].rearrange("p (h n) -> p h n", h=2)).then_inc(m_free, 1)

                def masked_max(hh, tt, c, w, bias):
                    bank = mr.take()
                    mr.wait_released(mr.n - 2)
                    apart(dve, waits_apart)
                    dve.tensor_tensor_reduce(junk[:, mr.n % 2, 0:w], bank[:, 0:w], bias, 1.0, -FLT_MAX,
                                             ALU.add, ALU.max, mx[:, hh * TT + tt, c:c + 1]).then_inc(m_free, 1)

                def negate(chunks):
                    mr.wait_released(mr.n)
                    v(dve.tensor_reduce(neg[:], mx[:, :, 0:chunks], AX.X, ALU.max, negate=True))
                    for part in range(3):
                        ins = dve.tensor_copy(neg_nat[:, :, part], neg[:])
                        if part < 2:
                            v(ins)
                            v(dve.tensor_tensor(neg[:], neg[:], neg_nat[:, :, part], ALU.subtract))
                        else:
                            ins.then_inc(neg_ready, 1)

                def rows_in(g):
                    for pair in range(2):
                        h = HG * g + 2 * pair
                        bank = mr.take().bitcast(BF16)
                        dve.tensor_copy(q_stack[PARTS:ROWS, h:h + 2, :],
                                        bank[PARTS:ROWS, :].rearrange("p (h n) -> p h n", h=2)).then_inc(m_free, 1)

                def copy_out(n):
                    dve.wait_ge(pv_done, b * PV_STEPS + (n + 2))
                    dve.tensor_copy(o_t, pv).then_inc(pv_copied, 1)

                def natural(g):
                    bank = mr.take().rearrange("p (t h c) -> p t h c", t=TT, h=HG)
                    mr.wait_released(mr.n - 1)
                    v(dve.reciprocal(rden[:], bank[:, :, :, DK]))
                    dst = o_nat[:, :, g * HG * DK:(g + 1) * HG * DK].rearrange("p t (h c) -> p t h c", h=HG)
                    for tt in range(TT):
                        ins = dve.tensor_tensor(dst[:, tt], bank[:, tt, :, 0:DK],
                                                rden[:, tt].unsqueeze(2).to_broadcast([P, HG, DK]), ALU.mult)
                        if tt == TT - 1:
                            ins.then_inc(m_free, 1)
                        else:
                            v.step(ins)

                def out_transposed():
                    for kt in range(KT):
                        bank = mr.take()
                        dve.tensor_copy(o_natT[:, kt, :], bank).then_inc(m_free, 1)

                dve.wait_ge(x_dma, 16 * b + 16)
                layer_norm(x_in, nat, nat_ready)
                dve.wait_ge(act_mask, b * TT + TT)
                v(dve.tensor_scalar(row_live[:], mask_sum[:], -KEYS * BIG, None, ALU.is_gt))
                dve.tensor_reduce(mask_any[:, 0:1], mask_sum[:], AX.X, ALU.min, negate=True).then_inc(live_ready, 1)

                def k_remainders(t):
                    for part in range(2):
                        dve.wait_ge(kcast, b * (3 * KT) + (3 * t + part + 1))
                        dve.tensor_tensor(kf, kf, k_part[part], ALU.subtract).then_inc(ksub, 1)

                for tt in range(TT):
                    bank = mr.take()
                    dve.tensor_tensor(qk[:, tt, 0:D], bank[:, 0:D], bq, ALU.add).then_inc(m_free, 1)
                mr.wait_released(mr.n)
                for tt in range(TT):
                    v.step(dve.tensor_scalar(qk[:, tt, 0:D], qk[:, tt, 0:D], row_live[:, tt:tt + 1], DK ** -0.5,
                                             ALU.mult, ALU.mult))
                k_remainders(0)
                for j in range(NKT):
                    r = min(P, KEYS - P * j)
                    bank = mr.take()
                    dve.tensor_tensor(v_aug[0:r, j, :, 0:DK], bank[0:r, 0:D].rearrange("p (h c) -> p h c", h=H),
                                      bv[0:r].rearrange("p (h c) -> p h c", h=H), ALU.add).then_inc(m_free, 1)
                v.settle()
                split_q()
                k_remainders(1)
                unstack(q_stack)
                for hh in range(HG):
                    for tt in range(TT):
                        for c, (lo, w) in enumerate(CHUNKS):
                            masked_max(hh, tt, c, w, mask_b[:, tt, lo:lo + w])
                negate(NCH)
                rows_in(0)

                for g in range(NG):
                    for j in range(NKT):
                        for work in cross_side_work(g, j):
                            if work[0] == "max":
                                hh, tt, c = work[1:]
                                lo, w = CHUNKS[c]
                                masked_max(hh, tt, c, w, mask_b[:, tt, lo:lo + w])
                            elif work[0] == "negate":
                                negate(NCH)
                            elif work[0] == "natural":
                                natural(g - 1)
                            elif work[0] == "rows":
                                rows_in(g + 1)
                    copy_out(NKT * (g + 1))
                for tt in range(TT):
                    v.step(dve.tensor_tensor(x_in[:, tt, :], x_in[:, tt, :], bo, ALU.add))
                natural(NG - 1)
                out_transposed()
                v.settle()
                for tt in range(TT):
                    bank = mr.take()
                    dve.tensor_tensor(x1[:, tt, :], bank[:, 0:D], x_in[:, tt, :], ALU.add).then_inc(m_free, 1)
                mr.wait_released(mr.n)
                dve.sem_inc(x1_done, 1)
                assert mr.n == M_CROSS_END

                layer_norm(x1, x2, None)
                rms_norm(x2, n1w)
                for tt in range(TT):
                    bank = mr.take()
                    dve.tensor_copy(qk[:, tt, :], bank).then_inc(m_free, 1)
                mr.wait_released(mr.n)
                for tt in range(TT):
                    v.step(dve.tensor_tensor(squares[:, tt, :], qk[:, tt, :], qk[:, tt, :], ALU.mult))
                v.settle()
                v(dve.tensor_reduce(ms[:], squares.rearrange("p t (h c) -> p (t h) c", c=DK), AX.X, ALU.add))
                root(dve.tensor_scalar(ms[:], ms[:], 1.0 / DK, RMS_EPS, ALU.mult, ALU.add))
                for part in range(2):
                    lo = D * (1 - part)
                    for tt in range(TT):
                        view = qk[:, tt, lo:lo + D].rearrange("p (h c) -> p h c", c=DK)
                        r0 = tt * 2 * H + lo // DK
                        v.step(dve.tensor_tensor(view, view, rs[:, r0:r0 + H].unsqueeze(2).to_broadcast([P, H, DK]),
                                                 ALU.mult))
                    v.settle()
                    for tt in range(TT):
                        ins = dve.tensor_tensor(qk[:, tt, lo:lo + D], qk[:, tt, lo:lo + D], qkw[:, lo:lo + D], ALU.mult)
                        if part == 0 and tt == TT - 1:
                            ins.then_inc(ks_nat_ready, 1)
                        else:
                            v.step(ins)
                    v.settle()
                for tt in range(TT):
                    bank = mr.take()
                    dve.tensor_copy(vs[:, tt, :, 0:DK], bank[:, 0:D].rearrange("p (h c) -> p h c", h=H))\
                        .then_inc(m_free, 1)
                split_q()
                unstack(q_stack)
                unstack(ks_stack)

                def self_max(hh, tt):
                    w = P * (tt + 1)
                    masked_max(hh, tt, 0, w, causal_q[:, S - w:S])

                for hh in range(HG):
                    for tt in range(TT):
                        self_max(hh, tt)
                negate(1)
                rows_in(0)
                for g in range(NG):
                    for j in range(TT):
                        for work in self_side_work(g, j):
                            if work[0] == "max":
                                self_max(*work[1:])
                            elif work[0] == "negate":
                                negate(1)
                            elif work[0] == "natural":
                                natural(g - 1)
                            elif work[0] == "rows":
                                rows_in(g + 1)
                    copy_out(NG * NKT + TT * (g + 1))
                natural(NG - 1)
                out_transposed()
                for tt in range(TT):
                    bank = mr.take()
                    dve.tensor_tensor(x2[:, tt, ZERO_COLS:D], bank[:, 0:DOUT], x2[:, tt, ZERO_COLS:D], ALU.add)\
                        .then_inc(m_free, 1)
                mr.wait_released(mr.n)

                dve.wait_ge(stored, b + 1)
                for tt in range(TT):
                    v.step(dve.tensor_tensor(acc[:, tt, :], x1[:, tt, :], x2[:, tt, :], ALU.add))
                rms_norm(x2, n2w)
                bank = mr.take()
                dve.tensor_scalar(lg[:], bank[:, 0:4 * TT].rearrange("p (t e) -> p t e", e=4), FLT_MAX, -FLT_MAX,
                                  ALU.min, ALU.max).then_inc(m_free, 1)
                mr.wait_released(mr.n)
                v(dve.tensor_reduce(l1[:], lg[:], AX.X, ALU.max))
                dve.tensor_tensor(lg[:], lg[:], l1[:].unsqueeze(2).to_broadcast([P, TT, 4]), ALU.subtract)\
                    .then_inc(gate_in, 1)
                dve.wait_ge(gate_exp, b + 1)
                v(dve.tensor_reduce(l1[:], lg[:], AX.X, ALU.add))
                v(dve.reciprocal(l1[:], l1[:]))
                v(dve.tensor_tensor(lg[:], lg[:], l1[:].unsqueeze(2).to_broadcast([P, TT, 4]), ALU.mult))
                v(dve.memset(rank[:], 0.0))
                for e in range(4):
                    if e > 0:
                        v.step(dve.tensor_tensor(lt[:, :, 0:e], lg[:, :, e:e + 1].to_broadcast([P, TT, e]),
                                                 lg[:, :, 0:e], ALU.is_gt))
                    if e < 3:
                        v.step(dve.tensor_tensor(lt[:, :, e + 1:4], lg[:, :, e:e + 1].to_broadcast([P, TT, 3 - e]),
                                                 lg[:, :, e + 1:4], ALU.is_ge))
                    v.settle()
                    if e > 0:
                        v.step(dve.tensor_tensor(rank[:, :, 0:e], rank[:, :, 0:e], lt[:, :, 0:e], ALU.add))
                    if e < 3:
                        v.step(dve.tensor_tensor(rank[:, :, e + 1:4], rank[:, :, e + 1:4], lt[:, :, e + 1:4], ALU.add))
                    v.settle()
                v(dve.tensor_scalar(rank[:], rank[:], 2.0, None, ALU.is_lt))
                v(dve.tensor_tensor(lg[:], lg[:], rank[:], ALU.mult))
                v(dve.tensor_reduce(l1[:], lg[:], AX.X, ALU.add))
                v(dve.tensor_scalar(l1[:], l1[:], 1e-8, None, ALU.add))
                v(dve.reciprocal(l1[:], l1[:]))
                v(dve.tensor_tensor(lg[:], lg[:], l1[:].unsqueeze(2).to_broadcast([P, TT, 4]), ALU.mult))
                h1 = hidden[:, 1]
                for t in range(HT):
                    bank = mr.take()
                    dve.wait_ge(s_free, b * S_USES + (S_FFN_AT + KT + HT + t + 1 + N_S))
                    dve.tensor_tensor(h1[:, t, :], bank, h1[:, t, :], ALU.mult).then_inc(m_free, 1)
                for e in range(4):
                    for tt in range(TT):
                        bank = mr.take()
                        mr.wait_released(mr.n - TT if e else mr.n - 1)
                        dve.scalar_tensor_tensor(acc[:, tt, ZERO_COLS:D], bank[:, 0:DOUT], lg[:, tt, e:e + 1],
                                                 acc[:, tt, ZERO_COLS:D], ALU.mult, ALU.add).then_inc(m_free, 1)
                mr.wait_released(mr.n)
                dve.sem_inc(out_ready, 1)
                assert mr.n == M_USES, (mr.n, M_USES)
                v.end()


def _tiles(w):
    k = w.shape[0] // P
    return w.reshape(k, P, w.shape[1]).transpose(1, 0, 2)


def kernel(**inputs):
    import numpy as np
    import concourse.bacc as bacc
    from concourse.bass_utils import run_bass_kernel_spmd

    a = {n: np.asarray(v) for n, v in inputs.items()}
    X, F = "L0_xattn_", "L0_ffn_"
    w_cross = np.stack([_tiles(a[X + n].T) for n in ("W_q", "W_k", "W_v", "W_o")], axis=1)
    w_self = np.concatenate([_tiles(a[F + n].T) for n in ("wq", "wk", "wv")]
                            + [_tiles(a[F + "wo"].T[:, ZERO_COLS:])], axis=2)
    rows = np.concatenate([a[X + "b_q"], a[X + "b_v"], a[X + "b_o"], a[F + "n1_w"], a[F + "n2_w"],
                           np.tile(a[F + "qn_w"], H), np.tile(a[F + "kn_w"], H)])
    cut = {"e0_down", "e1_down", "e2_l4", "e3_out"}
    ffn_w = np.concatenate([_tiles(a[F + n].T[:, ZERO_COLS:] if n in cut else a[F + n].T).reshape(P, -1)
                            for n in FFN_W], axis=1)
    arrays = {
        "x": a["x"],
        "ctx_t": a["ctx_1024"].transpose(0, 2, 1),
        "mask": a["mask_Bx1xSxS2_bf1"].reshape(B, S, KEYS).view(np.uint8),
        "w_cross": w_cross,
        "w_self": w_self,
        "rows": np.broadcast_to(rows, (P, rows.size)),
        "bias_k": a[X + "b_k"].reshape(KT, P).T,
        "gate_t": _tiles(a[F + "gate_w"].T),
        "ffn_w": ffn_w,
        "ones": np.ones((3, H * KEYS), dtype=mybir.dt.np(BF16)),
    }
    arrays = {n: np.ascontiguousarray(v) for n, v in arrays.items()}
    nc = bacc.Bacc("TRN2", target_bir_lowering=False, num_devices=1)
    t = {n: nc.dram_tensor(n, v.shape, mybir.dt.from_np(v.dtype), kind="ExternalInput").ap()
         for n, v in arrays.items()}
    out = nc.dram_tensor("out", (B, S, D), F32, kind="ExternalOutput").ap()
    xattn_ffn_kernel(
        nc, t["x"].rearrange("b (t p) d -> b p t d", p=P), t["ctx_t"].rearrange("b (k p) n -> b p k n", p=P),
        t["mask"].rearrange("b (t p) n -> b p t n", p=P), t["w_cross"], t["w_self"], t["rows"], t["bias_k"],
        t["gate_t"], t["ffn_w"], t["ones"], out.rearrange("b (t p) d -> b p t d", p=P))
    r = run_bass_kernel_spmd(nc, [arrays], core_ids=[0])
    return r.results[0]["out"]
```

```python
from contextlib import ExitStack

import concourse.bass as bass
from concourse import mybir

F32 = mybir.dt.float32
BF16 = mybir.dt.bfloat16
I32 = mybir.dt.int32
ALU = mybir.AluOpType
ACT = mybir.ActivationFunctionType
AX = mybir.AxisListType

P = 128
B, S, D = 8, 512, 256
KEYS = 1601
H, DK = 16, 16
HG = 4
NG = H // HG
TT = S // P
KT = D // P
NKT = -(-KEYS // P)
HID = 512
HT = HID // P
ZERO_COLS = 64
DOUT = D - ZERO_COLS
PARTS = 96
ROWS = PARTS + 3
VW = DK + 1
BIG = float(2 ** 30)
LN_EPS = 1e-5
RMS_EPS = 1.1920929e-07
FLT_MAX = 3.4028234e38
CHUNKS = []
for _c in range(4):
    _lo = sum(w for _, w in CHUNKS)
    CHUNKS.append((_lo, -(-(KEYS - _lo) // (4 - _c))))
NCH = len(CHUNKS)

Q_BLOCKS = ((0, 2, 4), (1, 5), (3,))
K_BLOCKS = ((0, 1, 3), (2, 5), (4,))

FFN_W = {}
_at = 0
for _name, _kt, _w in (("e0_up", KT, HID), ("e0_down", HT, DOUT),
                       ("e1_w1", KT, HID), ("e1_w2", KT, HID), ("e1_down", HT, DOUT),
                       ("e2_l1", KT, HID), ("e2_l2", HT, HID), ("e2_l3", HT, HID), ("e2_l4", HT, DOUT),
                       ("e3_down", KT, D), ("e3_up", KT, HID), ("e3_out", HT, DOUT)):
    FFN_W[_name] = (_at, _kt, _w)
    _at += _kt * _w
FFN_WORDS = _at
EXPERT_AT = [FFN_W[n][0] for n in ("e0_up", "e1_w1", "e2_l1", "e3_down")] + [FFN_WORDS]


N_M, N_S = 3, 4


def apart(eng, sem):
    eng.sem_inc(sem, 1)


class Ring:

    def __init__(self, eng, banks, sems, uses, b):
        assert uses % len(banks) == 0
        self.eng, self.banks, (self.full, self.free) = eng, banks, sems
        self.base, self.uses, self.n = b * uses, uses, 0

    def acquire(self):
        self.eng.wait_ge(self.free, self.base + (self.n + 1))
        self.n += 1
        return self.banks[(self.n - 1) % len(self.banks)]

    def take(self):
        self.eng.wait_ge(self.full, self.base + (self.n + 1))
        self.n += 1
        return self.banks[(self.n - 1) % len(self.banks)]

    def wait_released(self, n):
        self.eng.wait_ge(self.free, self.base + (n + len(self.banks)))

    def end(self):
        assert self.n == self.uses, (self.n, self.uses)


def later_ring(eng, banks, sems, uses, first, b):
    turn = first % len(banks)
    ring = Ring(eng, banks[turn:] + banks[:turn], sems, uses, b)
    ring.base = b * uses + first
    return ring


class Chain:

    def __init__(self, eng, sem, per_batch, b):
        self.eng, self.sem, self.per, self.base, self.n = eng, sem, per_batch, b * per_batch, 0

    def step(self, ins):
        self.n += 1
        ins.then_inc(self.sem, 1)

    def settle(self):
        self.eng.wait_ge(self.sem, self.base + self.n)

    def __call__(self, ins):
        self.step(ins)
        self.settle()

    def end(self):
        assert self.n == self.per, (self.n, self.per)


class Memory:

    def __init__(self, nc, ctx, sems, phase, banks):
        self.nc, self.ctx, self.sems, self.phase = nc, ctx, sems, phase
        self.s_banks, self.m_banks, self.pv = banks[0:N_S], banks[N_S:N_S + N_M], banks[7]

    def sb(self, name, shape, dt=F32):
        return self.ctx.enter_context(self.nc.sbuf_tensor(f"{self.phase}_{name}", shape, dt))

    def sem(self, name):
        return self.sems.enter_context(self.nc.semaphore(f"{self.phase}_{name}"))


def heads(ap):
    return ap.rearrange("p t (h c) -> p t h c", c=DK)


def next_batch(b):
    return (b + 1) % B



def setup_phase(nc, sems, consts, rows, bias_k):
    c = consts
    with ExitStack() as ctx:
        rows_dma, pool_setup, dve_setup = (sems.enter_context(nc.semaphore(n))
                                           for n in ("rows_dma", "pool_setup", "dve_setup"))
        block = ctx.enter_context(nc.Block())

        @block.sync
        def _(sp):
            sp.dma_start(c["row_c"], rows).then_inc(rows_dma, 16)
            sp.dma_start(c["bk"], bias_k).then_inc(rows_dma, 16)
            sp.wait_ge(rows_dma, 32)

        @block.gpsimd
        def _(pool):
            done = [0]

            def once(ins):
                done[0] += 1
                ins.then_inc(pool_setup, 1)
                pool.wait_ge(pool_setup, done[0])

            identf, causal_q, causal_k = c["identf"], c["causal_q"], c["causal_k"]
            once(pool.memset(identf, 0.0))
            once(pool.affine_select(out=identf, in_=identf, compare_op=ALU.not_equal, fill=1.0,
                                    base=0, pattern=[[-1, P]], channel_multiplier=1))
            once(pool.tensor_copy(c["identb"], identf))
            once(pool.memset(causal_q, 0.0))
            once(pool.affine_select(out=causal_q[:, S - P:S], in_=causal_q[:, S - P:S], compare_op=ALU.is_ge,
                                    fill=-BIG, base=0, pattern=[[-1, P]], channel_multiplier=1))
            once(pool.memset(causal_k, 0.0))
            once(pool.affine_select(out=causal_k, in_=causal_k, compare_op=ALU.is_ge,
                                    fill=-BIG, base=0, pattern=[[1, P]], channel_multiplier=-1))
            once(pool.memset(c["half"], -0.5))

        @block.vector
        def _(dve):
            qn = c["row_c"][:, 5 * D:6 * D]
            dve.wait_ge(rows_dma, 32)
            dve.tensor_scalar(qn, qn, DK ** -0.5, None, ALU.mult).then_inc(dve_setup, 1)
            dve.wait_ge(dve_setup, 1)


def cast_part(act, part_of, rest, blocks, part, sems, b):
    cast, left, copied = sems
    if part:
        act.wait_ge(left, b * 2 + part)
    act.activation(part_of(blocks[part][0]), rest, ACT.Copy).then_inc(cast, 1)
    if len(blocks[part]) > 1:
        act.wait_ge(cast, b * 3 + (part + 1))
    for i in blocks[part][1:]:
        act.activation(part_of(i), part_of(blocks[part][0]), ACT.Copy).then_inc(copied, 1)


def subtract_parts(eng, part_of, rest, blocks, sems, waits_apart, b):
    cast, left, _ = sems
    for part in range(2):
        eng.wait_ge(cast, b * 3 + (part + 1))
        apart(eng, waits_apart)
        eng.tensor_tensor(rest, rest, part_of(blocks[part][0]), ALU.subtract).then_inc(left, 1)


def wait_split(pe, sems, b):
    cast, _, copied = sems
    pe.wait_ge(cast, b * 3 + 3)
    pe.wait_ge(copied, b * 3 + 3)


def prepare_phase(nc, sems, banks, consts, x, ctx_t, mask, w_cross, scr):
    M_U, S_U = TT + NKT + 4, 2 * KT + KT * NCH + 4
    K_STORE, CASTS = 16 * 3 * KT, 3 * KT
    K_ORDER = ((0, 0), (0, 1), (1, 0), (0, 2), (1, 1), (1, 2))
    with ExitStack() as ctx:
        m = Memory(nc, ctx, sems, "prep", banks)
        sb, sem = m.sb, m.sem
        ident_f, ident_b, half, row_c, bk = (consts[n] for n in ("identf", "identb", "half", "row_c", "bk"))
        bq, bv = row_c[:, 0:D], row_c[:, D:2 * D]
        w = sb("w", [P, 3, KT, D])
        wq, wk, wv = (w[:, i] for i in range(3))
        big_c = sb("big_c", [P, 1])
        x_in, nat, natT = sb("x_in", [P, TT, D]), sb("nat", [P, TT, D]), sb("natT", [P, KT, S])
        q = sb("q", [P, TT, D])
        q_nat = sb("q_nat", [P, TT, H, PARTS], BF16)
        q_stack = sb("q_stack", [PARTS, H, S], BF16)
        ctx_sb = sb("ctx_sb", [P, 2, KT, KEYS])
        kf = sb("kf", [P, KT, KEYS])
        k_part = sb("k_part", [P, KT, 3, KEYS + KEYS % 2], BF16)
        v_aug = sb("v_aug", [P, NG, NKT, HG * VW])
        mask_b = sb("mask_b", [P, TT, KEYS], BF16)
        mask_sum, row_live, mask_any = sb("mask_sum", [P, TT]), sb("row_live", [P, TT]), sb("mask_any", [P, 3])
        masked_i = sb("masked_i", [1, 1], I32)
        stats, mv, ms, rs = sb("stats", [P, TT, 6]), sb("mv", [P, TT, 2]), sb("ms", [P, TT]), sb("rs", [P, TT])

        w_dma, x_dma, mask_dma = sem("w_dma"), sem("x_dma"), sem("mask_dma")
        ctx_dma = [sem(f"ctx{i}_dma") for i in range(2)]
        k_stored, v_stored, q_stored = sem("k_stored"), sem("v_stored"), sem("q_stored")
        mask_stored, flag_stored = sem("mask_stored"), sem("flag_stored")
        setup = sem("setup")
        s_sems, m_sems = (sem("s_full"), sem("s_free")), (sem("m_full"), sem("m_free"))
        ln_done = sem("ln_done")
        ms_ready, rs_ready = sem("ms_ready"), sem("rs_ready")
        mask_bias = sem("mask_bias")
        live_ready, flag_ready = sem("live_ready"), sem("flag_ready")
        q_ready = sem("q_ready")
        q_split = (sem("q_cast"), sem("q_left"), sem("q_copied"))
        kcast, ksub = sem("kcast"), sem("ksub")
        dve_steps, pool_steps, waits_apart = sem("dve_steps"), sem("pool_steps"), sem("waits_apart")

        def q_part(i):
            return q_nat[:, :, :, i * DK:(i + 1) * DK]

        block = ctx.enter_context(nc.Block())

        @block.sync
        def _(sp):
            sp.dma_start(x_in[:], x[0]).then_inc(x_dma, 16)
            sp.dma_start(w[:], w_cross[:, 0:3]).then_inc(w_dma, 16)
            sp.dma_start(ctx_sb[:, 0], ctx_t[0]).then_inc(ctx_dma[0], 16)
            for stored, n in ((k_stored, K_STORE), (v_stored, 16), (q_stored, 16), (mask_stored, 16), (flag_stored, 16)):
                sp.sem_inc(stored, n)
            with sp.Fori(0, B // 2) as pair:
                for u in range(2):
                    b = pair * 2 + u
                    sp.wait_ge(ln_done, b + 1)
                    apart(sp, waits_apart)
                    sp.dma_start(x_in[:], x[next_batch(b)]).then_inc(x_dma, 16)
                    sp.wait_ge(m_sems[1], b * M_U + N_M)
                    apart(sp, waits_apart)
                    sp.dma_start(ctx_sb[:, 1 - u], ctx_t[next_batch(b)]).then_inc(ctx_dma[1 - u], 16)
                    sp.wait_ge(mask_bias, b * TT + TT)
                    sp.dma_start(scr["mask"][b], mask_b[:]).then_inc(mask_stored, 16)
                    sp.wait_ge(flag_ready, b + 1)
                    sp.dma_start(scr["flag"][0:1, bass.ds(b, 1)], masked_i[:]).then_inc(flag_stored, 16)
                    for n, (t, part) in enumerate(K_ORDER):
                        sp.wait_ge(kcast, b * CASTS + (n + 1 + CASTS))
                        apart(sp, waits_apart)
                        sp.dma_start(scr["k"][part, b, t * P:(t + 1) * P, :], k_part[:, t, part, 0:KEYS])\
                            .then_inc(k_stored, 16)
                    sp.wait_ge(m_sems[1], b * M_U + (TT + NKT + N_M))
                    sp.dma_start(scr["v"][b], v_aug[:].rearrange("p g j c -> p g (j c)")).then_inc(v_stored, 16)
                    sp.wait_ge(m_sems[1], b * M_U + (M_U + N_M))
                    sp.wait_ge(s_sems[1], b * S_U + (S_U + N_S))
                    sp.dma_start(scr["q"][b], q_stack[:].rearrange("p (g h) n -> p g (h n)", g=NG)).then_inc(q_stored, 16)
            sp.wait_ge(k_stored, K_STORE * (B + 1))
            for stored in (v_stored, q_stored, mask_stored, flag_stored):
                sp.wait_ge(stored, 16 * (B + 1))

        @block.gpsimd
        def _(pool):
            pool.memset(big_c[:], -BIG).then_inc(setup, 1)
            pool.memset(v_aug[:], 1.0).then_inc(setup, 1)
            pool.dma_start(mask_b[:], mask[0]).then_inc(mask_dma, 16)
            pool.wait_ge(ms_ready, 1)
            pool.tensor_tensor(rs[:], ms[:], half[:, 0:TT], ALU.pow).then_inc(rs_ready, 1)
            with pool.Fori(0, B) as b:
                chain = Chain(pool, pool_steps, 2, b)
                pool.wait_ge(live_ready, b + 1)
                pool.wait_ge(flag_stored, 16 * b + 16)
                apart(pool, waits_apart)
                chain(pool.partition_all_reduce(mask_any[:, 1:2], mask_any[:, 0:1], P, bass.bass_isa.ReduceOp.max))
                apart(pool, waits_apart)
                chain(pool.tensor_scalar(mask_any[:, 2:3], mask_any[:, 1:2], 1.0 / BIG, 1.0, ALU.mult, ALU.min))
                apart(pool, waits_apart)
                pool.tensor_copy(masked_i[:], mask_any[0:1, 2:3]).then_inc(flag_ready, 1)
                pool.wait_ge(mask_stored, 16 * b + 32)
                apart(pool, waits_apart)
                pool.dma_start(mask_b[:], mask[next_batch(b)]).then_inc(mask_dma, 16)
                subtract_parts(pool, q_part, heads(q[:]), Q_BLOCKS, q_split, waits_apart, b)
                pool.wait_ge(ms_ready, b + 2)
                pool.tensor_tensor(rs[:], ms[:], half[:, 0:TT], ALU.pow).then_inc(rs_ready, 1)
                chain.end()

        @block.tensor
        def _(pe):
            mm, tr = pe.matmul, pe.transpose
            pe.wait_ge(w_dma, 16)
            with pe.Fori(0, B // 2) as pair:
                for u in range(2):
                    b = pair * 2 + u
                    sr, mr = Ring(pe, m.s_banks, s_sems, S_U, b), Ring(pe, m.m_banks, m_sems, M_U, b)
                    pe.wait_ge(ln_done, b + 1)
                    for kt in range(KT):
                        for half_of in range(2):
                            bank = sr.acquire()
                            for i in range(TT // 2):
                                tt = half_of * (TT // 2) + i
                                last = tr(bank[:, i * P:(i + 1) * P], nat[:, tt, kt * P:(kt + 1) * P], ident_f[:])
                            last.then_inc(s_sems[0], 1)
                    sr.wait_released(sr.n)
                    for tt in range(TT):
                        bank = mr.acquire()
                        for kt in range(KT):
                            last = mm(bank[:, 0:D], natT[:, kt, tt * P:(tt + 1) * P], wq[:, kt, :],
                                      start=kt == 0, stop=kt == KT - 1)
                        last.then_inc(m_sems[0], 1)
                    pe.wait_ge(ctx_dma[u], 16 * pair + 16)
                    for t in range(KT):
                        for lo, n in CHUNKS:
                            bank = sr.acquire()
                            for kt in range(KT):
                                last = mm(bank[:, 0:n], wk[:, kt, t * P:(t + 1) * P], ctx_sb[:, u, kt, lo:lo + n],
                                          start=kt == 0, stop=kt == KT - 1)
                            last.then_inc(s_sems[0], 1)
                    for j in range(NKT):
                        r = min(P, KEYS - P * j)
                        bank = mr.acquire()
                        for kt in range(KT):
                            last = mm(bank[0:r, 0:D], ctx_sb[:, u, kt, j * P:j * P + r], wv[:, kt, :],
                                      start=kt == 0, stop=kt == KT - 1)
                        last.then_inc(m_sems[0], 1)
                    wait_split(pe, q_split, b)
                    for n in range(H // 2):
                        ring, full = ((mr, m_sems[0]), (sr, s_sems[0]))[n % 2]
                        bank = ring.acquire().bitcast(BF16)
                        for i in range(2):
                            for tt in range(TT):
                                at = i * S + tt * P
                                last = tr(bank[0:PARTS, at:at + P], q_nat[:, tt, 2 * n + i, :], ident_b[:])
                        last.then_inc(full, 1)
                    mr.end(), sr.end()

        @block.scalar
        def _(act):
            act.sem_inc(s_sems[1], N_S)
            act.wait_ge(setup, 2)

            def bias_mask(b):
                act.wait_ge(mask_dma, 16 * b + 16)
                for tt in range(TT):
                    act.activation(mask_b[:, tt, :], mask_b[:, tt, :], ACT.Identity, bias=big_c[:], scale=BIG,
                                   accum_out=mask_sum[:, tt:tt + 1]).then_inc(mask_bias, 1)

            act.sem_inc(kcast, CASTS)
            bias_mask(0)
            with act.Fori(0, B) as b:
                sr = Ring(act, m.s_banks, s_sems, S_U, b)

                def keys(t):
                    act.wait_ge(kcast, b * CASTS + (K_ORDER.index((t, 2)) + 1))
                    for lo, n in CHUNKS:
                        bank = sr.take()
                        act.activation(kf[:, t, lo:lo + n], bank[:, 0:n], ACT.Identity, bias=bk[:, t:t + 1])\
                            .then_inc(s_sems[1], 1)

                def key_part(t, part):
                    if part == 0:
                        act.wait_ge(s_sems[1], b * S_U + (2 * KT + NCH * (t + 1) + N_S))
                        act.wait_ge(k_stored, b * K_STORE + K_STORE)
                    else:
                        act.wait_ge(ksub, b * (2 * KT) + (2 * t + part))
                    act.activation(k_part[:, t, part, 0:KEYS], kf[:, t, :], ACT.Copy).then_inc(kcast, 1)

                for kt in range(KT):
                    for half_of in range(2):
                        bank = sr.take()
                        act.activation(natT[:, kt, half_of * (S // 2):(half_of + 1) * (S // 2)], bank[:, 0:S // 2],
                                       ACT.Copy).then_inc(s_sems[1], 1)
                keys(0)
                act.wait_ge(q_ready, b + 1)
                cast_part(act, q_part, heads(q[:]), Q_BLOCKS, 0, q_split, b)
                key_part(0, 0)
                cast_part(act, q_part, heads(q[:]), Q_BLOCKS, 1, q_split, b)
                keys(1)
                cast_part(act, q_part, heads(q[:]), Q_BLOCKS, 2, q_split, b)
                for t, part in K_ORDER[1:]:
                    key_part(t, part)
                act.wait_ge(live_ready, b + 1)
                bias_mask(b + 1)
                act.wait_ge(q_stored, 16 * b + 16)
                for n in range(1, H // 2, 2):
                    bank = sr.take().bitcast(BF16)
                    act.activation(q_stack[:, 2 * n:2 * n + 2, :],
                                   bank[0:PARTS, :].rearrange("p (h n) -> p h n", h=2), ACT.Copy).then_inc(s_sems[1], 1)
                sr.end()

        @block.vector
        def _(dve):
            dve.wait_ge(setup, 2)
            dve.sem_inc(m_sems[1], N_M)

            def moments(v, b):
                dve.wait_ge(x_dma, 16 * b + 16)
                for tt in range(TT):
                    v.step(dve.bn_stats(stats[:, tt, :], x_in[:, tt, :]))
                v.settle()
                apart(dve, waits_apart)
                for tt in range(TT):
                    v.step(dve.bn_aggr(mv[:, tt, :], stats[:, tt, :]))
                v.settle()
                dve.tensor_scalar(ms[:], mv[:, :, 1], LN_EPS, None, ALU.add).then_inc(ms_ready, 1)

            def normalise(v, b):
                dve.wait_ge(rs_ready, b + 1)
                for tt in range(TT):
                    ins = dve.tensor_scalar(nat[:, tt, :], x_in[:, tt, :], mv[:, tt, 0:1], rs[:, tt:tt + 1],
                                            ALU.subtract, ALU.mult)
                    if tt == TT - 1:
                        ins.then_inc(ln_done, 1)
                    else:
                        v.step(ins)

            def live(v, b):
                dve.wait_ge(mask_bias, b * TT + TT)
                v(dve.tensor_scalar(row_live[:], mask_sum[:], -KEYS * BIG, None, ALU.is_gt))
                dve.tensor_reduce(mask_any[:, 0:1], mask_sum[:], AX.X, ALU.min, negate=True).then_inc(live_ready, 1)

            first = Chain(dve, dve_steps, 12, 0)
            moments(first, 0)
            normalise(first, 0)
            live(first, 0)
            first.end()
            with dve.Fori(0, B) as b:
                v = Chain(dve, dve_steps, 15, b)
                v.base = b * 15 + 12
                mr = Ring(dve, m.m_banks, m_sems, M_U, b)
                for tt in range(TT):
                    bank = mr.take()
                    dve.tensor_tensor(q[:, tt, :], bank[:, 0:D], bq, ALU.add).then_inc(m_sems[1], 1)
                mr.wait_released(mr.n)
                for tt in range(TT):
                    ins = dve.tensor_scalar(q[:, tt, :], q[:, tt, :], row_live[:, tt:tt + 1], DK ** -0.5,
                                            ALU.mult, ALU.mult)
                    ins.then_inc(q_ready, 1) if tt == TT - 1 else v.step(ins)
                moments(v, b + 1)

                def remainders(t):
                    for part in range(2):
                        dve.wait_ge(kcast, b * CASTS + (K_ORDER.index((t, part)) + 1 + CASTS))
                        dve.tensor_tensor(kf[:, t, :], kf[:, t, :], k_part[:, t, part, 0:KEYS], ALU.subtract)\
                            .then_inc(ksub, 1)

                dve.wait_ge(v_stored, 16 * b + 16)
                for j in range(NKT):
                    r = min(P, KEYS - P * j)
                    bank = mr.take()
                    dve.tensor_tensor(v_aug[0:r, :, j, :].rearrange("p g (h c) -> p g h c", h=HG)[:, :, :, 0:DK],
                                      bank[0:r, 0:D].rearrange("p (g h c) -> p g h c", g=NG, h=HG),
                                      bv[0:r].rearrange("p (g h c) -> p g h c", g=NG, h=HG), ALU.add)\
                        .then_inc(m_sems[1], 1)
                remainders(0)
                dve.wait_ge(s_sems[1], b * S_U + (2 * KT + N_S))
                normalise(v, b + 1)
                dve.wait_ge(q_stored, 16 * b + 16)
                for n in range(0, H // 2, 2):
                    bank = mr.take().bitcast(BF16)
                    dve.tensor_copy(q_stack[:, 2 * n:2 * n + 2, :],
                                    bank[0:PARTS, :].rearrange("p (h n) -> p h n", h=2)).then_inc(m_sems[1], 1)
                remainders(1)
                dve.wait_ge(q_ready, b + 1)
                dve.wait_ge(flag_ready, b + 1)
                live(v, b + 1)
                v.end(), mr.end()


PER_STEP = 6
NATURAL_AT = 4 * PER_STEP + 3


def cross_side_work(j):
    units = [("max", hh, tt, c) for tt in range(TT) for hh in range(HG) for c in range(NCH)]
    work = units[PER_STEP * j:PER_STEP * (j + 1)]
    if j == 4:
        work.insert(2, ("natural",))
    if j == NKT - 1:
        work.append(("rows",))
    return work


def cross_phase(nc, sems, banks, consts, scr, ones):
    M_U, S_U = NG * (HG * TT * NCH + HG + 1), NG * NKT * HG
    PV_STEPS = NG * NKT
    G_MAX = HG * TT * NCH
    FIRST = G_MAX + HG
    with ExitStack() as ctx:
        m = Memory(nc, ctx, sems, "cross", banks)
        sb, sem, pv = m.sb, m.sem, m.pv
        ident_f, ident_b = consts["identf"], consts["identb"]
        k_stack = sb("k_stack", [ROWS, H, KEYS], BF16)
        q_stack = sb("q_stack", [ROWS, H, S], BF16)
        v_aug = sb("v_aug", [P, NG, NKT, HG, VW])
        mask_max = sb("mask_max", [P, TT, KEYS], BF16)
        mask_exp = sb("mask_exp", [P, TT, KEYS], BF16)
        flags = sb("flags", [1, B], I32)
        probs = sb("probs", [P, 2, HG, S])
        o_t, o_nat = sb("o_t", [P, S]), sb("o_nat", [P, 2, TT, HG, DK])
        junk = sb("junk", [P, 2, S], BF16)
        mx, neg = sb("mx", [P, TT * HG, NCH]), sb("neg", [P, TT * HG])
        neg_nat, rden = sb("neg_nat", [P, TT, HG, 3], BF16), sb("rden", [P, TT, HG])

        kqv_dma = [sem(f"kqv{g}_dma") for g in range(NG)]
        mask_max_dma = [sem(f"mask_max{tt}_dma") for tt in range(TT)]
        mask_exp_dma, flag_dma, ones_dma = sem("mask_exp_dma"), sem("flag_dma"), sem("ones_dma")
        o_stored = [sem(f"o_stored{i}") for i in range(2)]
        s_sems, m_sems = (sem("s_full"), sem("s_free")), (sem("m_full"), sem("m_free"))
        pv_done, pv_copied = sem("pv_done"), sem("pv_copied")
        neg_ready = sem("neg_ready")
        dve_steps, waits_apart = sem("dve_steps"), sem("waits_apart")
        KQV = 16 * (6 + 2)
        block = ctx.enter_context(nc.Block())

        @block.sync
        def _(sp):
            def load_group(b, g):
                rows = slice(g * HG * DK, (g + 1) * HG * DK)
                for part, blocks in enumerate(K_BLOCKS):
                    for blk in blocks:
                        sp.dma_start(k_stack[blk * DK:(blk + 1) * DK, g * HG:(g + 1) * HG, :],
                                     scr["k"][part, b, rows, :].rearrange("(h d) n -> d h n", h=HG))\
                            .then_inc(kqv_dma[g], 16)
                sp.dma_start(q_stack[0:PARTS, g * HG:(g + 1) * HG, :].rearrange("p h n -> p (h n)"),
                             scr["q"][b, :, g, :]).then_inc(kqv_dma[g], 16)
                sp.dma_start(v_aug[:, g].rearrange("p j h c -> p (j h c)"), scr["v"][b, :, g, :])\
                    .then_inc(kqv_dma[g], 16)

            def load_mask_max(b, tt):
                sp.dma_start(mask_max[:, tt, :], scr["mask"][b, :, tt, :]).then_inc(mask_max_dma[tt], 16)

            sp.dma_start(k_stack[PARTS:ROWS, :, :], ones).then_inc(ones_dma, 16)
            sp.dma_start(flags[:], scr["flag"]).then_inc(flag_dma, 16)
            for stored in o_stored:
                sp.sem_inc(stored, 16)
            load_group(0, 0)
            for tt in range(TT):
                load_mask_max(0, tt)
            for g in range(1, NG):
                load_group(0, g)
            sp.dma_start(mask_exp[:], scr["mask"][0]).then_inc(mask_exp_dma, 16)
            with sp.Fori(0, B) as b:
                for g in range(NG):
                    sp.wait_ge(m_sems[1], b * M_U + (g * (G_MAX + HG + 1) + NATURAL_AT + FIRST + N_M))
                    sp.dma_start(scr["o"][b * NG + g], o_nat[:, g % 2]).then_inc(o_stored[g % 2], 16)
                    if g == NG - 2:
                        for tt in range(TT):
                            sp.wait_ge(m_sems[1], b * M_U + (g * (G_MAX + HG + 1) + 1 + (tt + 1) * HG * NCH
                                                             + FIRST + N_M))
                            apart(sp, waits_apart)
                            load_mask_max(next_batch(b), tt)
                    sp.wait_ge(pv_done, b * PV_STEPS + ((g + 1) * NKT + 2))
                    apart(sp, waits_apart)
                    load_group(next_batch(b), g)
                sp.dma_start(mask_exp[:], scr["mask"][next_batch(b)]).then_inc(mask_exp_dma, 16)
            sp.wait_ge(m_sems[1], M_U * B + (FIRST + 1 + N_M))
            sp.dma_start(scr["o"][B * NG], o_nat[:, 0]).then_inc(o_stored[0], 16)
            sp.wait_ge(o_stored[0], 16 * (B * NG // 2 + 2))
            sp.wait_ge(o_stored[1], 16 * (B * NG // 2 + 1))
            for s in kqv_dma:
                sp.wait_ge(s, KQV * (B + 1))
            for s in mask_max_dma + [mask_exp_dma]:
                sp.wait_ge(s, 16 * (B + 1))

        @block.tensor
        def _(pe):
            mm, tr = pe.matmul, pe.transpose
            pe.wait_ge(ones_dma, 16)
            pe.wait_ge(flag_dma, 16)

            def max_chunk(mr, g, hh, tt, c):
                h, (lo, w) = HG * g + hh, CHUNKS[c]
                bank = mr.acquire()
                mm(bank[:, 0:w], q_stack[0:PARTS, h, tt * P:(tt + 1) * P], k_stack[0:PARTS, h, lo:lo + w],
                   start=True, stop=True).then_inc(m_sems[0], 1)

            def max_rows(mr, groups):
                pe.wait_ge(neg_ready, groups + 1)
                for hh in range(HG):
                    bank = mr.acquire().bitcast(BF16)
                    for tt in range(TT):
                        last = tr(bank[PARTS:ROWS, tt * P:(tt + 1) * P], neg_nat[:, tt, hh, :], ident_b[:])
                    last.then_inc(m_sems[0], 1)

            def natural(mr, groups):
                pe.wait_ge(pv_copied, groups + 1)
                bank = mr.acquire()
                for tt in range(TT):
                    last = tr(bank[:, tt * P:(tt + 1) * P], o_t[:, tt * P:(tt + 1) * P], ident_f[:])
                last.then_inc(m_sems[0], 1)

            first = Ring(pe, m.m_banks, m_sems, M_U, 0)
            pe.wait_ge(kqv_dma[0], KQV)
            for work in [w for j in range(NKT) for w in cross_side_work(j) if w[0] == "max"]:
                max_chunk(first, 0, *work[1:])
            max_rows(first, 0)
            assert first.n == G_MAX + HG

            def group_of_heads(b, g, sr, mr, masked):
                mr.wait_released(mr.n)
                for j in range(NKT):
                    r = min(P, KEYS - P * j)
                    side = cross_side_work(j)
                    if j == 0:
                        nxt = (g + 1) % NG
                        pe.wait_ge(kqv_dma[nxt], b * KQV + (KQV * (2 if nxt == 0 else 1)))

                    def beside(n):
                        for work in side[:n]:
                            if work[0] == "max":
                                max_chunk(mr, nxt, *work[1:])
                            elif work[0] == "natural":
                                natural(mr, b * NG + g)
                            else:
                                max_rows(mr, b * NG + g + 1)
                        del side[:n]

                    for hh in range(HG):
                        h = HG * g + hh
                        bank = sr.acquire()
                        if masked:
                            for tt in range(TT):
                                mm(bank[0:r, tt * P:(tt + 1) * P], mask_exp[:, tt, j * P:j * P + r], ident_b[:],
                                   start=tt == 0, stop=False, skip_group_check=True)
                        mm(bank[0:r, :], k_stack[0:ROWS, h, j * P:j * P + r], q_stack[0:ROWS, h, :],
                           start=not masked, stop=True, skip_group_check=masked).then_inc(s_sems[0], 1)
                        beside(1)
                    if j > 0:
                        products(b, g, sr, j - 1, sr.n - HG)
                    beside(len(side))
                products(b, g, sr, NKT - 1, sr.n)

            def products(b, g, sr, j, exps):
                r = min(P, KEYS - P * j)
                sr.wait_released(exps)
                if j == 0:
                    pe.wait_ge(pv_copied, b * NG + g + 1)
                for hh in range(HG):
                    last = mm(pv[32 * hh:32 * hh + VW, :], v_aug[0:r, g, j, hh, :],
                              probs[0:r, (g * NKT + j) % 2, hh, :], start=j == 0, stop=j == NKT - 1)
                last.then_inc(pv_done, 1)

            def heads_of_batch(b, masked):
                sr, mr = Ring(pe, m.s_banks, s_sems, S_U, b), later_ring(pe, m.m_banks, m_sems, M_U, FIRST, b)
                if masked:
                    pe.wait_ge(mask_exp_dma, 16 * b + 16)
                for g in range(NG):
                    group_of_heads(b, g, sr, mr, masked)
                sr.end(), mr.end()

            with pe.Fori(0, B) as b:
                with pe.If(pe.value_load(flags[0:1, bass.ds(b, 1)])):
                    heads_of_batch(b, True)
                with pe.Else():
                    heads_of_batch(b, False)
            last = later_ring(pe, m.m_banks, m_sems, M_U, FIRST, B)
            natural(last, B * NG)

        @block.scalar
        def _(act):
            act.sem_inc(s_sems[1], N_S)
            act.sem_inc(pv_done, 2)
            act.sem_inc(pv_copied, 1)
            with act.Fori(0, B) as b:
                sr = Ring(act, m.s_banks, s_sems, S_U, b)
                for step in range(PV_STEPS):
                    r = min(P, KEYS - P * (step % NKT))
                    act.wait_ge(pv_done, b * PV_STEPS + (step + 1))
                    for hh in range(HG):
                        bank = sr.take()
                        act.activation(probs[0:r, step % 2, hh, :], bank[0:r, :], ACT.Exp).then_inc(s_sems[1], 1)
                sr.end()

        @block.vector
        def _(dve):
            dve.memset(pv, 0.0).then_inc(dve_steps, 1)
            dve.memset(o_t[:], 1.0).then_inc(dve_steps, 1)
            dve.wait_ge(dve_steps, 2)
            dve.sem_inc(m_sems[1], N_M)

            def masked_max(mr, hh, tt, c):
                lo, w = CHUNKS[c]
                mr.wait_released(mr.n - 1)
                bank = mr.take()
                apart(dve, waits_apart)
                dve.tensor_tensor_reduce(junk[:, mr.n % 2, 0:w], bank[:, 0:w], mask_max[:, tt, lo:lo + w], 1.0,
                                         -FLT_MAX, ALU.add, ALU.max, mx[:, tt * HG + hh, c:c + 1])\
                    .then_inc(m_sems[1], 1)

            def negate(v, mr):
                mr.wait_released(mr.n)
                v(dve.tensor_reduce(neg[:], mx[:], AX.X, ALU.max, negate=True))
                flat = neg_nat[:].rearrange("p t h c -> p (t h) c")
                for part in range(3):
                    ins = dve.tensor_copy(flat[:, :, part], neg[:])
                    if part < 2:
                        v(ins)
                        v(dve.tensor_tensor(neg[:], neg[:], flat[:, :, part], ALU.subtract))
                    else:
                        ins.then_inc(neg_ready, 1)

            def rows_in(mr, g):
                for hh in range(HG):
                    bank = mr.take().bitcast(BF16)
                    dve.tensor_copy(q_stack[PARTS:ROWS, HG * g + hh, :], bank[PARTS:ROWS, 0:S]).then_inc(m_sems[1], 1)

            def natural(v, mr, slot):
                bank = mr.take().rearrange("p (t h c) -> p t h c", t=TT, h=HG)
                v(dve.reciprocal(rden[:], bank[:, :, :, DK]))
                dve.tensor_tensor(o_nat[:, slot], bank[:, :, :, 0:DK],
                                  rden[:].unsqueeze(3).to_broadcast([P, TT, HG, DK]), ALU.mult).then_inc(m_sems[1], 1)

            first, v = Ring(dve, m.m_banks, m_sems, M_U, 0), Chain(dve, dve_steps, 5, 0)
            v.base = 2
            for work in [w for j in range(NKT) for w in cross_side_work(j) if w[0] == "max"]:
                if first.n % (HG * NCH) == 0:
                    dve.wait_ge(mask_max_dma[work[2]], 16)
                if first.n == 0:
                    lo, w = CHUNKS[0]
                    bank = first.take()
                    dve.tensor_tensor_reduce(junk[:, 1, 0:w], bank[:, 0:w], mask_max[:, 0, lo:lo + w], 1.0,
                                             -FLT_MAX, ALU.add, ALU.max, mx[:, 0, 0:1]).then_inc(m_sems[1], 1)
                else:
                    masked_max(first, *work[1:])
            negate(v, first)
            rows_in(first, 0)
            v.end()
            with dve.Fori(0, B) as b:
                v, mr = Chain(dve, dve_steps, 6 * NG, b), later_ring(dve, m.m_banks, m_sems, M_U, FIRST, b)
                v.base = b * v.per + 7
                for g in range(NG):
                    nxt = (g + 1) % NG
                    for j in range(NKT):
                        for work in cross_side_work(j):
                            if work[0] == "max":
                                if work[1] == 0 and work[3] == 0 and nxt == 0:
                                    dve.wait_ge(mask_max_dma[work[2]], 16 * b + 32)
                                masked_max(mr, *work[1:])
                            elif work[0] == "natural":
                                dve.wait_ge(o_stored[g % 2], b * (16 * NG // 2) + 16 * (g // 2 + 1))
                                natural(v, mr, g % 2)
                            else:
                                negate(v, mr)
                                rows_in(mr, nxt)
                    dve.wait_ge(pv_done, b * PV_STEPS + ((g + 1) * NKT + 2))
                    dve.tensor_copy(o_t[:], pv).then_inc(pv_copied, 1)
                v.end(), mr.end()
            last = later_ring(dve, m.m_banks, m_sems, M_U, FIRST, B)
            bank = last.take().rearrange("p (t h c) -> p t h c", t=TT, h=HG)
            v = Chain(dve, dve_steps, 1, 0)
            v.base = B * 6 * NG + 7
            v(dve.reciprocal(rden[:], bank[:, :, :, DK]))
            dve.wait_ge(o_stored[0], 16 * (B * NG // 2 + 1))
            dve.tensor_tensor(o_nat[:, 0], bank[:, :, :, 0:DK], rden[:].unsqueeze(3).to_broadcast([P, TT, HG, DK]),
                              ALU.mult).then_inc(m_sems[1], 1)


def stack_of_two(eng, bank_of, src, pair, ident_b):
    bank = bank_of.bitcast(BF16)
    for i in range(2):
        for tt in range(TT):
            at = i * S + tt * P
            last = eng.transpose(bank[0:PARTS, at:at + P], src[:, tt, 2 * pair + i, :], ident_b)
    return last


def self_inputs_phase(nc, sems, banks, consts, x, w_cross, w_self, scr):
    BY_DVE = 4
    PAIRS = H // 2
    M_ROWS, S_ROWS = 2 * TT, 2 * KT + TT
    M_U, S_U = M_ROWS + 2 * PAIRS // BY_DVE, S_ROWS + 2 * (PAIRS - PAIRS // BY_DVE)
    INPUTS = 16 * (1 + NG)
    with ExitStack() as ctx:
        m = Memory(nc, ctx, sems, "inputs", banks)
        sb, sem = m.sb, m.sem
        ident_f, ident_b, half, row_c = (consts[n] for n in ("identf", "identb", "half", "row_c"))
        bo, n1w, qkw = row_c[:, 2 * D:3 * D], row_c[:, 3 * D:4 * D], row_c[:, 5 * D:7 * D]
        wo, wqkv = sb("wo", [P, KT, D]), sb("wqkv", [P, KT, 3 * D])
        x_in, o_nat, o_natT = sb("x_in", [P, TT, D]), sb("o_nat", [P, TT, D]), sb("o_natT", [P, KT, S])
        x1, xn = sb("x1", [P, TT, D]), sb("xn", [P, TT, D])
        nat, natT = sb("nat", [P, TT, D]), sb("natT", [P, KT, S])
        qk, squares = sb("qk", [P, TT, 2 * D]), sb("squares", [P, TT, 2 * D])
        vs = sb("vs", [P, NG, TT, HG, VW])
        q_nat, k_nat = sb("q_nat", [P, TT, H, PARTS], BF16), sb("k_nat", [P, TT, H, PARTS], BF16)
        q_stack, k_stack = sb("q_stack", [PARTS, H, S], BF16), sb("k_stack", [PARTS, H, S], BF16)
        junk, stats, mv = sb("junk", [P, TT, D], BF16), sb("stats", [P, TT, 6]), sb("mv", [P, TT, 2])
        sums = sb("sums", [P, TT])
        ln_ms, ln_rs, rms_ms, rms_rs = (sb(n, [P, TT]) for n in ("ln_ms", "ln_rs", "rms_ms", "rms_rs"))
        head_ms, head_rs = sb("head_ms", [P, 2 * TT * H]), sb("head_rs", [P, 2 * TT * H])

        w_dma, in_dma, setup = sem("w_dma"), sem("in_dma"), sem("setup")
        x1_stored, xn_stored = sem("x1_stored"), sem("xn_stored")
        q_stored, k_stored, v_stored = sem("q_stored"), sem("k_stored"), sem("v_stored")
        s_sems, m_sems = (sem("s_full"), sem("s_free")), (sem("m_full"), sem("m_free"))
        x1_ready, xn_ready, nat_ready = sem("x1_ready"), sem("xn_ready"), sem("nat_ready")
        ln_in, ln_out, rms_in, rms_out, head_in, head_out = (
            sem(n) for n in ("ln_in", "ln_out", "rms_in", "rms_out", "head_in", "head_out"))
        keys_ready, queries_ready = sem("keys_ready"), sem("queries_ready")
        k_split, q_split = ((sem(f"{n}_cast"), sem(f"{n}_left"), sem(f"{n}_copied")) for n in "kq")
        dve_steps, waits_apart = sem("dve_steps"), sem("waits_apart")
        queries, keys = heads(qk[:, :, 0:D]), heads(qk[:, :, D:2 * D])

        def q_part(i):
            return q_nat[:, :, :, i * DK:(i + 1) * DK]

        def k_part(i):
            return k_nat[:, :, :, i * DK:(i + 1) * DK]
        block = ctx.enter_context(nc.Block())

        @block.sync
        def _(sp):
            def load_inputs(b):
                sp.dma_start(x_in[:], x[b]).then_inc(in_dma, 16)
                for g in range(NG):
                    sp.dma_start(o_nat[:, :, g * HG * DK:(g + 1) * HG * DK],
                                 scr["o"][b * NG + (g + 1)].rearrange("p t h c -> p t (h c)")).then_inc(in_dma, 16)

            def rows(b):
                sp.wait_ge(x1_ready, b + 1)
                apart(sp, waits_apart)
                load_inputs(next_batch(b))
                sp.dma_start(scr["x1"][b], x1[:]).then_inc(x1_stored, 16)
                sp.wait_ge(xn_ready, b + 1)
                sp.dma_start(scr["xn"][b], xn[:]).then_inc(xn_stored, 16)

            sp.dma_start(wo[:], w_cross[:, 3]).then_inc(w_dma, 16)
            sp.dma_start(wqkv[:], w_self[:, :, 0:3 * D]).then_inc(w_dma, 16)
            load_inputs(0)
            for stored in (x1_stored, xn_stored, q_stored, k_stored, v_stored):
                sp.sem_inc(stored, 16)
            rows(0)
            sp.wait_ge(m_sems[1], M_ROWS + N_M)
            sp.dma_start(scr["vs"][0], vs[:].rearrange("p g j h c -> p g (j h c)")).then_inc(v_stored, 16)
            with sp.Fori(0, B) as b:
                rows(b + 1)
                sp.wait_ge(m_sems[1], b * M_U + (M_ROWS + TT + PAIRS // BY_DVE + N_M))
                sp.wait_ge(s_sems[1], b * S_U + (S_ROWS + KT + PAIRS - PAIRS // BY_DVE + N_S))
                sp.dma_start(scr["qs"][b], q_stack[:].rearrange("p (g h) n -> p g (h n)", g=NG)).then_inc(q_stored, 16)
                sp.wait_ge(m_sems[1], b * M_U + (M_ROWS + TT + 2 * PAIRS // BY_DVE + N_M))
                apart(sp, waits_apart)
                sp.wait_ge(s_sems[1], b * S_U + (S_ROWS + 2 * KT + 2 * (PAIRS - PAIRS // BY_DVE) + N_S))
                sp.dma_start(scr["ks"][b], k_stack[:].rearrange("p (g h) n -> p g (h n)", g=NG)).then_inc(k_stored, 16)
                sp.wait_ge(m_sems[1], b * M_U + (M_ROWS + M_U + N_M))
                sp.dma_start(scr["vs"][b + 1], vs[:].rearrange("p g j h c -> p g (j h c)")).then_inc(v_stored, 16)
            for stored, n in ((x1_stored, B + 2), (xn_stored, B + 2), (q_stored, B + 1), (k_stored, B + 1),
                              (v_stored, B + 2)):
                sp.wait_ge(stored, 16 * n)
            sp.wait_ge(in_dma, INPUTS * (B + 2))

        @block.gpsimd
        def _(pool):
            pool.memset(vs[:], 1.0).then_inc(setup, 1)

            def root(b, sem_in, sem_out, ms, rs, width):
                pool.wait_ge(sem_in, b + 1)
                pool.tensor_tensor(rs[:], ms[:], half[:, 0:width], ALU.pow).then_inc(sem_out, 1)

            root(0, ln_in, ln_out, ln_ms, ln_rs, TT)
            root(0, rms_in, rms_out, rms_ms, rms_rs, TT)
            with pool.Fori(0, B) as b:
                root(b, head_in, head_out, head_ms, head_rs, 2 * TT * H)
                root(b + 1, ln_in, ln_out, ln_ms, ln_rs, TT)
                root(b + 1, rms_in, rms_out, rms_ms, rms_rs, TT)
                subtract_parts(pool, k_part, keys, K_BLOCKS, k_split, waits_apart, b)

        @block.tensor
        def _(pe):
            mm, tr = pe.matmul, pe.transpose
            pe.wait_ge(w_dma, 32)
            pe.wait_ge(setup, 1)

            def transposed(sr, src):
                for kt in range(KT):
                    bank = sr.acquire()
                    for tt in range(TT):
                        last = tr(bank[:, tt * P:(tt + 1) * P], src[:, tt, kt * P:(kt + 1) * P], ident_f)
                    last.then_inc(s_sems[0], 1)

            def project(ring, full, src, w, width):
                for tt in range(TT):
                    bank = ring.acquire()
                    for kt in range(KT):
                        last = mm(bank[:, 0:width], src[:, kt, tt * P:(tt + 1) * P], w[:, kt, :],
                                  start=kt == 0, stop=kt == KT - 1)
                    last.then_inc(full, 1)

            def project_out(sr, mr, b):
                pe.wait_ge(in_dma, INPUTS * b + INPUTS)
                transposed(sr, o_nat)
                sr.wait_released(sr.n)
                project(mr, m_sems[0], o_natT, wo, D)

            def stacks(sr, mr, src):
                for pair in range(PAIRS):
                    ring, full = (sr, s_sems[0]) if pair % BY_DVE else (mr, m_sems[0])
                    stack_of_two(pe, ring.acquire(), src, pair, ident_b).then_inc(full, 1)

            def project_qkv(sr, mr):
                project(sr, s_sems[0], natT, wqkv[:, :, 0:2 * D], 2 * D)
                project(mr, m_sems[0], natT, wqkv[:, :, 2 * D:3 * D], D)

            sr, mr = Ring(pe, m.s_banks, s_sems, S_U, 0), Ring(pe, m.m_banks, m_sems, M_U, 0)
            project_out(sr, mr, 0)
            pe.wait_ge(nat_ready, 1)
            transposed(sr, nat)
            sr.wait_released(sr.n)
            project_qkv(sr, mr)
            assert (sr.n, mr.n) == (S_ROWS, M_ROWS)
            with pe.Fori(0, B) as b:
                sr = later_ring(pe, m.s_banks, s_sems, S_U, S_ROWS, b)
                mr = later_ring(pe, m.m_banks, m_sems, M_U, M_ROWS, b)
                project_out(sr, mr, b + 1)
                wait_split(pe, q_split, b)
                stacks(sr, mr, q_nat)
                pe.wait_ge(nat_ready, b + 2)
                transposed(sr, nat)
                wait_split(pe, k_split, b)
                stacks(sr, mr, k_nat)
                sr.wait_released(S_U - TT - (PAIRS - PAIRS // BY_DVE))
                project_qkv(sr, mr)
                sr.end(), mr.end()

        @block.scalar
        def _(act):
            act.sem_inc(s_sems[1], N_S)

            def copies(sr, dst, n, width=S):
                for i in range(n):
                    bank = sr.take()
                    act.activation(dst[:, i, 0:width], bank[:, 0:width], ACT.Copy).then_inc(s_sems[1], 1)

            def stacks(sr, dst):
                for pair in range(PAIRS):
                    if pair % BY_DVE:
                        bank = sr.take().bitcast(BF16)
                        act.activation(dst[:, 2 * pair:2 * pair + 2, :],
                                       bank[0:PARTS, :].rearrange("p (h n) -> p h n", h=2), ACT.Copy)\
                            .then_inc(s_sems[1], 1)

            sr = Ring(act, m.s_banks, s_sems, S_U, 0)
            copies(sr, o_natT, KT)
            copies(sr, natT, KT)
            copies(sr, qk, TT)
            with act.Fori(0, B) as b:
                sr = later_ring(act, m.s_banks, s_sems, S_U, S_ROWS, b)
                copies(sr, o_natT, KT)
                act.wait_ge(keys_ready, b + 1)
                cast_part(act, k_part, keys, K_BLOCKS, 0, k_split, b)
                cast_part(act, k_part, keys, K_BLOCKS, 1, k_split, b)
                act.wait_ge(queries_ready, b + 1)
                cast_part(act, q_part, queries, Q_BLOCKS, 0, q_split, b)
                cast_part(act, k_part, keys, K_BLOCKS, 2, k_split, b)
                cast_part(act, q_part, queries, Q_BLOCKS, 1, q_split, b)
                cast_part(act, q_part, queries, Q_BLOCKS, 2, q_split, b)
                act.wait_ge(q_stored, 16 * b + 16)
                stacks(sr, q_stack)
                copies(sr, natT, KT)
                act.wait_ge(k_stored, 16 * b + 16)
                stacks(sr, k_stack)
                act.wait_ge(q_split[0], b * 3 + 3)
                act.wait_ge(k_split[0], b * 3 + 3)
                copies(sr, qk, TT)
                sr.end()

        @block.vector
        def _(dve):
            dve.wait_ge(setup, 1)
            dve.sem_inc(m_sems[1], N_M)

            def rows_x1(v, mr, b):
                dve.wait_ge(in_dma, INPUTS * b + INPUTS)
                for tt in range(TT):
                    v.step(dve.tensor_tensor(x_in[:, tt, :], x_in[:, tt, :], bo, ALU.add))
                dve.wait_ge(x1_stored, 16 * b + 16)
                v.settle()
                for tt in range(TT):
                    bank = mr.take()
                    dve.tensor_tensor(x1[:, tt, :], bank[:, 0:D], x_in[:, tt, :], ALU.add).then_inc(m_sems[1], 1)
                mr.wait_released(mr.n)
                dve.sem_inc(x1_ready, 1)
                for tt in range(TT):
                    v.step(dve.bn_stats(stats[:, tt, :], x1[:, tt, :]))
                v.settle()
                apart(dve, waits_apart)
                for tt in range(TT):
                    v.step(dve.bn_aggr(mv[:, tt, :], stats[:, tt, :]))
                v.settle()
                dve.tensor_scalar(ln_ms[:], mv[:, :, 1], LN_EPS, None, ALU.add).then_inc(ln_in, 1)

            def rows_xn(v, b):
                dve.wait_ge(ln_out, b + 1)
                dve.wait_ge(xn_stored, 16 * b + 16)
                for tt in range(TT):
                    v.step(dve.tensor_scalar(xn[:, tt, :], x1[:, tt, :], mv[:, tt, 0:1], ln_rs[:, tt:tt + 1],
                                             ALU.subtract, ALU.mult))
                v.settle()
                dve.sem_inc(xn_ready, 1)
                for tt in range(TT):
                    v.step(dve.tensor_tensor_reduce(junk[:, tt, :], xn[:, tt, :], xn[:, tt, :], 1.0, 0.0,
                                                    ALU.mult, ALU.add, sums[:, tt:tt + 1]))
                v.settle()
                dve.tensor_scalar(rms_ms[:], sums[:], 1.0 / D, RMS_EPS, ALU.mult, ALU.add).then_inc(rms_in, 1)

            def rows_nat(v, b):
                dve.wait_ge(rms_out, b + 1)
                for tt in range(TT):
                    ins = dve.scalar_tensor_tensor(nat[:, tt, :], xn[:, tt, :], rms_rs[:, tt:tt + 1], n1w,
                                                   ALU.mult, ALU.mult)
                    ins.then_inc(nat_ready, 1) if tt == TT - 1 else v.step(ins)

            def values(mr, b):
                dve.wait_ge(v_stored, 16 * b + 16)
                for tt in range(TT):
                    bank = mr.take()
                    dve.tensor_copy(vs[:, :, tt, :, 0:DK], bank[:, 0:D].rearrange("p (g h c) -> p g h c", g=NG, h=HG))\
                        .then_inc(m_sems[1], 1)

            def stacks(mr, dst):
                for pair in range(0, PAIRS, BY_DVE):
                    bank = mr.take().bitcast(BF16)
                    dve.tensor_copy(dst[:, 2 * pair:2 * pair + 2, :],
                                    bank[0:PARTS, :].rearrange("p (h n) -> p h n", h=2)).then_inc(m_sems[1], 1)

            v, mr = Chain(dve, dve_steps, 23, 0), Ring(dve, m.m_banks, m_sems, M_U, 0)
            rows_x1(v, mr, 0)
            rows_xn(v, 0)
            rows_nat(v, 0)
            values(mr, 0)
            v.end()
            with dve.Fori(0, B) as b:
                v, mr = Chain(dve, dve_steps, 42, b), later_ring(dve, m.m_banks, m_sems, M_U, M_ROWS, b)
                v.base = b * v.per + 23
                dve.wait_ge(s_sems[1], b * S_U + (S_ROWS + N_S))
                for tt in range(TT):
                    v.step(dve.tensor_tensor(squares[:, tt, :], qk[:, tt, :], qk[:, tt, :], ALU.mult))
                v.settle()
                v(dve.tensor_reduce(head_ms[:], squares[:].rearrange("p t (h c) -> p (t h) c", c=DK), AX.X, ALU.add))
                dve.tensor_scalar(head_ms[:], head_ms[:], 1.0 / DK, RMS_EPS, ALU.mult, ALU.add).then_inc(head_in, 1)
                rows_x1(v, mr, b + 1)

                def head_norm(lo, ready):
                    for tt in range(TT):
                        view = qk[:, tt, lo:lo + D].rearrange("p (h c) -> p h c", c=DK)
                        r0 = tt * 2 * H + lo // DK
                        v.step(dve.tensor_tensor(view, view, head_rs[:, r0:r0 + H].unsqueeze(2)
                                                 .to_broadcast([P, H, DK]), ALU.mult))
                    v.settle()
                    for tt in range(TT):
                        ins = dve.tensor_tensor(qk[:, tt, lo:lo + D], qk[:, tt, lo:lo + D], qkw[:, lo:lo + D], ALU.mult)
                        ins.then_inc(ready, 1) if tt == TT - 1 else v.step(ins)

                dve.wait_ge(head_out, b + 1)
                head_norm(D, keys_ready)
                rows_xn(v, b + 1)
                head_norm(0, queries_ready)
                rows_nat(v, b + 1)
                subtract_parts(dve, q_part, queries, Q_BLOCKS, q_split, waits_apart, b)
                dve.wait_ge(q_stored, 16 * b + 16)
                stacks(mr, q_stack)
                dve.wait_ge(k_stored, 16 * b + 16)
                stacks(mr, k_stack)
                values(mr, b + 1)
                v.end(), mr.end()


def self_side_work(j):
    units = [("max", hh, tt) for hh in range(HG) for tt in range(TT)]
    work = units[6 * j:6 * (j + 1)]
    if j == 0:
        work.insert(3, ("natural",))
    if j == TT - 1:
        work.append(("rows",))
    return work


def self_phase(nc, sems, banks, consts, scr, ones):
    G_M, G_S = HG * TT + 2, HG * TT + HG - 1
    M_U, S_U = NG * G_M, NG * G_S
    M_FIRST, S_FIRST = HG * TT + 1, HG - 1
    PV_STEPS = NG * TT
    with ExitStack() as ctx:
        m = Memory(nc, ctx, sems, "self", banks)
        sb, sem, pv = m.sb, m.sem, m.pv
        ident_f, ident_b, causal_q, causal_k = (consts[n] for n in ("identf", "identb", "causal_q", "causal_k"))
        k_stack = sb("k_stack", [ROWS, H, S], BF16)
        q_stack = sb("q_stack", [ROWS, H, S], BF16)
        vs = sb("vs", [P, NG, TT, HG, VW])
        probs = sb("probs", [P, 2, HG, S])
        o_t, o_nat = sb("o_t", [P, S]), sb("o_nat", [P, 2, TT, HG, DK])
        junk = sb("junk", [P, 2, S], BF16)
        mx, neg = sb("mx", [P, TT * HG]), sb("neg", [P, TT * HG])
        neg_nat, rden = sb("neg_nat", [P, TT, HG, 3], BF16), sb("rden", [P, TT, HG])

        kqv_dma = [sem(f"kqv{g}_dma") for g in range(NG)]
        ones_dma = sem("ones_dma")
        o_stored = [sem(f"o_stored{i}") for i in range(2)]
        s_sems, m_sems = (sem("s_full"), sem("s_free")), (sem("m_full"), sem("m_free"))
        pv_done, pv_copied = sem("pv_done"), sem("pv_copied")
        neg_ready = sem("neg_ready")
        dve_steps, waits_apart = sem("dve_steps"), sem("waits_apart")
        KQV = 16 * 3
        NATURAL = 4
        block = ctx.enter_context(nc.Block())

        @block.sync
        def _(sp):
            def load_group(b, g):
                hs = slice(g * HG, (g + 1) * HG)
                for stack, name in ((k_stack, "ks"), (q_stack, "qs")):
                    sp.dma_start(stack[0:PARTS, hs, :].rearrange("p h n -> p (h n)"), scr[name][b, :, g, :])\
                        .then_inc(kqv_dma[g], 16)
                sp.dma_start(vs[:, g].rearrange("p j h c -> p (j h c)"), scr["vs"][b, :, g, :])\
                    .then_inc(kqv_dma[g], 16)

            sp.dma_start(k_stack[PARTS:ROWS, :, :], ones[:, :, 0:S]).then_inc(ones_dma, 16)
            for stored in o_stored:
                sp.sem_inc(stored, 16)
            for g in range(NG):
                load_group(0, g)
            with sp.Fori(0, B) as b:
                for g in range(NG):
                    sp.wait_ge(m_sems[1], b * M_U + (g * G_M + NATURAL + M_FIRST + N_M))
                    sp.dma_start(scr["os"][b * NG + g], o_nat[:, g % 2]).then_inc(o_stored[g % 2], 16)
                    sp.wait_ge(pv_done, b * PV_STEPS + ((g + 1) * TT + 2))
                    apart(sp, waits_apart)
                    load_group(next_batch(b), g)
            sp.wait_ge(m_sems[1], M_U * B + (M_FIRST + 1 + N_M))
            sp.dma_start(scr["os"][B * NG], o_nat[:, 0]).then_inc(o_stored[0], 16)
            sp.wait_ge(o_stored[0], 16 * (B * NG // 2 + 2))
            sp.wait_ge(o_stored[1], 16 * (B * NG // 2 + 1))
            for s in kqv_dma:
                sp.wait_ge(s, KQV * (B + 1))

        @block.tensor
        def _(pe):
            mm, tr = pe.matmul, pe.transpose
            pe.wait_ge(ones_dma, 16)

            def max_tile(mr, g, hh, tt):
                h, w = HG * g + hh, P * (tt + 1)
                bank = mr.acquire()
                mm(bank[:, 0:w], q_stack[0:PARTS, h, tt * P:(tt + 1) * P], k_stack[0:PARTS, h, 0:w],
                   start=True, stop=True).then_inc(m_sems[0], 1)

            def max_rows(sr, mr, groups):
                pe.wait_ge(neg_ready, groups + 1)
                for hh in range(HG):
                    ring, full = (sr, s_sems[0]) if hh else (mr, m_sems[0])
                    bank = ring.acquire().bitcast(BF16)
                    for tt in range(TT):
                        last = tr(bank[PARTS:ROWS, tt * P:(tt + 1) * P], neg_nat[:, tt, hh, :], ident_b)
                    last.then_inc(full, 1)

            def natural(mr, groups):
                pe.wait_ge(pv_copied, groups + 1)
                bank = mr.acquire()
                for tt in range(TT):
                    last = tr(bank[:, tt * P:(tt + 1) * P], o_t[:, tt * P:(tt + 1) * P], ident_f)
                last.then_inc(m_sems[0], 1)

            sr, mr = Ring(pe, m.s_banks, s_sems, S_U, 0), Ring(pe, m.m_banks, m_sems, M_U, 0)
            pe.wait_ge(kqv_dma[0], KQV)
            for work in [w for j in range(TT) for w in self_side_work(j) if w[0] == "max"]:
                max_tile(mr, 0, *work[1:])
            max_rows(sr, mr, 0)
            assert (mr.n, sr.n) == (M_FIRST, S_FIRST)

            def products(b, g, sr, j, exps):
                sr.wait_released(exps)
                if j == 0:
                    pe.wait_ge(pv_copied, b * NG + g + 1)
                for hh in range(HG):
                    last = mm(pv[32 * hh:32 * hh + VW, P * j:S], vs[:, g, j, hh, :],
                              probs[:, j % 2, hh, 0:S - P * j], start=j == 0, stop=j == TT - 1)
                last.then_inc(pv_done, 1)

            with pe.Fori(0, B) as b:
                sr = later_ring(pe, m.s_banks, s_sems, S_U, S_FIRST, b)
                mr = later_ring(pe, m.m_banks, m_sems, M_U, M_FIRST, b)
                for g in range(NG):
                    nxt = (g + 1) % NG
                    mr.wait_released(mr.n)
                    sr.wait_released(sr.n)
                    pe.wait_ge(kqv_dma[nxt], b * KQV + (KQV * (2 if nxt == 0 else 1)))
                    for j in range(TT):
                        lo, side = P * j, self_side_work(j)

                        def beside(n):
                            for work in side[:n]:
                                if work[0] == "max":
                                    max_tile(mr, nxt, *work[1:])
                                elif work[0] == "natural":
                                    natural(mr, b * NG + g)
                                else:
                                    max_rows(sr, mr, b * NG + g + 1)
                            del side[:n]

                        for hh in range(HG):
                            h = HG * g + hh
                            bank = sr.acquire()
                            mm(bank[:, 0:S - lo], k_stack[0:ROWS, h, lo:lo + P], q_stack[0:ROWS, h, lo:S],
                               start=True, stop=False)
                            mm(bank[:, 0:P], ident_b, causal_k, start=False, stop=True).then_inc(s_sems[0], 1)
                            if side and side[0][0] != "rows":
                                beside(1)
                        exps = sr.n
                        if j > 0:
                            products(b, g, sr, j - 1, exps - HG)
                        beside(len(side))
                    products(b, g, sr, TT - 1, exps)
                sr.end(), mr.end()
            natural(later_ring(pe, m.m_banks, m_sems, M_U, M_FIRST, B), B * NG)

        @block.scalar
        def _(act):
            act.sem_inc(s_sems[1], N_S)
            act.sem_inc(pv_done, 2)
            act.sem_inc(pv_copied, 1)

            def rows_in(sr, g):
                for hh in range(1, HG):
                    bank = sr.take().bitcast(BF16)
                    act.activation(q_stack[PARTS:ROWS, HG * g + hh, :], bank[PARTS:ROWS, 0:S], ACT.Copy)\
                        .then_inc(s_sems[1], 1)

            rows_in(Ring(act, m.s_banks, s_sems, S_U, 0), 0)
            with act.Fori(0, B) as b:
                sr = later_ring(act, m.s_banks, s_sems, S_U, S_FIRST, b)
                for g in range(NG):
                    for j in range(TT):
                        act.wait_ge(pv_done, b * PV_STEPS + (g * TT + j + 1))
                        for hh in range(HG):
                            bank = sr.take()
                            act.activation(probs[:, j % 2, hh, 0:S - P * j], bank[:, 0:S - P * j], ACT.Exp)\
                                .then_inc(s_sems[1], 1)
                    rows_in(sr, (g + 1) % NG)
                sr.end()

        @block.vector
        def _(dve):
            dve.memset(pv, 0.0).then_inc(dve_steps, 1)
            dve.memset(o_t[:], 1.0).then_inc(dve_steps, 1)
            dve.wait_ge(dve_steps, 2)
            dve.sem_inc(m_sems[1], N_M)

            def masked_max(mr, hh, tt):
                w = P * (tt + 1)
                mr.wait_released(max(mr.n - 1, 1 - N_M))
                bank = mr.take()
                apart(dve, waits_apart)
                dve.tensor_tensor_reduce(junk[:, mr.n % 2, 0:w], bank[:, 0:w], causal_q[:, S - w:S], 1.0,
                                         -FLT_MAX, ALU.add, ALU.max, mx[:, tt * HG + hh:tt * HG + hh + 1])\
                    .then_inc(m_sems[1], 1)

            def negate(v, mr):
                mr.wait_released(mr.n)
                v(dve.tensor_scalar(neg[:], mx[:], -1.0, None, ALU.mult))
                flat = neg_nat[:].rearrange("p t h c -> p (t h) c")
                for part in range(3):
                    ins = dve.tensor_copy(flat[:, :, part], neg[:])
                    if part < 2:
                        v(ins)
                        v(dve.tensor_tensor(neg[:], neg[:], flat[:, :, part], ALU.subtract))
                    else:
                        ins.then_inc(neg_ready, 1)

            def row_in(mr, g):
                bank = mr.take().bitcast(BF16)
                dve.tensor_copy(q_stack[PARTS:ROWS, HG * g, :], bank[PARTS:ROWS, 0:S]).then_inc(m_sems[1], 1)

            def natural(v, mr, slot):
                bank = mr.take().rearrange("p (t h c) -> p t h c", t=TT, h=HG)
                v(dve.reciprocal(rden[:], bank[:, :, :, DK]))
                dve.tensor_tensor(o_nat[:, slot], bank[:, :, :, 0:DK],
                                  rden[:].unsqueeze(3).to_broadcast([P, TT, HG, DK]), ALU.mult).then_inc(m_sems[1], 1)

            v, mr = Chain(dve, dve_steps, 5, 0), Ring(dve, m.m_banks, m_sems, M_U, 0)
            v.base = 2
            for work in [w for j in range(TT) for w in self_side_work(j) if w[0] == "max"]:
                masked_max(mr, *work[1:])
            negate(v, mr)
            row_in(mr, 0)
            v.end()
            with dve.Fori(0, B) as b:
                v, mr = Chain(dve, dve_steps, 6 * NG, b), later_ring(dve, m.m_banks, m_sems, M_U, M_FIRST, b)
                v.base = b * v.per + 7
                for g in range(NG):
                    for j in range(TT):
                        for work in self_side_work(j):
                            if work[0] == "max":
                                masked_max(mr, *work[1:])
                            elif work[0] == "natural":
                                dve.wait_ge(o_stored[g % 2], b * (16 * NG // 2) + 16 * (g // 2 + 1))
                                natural(v, mr, g % 2)
                            else:
                                negate(v, mr)
                                row_in(mr, (g + 1) % NG)
                    dve.wait_ge(pv_done, b * PV_STEPS + ((g + 1) * TT + 2))
                    dve.tensor_copy(o_t[:], pv).then_inc(pv_copied, 1)
                v.end(), mr.end()
            mr = later_ring(dve, m.m_banks, m_sems, M_U, M_FIRST, B)
            v = Chain(dve, dve_steps, 1, 0)
            v.base = B * 6 * NG + 7
            dve.wait_ge(o_stored[0], 16 * (B * NG // 2 + 1))
            natural(v, mr, 0)


def expert_phase(nc, sems, banks, consts, w_self, gate_t, ffn_w, scr, out):
    M_FRONT, S_FRONT = KT + TT + 1, KT
    M_U, S_U = M_FRONT + HT + 4 * TT, S_FRONT + 2 * HT + 3 * HT + KT + HT
    S_SILU = HT
    INPUTS = 16 * (2 + NG)
    with ExitStack() as ctx:
        m = Memory(nc, ctx, sems, "expert", banks)
        sb, sem = m.sb, m.sem
        ident_f, half, row_c = (consts[n] for n in ("identf", "half", "row_c"))
        n2w = row_c[:, 4 * D:5 * D]
        fw, wo, gate_w = sb("fw", [P, FFN_WORDS]), sb("wo", [P, KT, DOUT]), sb("gate_w", [P, KT, 4])
        o_nat, o_natT = sb("o_nat", [P, TT, D]), sb("o_natT", [P, KT, S])
        x1, x2 = sb("x1", [P, TT, D]), sb("x2", [P, TT, D])
        nat, natT = sb("nat", [P, TT, D]), sb("natT", [P, KT, S])
        acc, lg = sb("acc", [P, 2, TT, D]), sb("lg", [P, 2, TT, 4])
        hidden = sb("hidden", [P, 3, HT, S])
        h0, h1, h2 = (hidden[:, i] for i in range(3))
        junk, sums = sb("junk", [P, TT, D], BF16), sb("sums", [P, TT])
        rms_ms, rms_rs = sb("rms_ms", [P, TT]), sb("rms_rs", [P, TT])
        lt, rank, l1 = sb("lt", [P, TT, 4]), sb("rank", [P, TT, 4]), sb("l1", [P, TT])

        w_dma, in_dma = sem("w_dma"), sem("in_dma")
        expert_dma = [sem(f"expert{e}_dma") for e in range(4)]
        out_stored = [sem(f"out_stored{i}") for i in range(2)]
        s_sems, m_sems = (sem("s_full"), sem("s_free")), (sem("m_full"), sem("m_free"))
        rms_in, rms_out = sem("rms_in"), sem("rms_out")
        nat_ready = sem("nat_ready")
        gate_in, gate_exp = sem("gate_in"), sem("gate_exp")
        out_ready = sem("out_ready")
        dve_steps, waits_apart = sem("dve_steps"), sem("waits_apart")
        block = ctx.enter_context(nc.Block())

        @block.sync
        def _(sp):
            def load_inputs(b):
                for g in range(NG):
                    sp.dma_start(o_nat[:, :, g * HG * DK:(g + 1) * HG * DK],
                                 scr["os"][b * NG + (g + 1)].rearrange("p t h c -> p t (h c)")).then_inc(in_dma, 16)
                sp.dma_start(x2[:], scr["xn"][b]).then_inc(in_dma, 16)
                sp.dma_start(x1[:], scr["x1"][b]).then_inc(in_dma, 16)

            load_inputs(0)
            sp.dma_start(wo[:], w_self[:, :, 3 * D:3 * D + DOUT]).then_inc(w_dma, 16)
            sp.dma_start(gate_w[:], gate_t).then_inc(w_dma, 16)
            for e in range(4):
                sp.dma_start(fw[:, EXPERT_AT[e]:EXPERT_AT[e + 1]], ffn_w[:, EXPERT_AT[e]:EXPERT_AT[e + 1]])\
                    .then_inc(expert_dma[e], 16)
            for stored in out_stored:
                sp.sem_inc(stored, 16)
            with sp.Fori(0, B // 2) as pair:
                for u in range(2):
                    b = pair * 2 + u
                    sp.wait_ge(nat_ready, b + 1)
                    apart(sp, waits_apart)
                    load_inputs(next_batch(b))
                    sp.wait_ge(out_ready, b + 1)
                    sp.dma_start(out[b], acc[:, u]).then_inc(out_stored[u], 16)
            for stored in out_stored:
                sp.wait_ge(stored, 16 * (B // 2 + 1))
            sp.wait_ge(in_dma, INPUTS * (B + 1))

        @block.gpsimd
        def _(pool):
            def root(b):
                pool.wait_ge(rms_in, b + 1)
                pool.tensor_tensor(rms_rs[:], rms_ms[:], half[:, 0:TT], ALU.pow).then_inc(rms_out, 1)

            root(0)
            with pool.Fori(0, B) as b:
                root(b + 1)

        @block.tensor
        def _(pe):
            mm, tr = pe.matmul, pe.transpose
            pe.wait_ge(w_dma, 32)

            def transposed(ring, full, src):
                for kt in range(KT):
                    bank = ring.acquire()
                    for tt in range(TT):
                        last = tr(bank[:, tt * P:(tt + 1) * P], src[:, tt, kt * P:(kt + 1) * P], ident_f)
                    last.then_inc(full, 1)

            def attention_transposed(mr, b):
                pe.wait_ge(in_dma, INPUTS * b + INPUTS)
                transposed(mr, m_sems[0], o_nat)

            def project_out(mr):
                mr.wait_released(mr.n)
                for tt in range(TT):
                    bank = mr.acquire()
                    for kt in range(KT):
                        last = mm(bank[:, 0:DOUT], o_natT[:, kt, tt * P:(tt + 1) * P], wo[:, kt, :],
                                  start=kt == 0, stop=kt == KT - 1)
                    last.then_inc(m_sems[0], 1)

            def rows_transposed(sr, b):
                pe.wait_ge(nat_ready, b + 1)
                transposed(sr, s_sems[0], nat)

            def gates(mr):
                bank = mr.acquire()
                for tt in range(TT):
                    for kt in range(KT):
                        last = mm(bank[:, 4 * tt:4 * tt + 4], natT[:, kt, tt * P:(tt + 1) * P], gate_w[:, kt, :],
                                  start=kt == 0, stop=kt == KT - 1)
                last.then_inc(m_sems[0], 1)

            def layer(name, src, ring, full):
                at, kts, w = FFN_W[name]
                for t in range(w // P):
                    bank = ring.acquire()
                    for kt in range(kts):
                        last = mm(bank[:, :], fw[:, at + kt * w + t * P:at + kt * w + (t + 1) * P], src[:, kt, :],
                                  start=kt == 0, stop=kt == kts - 1)
                    last.then_inc(full, 1)

            def down(name, src, mr):
                at, kts, w = FFN_W[name]
                for tt in range(TT):
                    bank = mr.acquire()
                    for kt in range(kts):
                        last = mm(bank[:, 0:w], src[:, kt, tt * P:(tt + 1) * P], fw[:, at + kt * w:at + (kt + 1) * w],
                                  start=kt == 0, stop=kt == kts - 1)
                    last.then_inc(m_sems[0], 1)

            sr, mr = Ring(pe, m.s_banks, s_sems, S_U, 0), Ring(pe, m.m_banks, m_sems, M_U, 0)
            attention_transposed(mr, 0)
            project_out(mr)
            rows_transposed(sr, 0)
            sr.wait_released(sr.n)
            gates(mr)
            assert (sr.n, mr.n) == (S_FRONT, M_FRONT)
            with pe.Fori(0, B) as b:
                sr = later_ring(pe, m.s_banks, s_sems, S_U, S_FRONT, b)
                mr = later_ring(pe, m.m_banks, m_sems, M_U, M_FRONT, b)
                pe.wait_ge(expert_dma[0], 16)
                layer("e0_up", natT, sr, s_sems[0])
                pe.wait_ge(expert_dma[1], 16)
                layer("e1_w1", natT, sr, s_sems[0])
                layer("e1_w2", natT, mr, m_sems[0])
                h1_done = mr.n
                sr.wait_released(HT)
                down("e0_down", h0, mr)
                attention_transposed(mr, b + 1)
                pe.wait_ge(expert_dma[2], 16)
                layer("e2_l1", natT, sr, s_sems[0])
                h0_done = sr.n
                project_out(mr)
                mr.wait_released(h1_done)
                down("e1_down", h1, mr)
                sr.wait_released(h0_done)
                layer("e2_l2", h0, sr, s_sems[0])
                h1_done = sr.n
                pe.wait_ge(expert_dma[3], 16)
                layer("e3_down", natT, sr, s_sems[0])
                h2_done = sr.n
                sr.wait_released(h1_done)
                layer("e2_l3", h1, sr, s_sems[0])
                h0_done = sr.n
                rows_transposed(sr, b + 1)
                natT_done = sr.n
                sr.wait_released(h2_done)
                layer("e3_up", h2, sr, s_sems[0])
                sr.wait_released(h0_done)
                down("e2_l4", h0, mr)
                sr.wait_released(natT_done)
                gates(mr)
                sr.wait_released(sr.n)
                down("e3_out", h1, mr)
                sr.end(), mr.end()

        @block.scalar
        def _(act):
            act.sem_inc(s_sems[1], N_S)

            def empty(sr, dst, tiles, func):
                for t in range(tiles):
                    bank = sr.take()
                    act.activation(dst[:, t, :], bank[:, 0:S], func).then_inc(s_sems[1], 1)

            def exp_gates(slot, b):
                act.wait_ge(gate_in, b + 1)
                act.activation(lg[:, slot], lg[:, slot], ACT.Exp).then_inc(gate_exp, 1)

            empty(Ring(act, m.s_banks, s_sems, S_U, 0), natT, KT, ACT.Copy)
            exp_gates(0, 0)
            with act.Fori(0, B // 2) as pair:
                for u in range(2):
                    b = pair * 2 + u
                    sr = later_ring(act, m.s_banks, s_sems, S_U, S_FRONT, b)
                    empty(sr, h0, HT, ACT.Gelu)
                    empty(sr, h1, HT, ACT.Silu)
                    empty(sr, h0, HT, ACT.Gelu)
                    empty(sr, h1, HT, ACT.Gelu)
                    empty(sr, h2, KT, ACT.Gelu)
                    empty(sr, h0, HT, ACT.Gelu)
                    empty(sr, natT, KT, ACT.Copy)
                    empty(sr, h1, HT, ACT.Gelu)
                    exp_gates(1 - u, b + 1)
                    sr.end()

        @block.vector
        def _(dve):
            dve.sem_inc(m_sems[1], N_M)

            def attention_transposed(mr):
                for kt in range(KT):
                    bank = mr.take()
                    dve.tensor_copy(o_natT[:, kt, :], bank).then_inc(m_sems[1], 1)

            def rows_x2(v, mr, slot, b, stored):
                dve.wait_ge(in_dma, INPUTS * b + INPUTS)
                for tt in range(TT):
                    bank = mr.take()
                    dve.tensor_tensor(x2[:, tt, ZERO_COLS:D], bank[:, 0:DOUT], x2[:, tt, ZERO_COLS:D], ALU.add)\
                        .then_inc(m_sems[1], 1)
                mr.wait_released(mr.n)
                for tt in range(TT):
                    v.step(dve.tensor_tensor_reduce(junk[:, tt, :], x2[:, tt, :], x2[:, tt, :], 1.0, 0.0,
                                                    ALU.mult, ALU.add, sums[:, tt:tt + 1]))
                v.settle()
                dve.tensor_scalar(rms_ms[:], sums[:], 1.0 / D, RMS_EPS, ALU.mult, ALU.add).then_inc(rms_in, 1)
                dve.wait_ge(out_stored[slot], stored)
                for tt in range(TT):
                    v.step(dve.tensor_tensor(acc[:, slot, tt, :], x1[:, tt, :], x2[:, tt, :], ALU.add))
                v.settle()

            def rows_nat(v, b):
                dve.wait_ge(rms_out, b + 1)
                for tt in range(TT):
                    ins = dve.scalar_tensor_tensor(nat[:, tt, :], x2[:, tt, :], rms_rs[:, tt:tt + 1], n2w,
                                                   ALU.mult, ALU.mult)
                    ins.then_inc(nat_ready, 1) if tt == TT - 1 else v.step(ins)

            def logits(v, mr, slot):
                g = lg[:, slot]
                bank = mr.take()
                dve.tensor_scalar(g, bank[:, 0:4 * TT].rearrange("p (t e) -> p t e", e=4), FLT_MAX, -FLT_MAX,
                                  ALU.min, ALU.max).then_inc(m_sems[1], 1)
                mr.wait_released(mr.n)
                v(dve.tensor_reduce(l1[:], g, AX.X, ALU.max))
                dve.tensor_tensor(g, g, l1[:].unsqueeze(2).to_broadcast([P, TT, 4]), ALU.subtract).then_inc(gate_in, 1)

            def weights(v, slot, b):
                g = lg[:, slot]
                dve.wait_ge(gate_exp, b + 1)
                v(dve.tensor_reduce(l1[:], g, AX.X, ALU.add))
                v(dve.reciprocal(l1[:], l1[:]))
                v(dve.tensor_tensor(g, g, l1[:].unsqueeze(2).to_broadcast([P, TT, 4]), ALU.mult))
                v(dve.memset(rank[:], 0.0))
                for e in range(4):
                    if e > 0:
                        v.step(dve.tensor_tensor(lt[:, :, 0:e], g[:, :, e:e + 1].to_broadcast([P, TT, e]),
                                                 g[:, :, 0:e], ALU.is_gt))
                    if e < 3:
                        v.step(dve.tensor_tensor(lt[:, :, e + 1:4], g[:, :, e:e + 1].to_broadcast([P, TT, 3 - e]),
                                                 g[:, :, e + 1:4], ALU.is_ge))
                    v.settle()
                    if e > 0:
                        v.step(dve.tensor_tensor(rank[:, :, 0:e], rank[:, :, 0:e], lt[:, :, 0:e], ALU.add))
                    if e < 3:
                        v.step(dve.tensor_tensor(rank[:, :, e + 1:4], rank[:, :, e + 1:4], lt[:, :, e + 1:4], ALU.add))
                    v.settle()
                v(dve.tensor_scalar(rank[:], rank[:], 2.0, None, ALU.is_lt))
                v(dve.tensor_tensor(g, g, rank[:], ALU.mult))
                v(dve.tensor_reduce(l1[:], g, AX.X, ALU.add))
                v(dve.tensor_scalar(l1[:], l1[:], 1e-8, None, ALU.add))
                v(dve.reciprocal(l1[:], l1[:]))
                v(dve.tensor_tensor(g, g, l1[:].unsqueeze(2).to_broadcast([P, TT, 4]), ALU.mult))

            def down(mr, slot, e):
                for tt in range(TT):
                    bank = mr.take()
                    mr.wait_released(mr.n - TT)
                    dve.scalar_tensor_tensor(acc[:, slot, tt, ZERO_COLS:D], bank[:, 0:DOUT], lg[:, slot, tt, e:e + 1],
                                             acc[:, slot, tt, ZERO_COLS:D], ALU.mult, ALU.add).then_inc(m_sems[1], 1)

            v, mr = Chain(dve, dve_steps, 34, 0), Ring(dve, m.m_banks, m_sems, M_U, 0)
            attention_transposed(mr)
            rows_x2(v, mr, 0, 0, 16)
            rows_nat(v, 0)
            logits(v, mr, 0)
            weights(v, 0, 0)
            v.end()
            with dve.Fori(0, B // 2) as pair:
                for u in range(2):
                    b = pair * 2 + u
                    v, mr = Chain(dve, dve_steps, 34, b + 1), later_ring(dve, m.m_banks, m_sems, M_U, M_FRONT, b)
                    for t in range(HT):
                        bank = mr.take()
                        dve.wait_ge(s_sems[1], b * S_U + (S_FRONT + S_SILU + t + 1 + N_S))
                        dve.tensor_tensor(h1[:, t, :], bank, h1[:, t, :], ALU.mult).then_inc(m_sems[1], 1)
                    down(mr, u, 0)
                    attention_transposed(mr)
                    rows_x2(v, mr, 1 - u, b + 1, pair * 16 + (16 + 16 * u))
                    rows_nat(v, b + 1)
                    down(mr, u, 1)
                    down(mr, u, 2)
                    logits(v, mr, 1 - u)
                    down(mr, u, 3)
                    mr.wait_released(mr.n)
                    dve.sem_inc(out_ready, 1)
                    weights(v, 1 - u, b + 1)
                    v.end(), mr.end()


def xattn_ffn_kernel(nc, x, ctx_t, mask, w_cross, w_self, rows, bias_k, gate_t, ffn_w, ones, out):
    def scratch(name, shape, dt=F32):
        return nc.dram_tensor(f"scratch_{name}", shape, dt).ap()

    scr = {
        "k": scratch("k", (3, B, D, KEYS), BF16), "q": scratch("q", (B, PARTS, NG, HG * S), BF16),
        "v": scratch("v", (B, P, NG, NKT * HG * VW)),
        "mask": scratch("mask", (B, P, TT, KEYS), BF16), "flag": scratch("flag", (1, B), I32),
        "o": scratch("o", (B * NG + 1, P, TT, HG, DK)),
        "x1": scratch("x1", (B + 1, P, TT, D)), "xn": scratch("xn", (B + 1, P, TT, D)),
        "qs": scratch("qs", (B, PARTS, NG, HG * S), BF16), "ks": scratch("ks", (B, PARTS, NG, HG * S), BF16),
        "vs": scratch("vs", (B + 1, P, NG, TT * HG * VW)),
        "os": scratch("os", (B * NG + 1, P, TT, HG, DK)),
    }
    with ExitStack() as ctx:
        banks = [ctx.enter_context(nc.psum_tensor(f"bank{i}", [P, 512], F32))[:] for i in range(8)]

        def sb(name, shape, dt=F32):
            return ctx.enter_context(nc.sbuf_tensor(name, shape, dt))[:]

        consts = {
            "row_c": sb("row_c", [P, 7 * D]), "bk": sb("bk", [P, KT]),
            "identf": sb("identf", [P, P]), "identb": sb("identb", [P, P], BF16),
            "causal_q": sb("causal_q", [P, S], BF16),
            "causal_k": sb("causal_k", [P, P], BF16),
            "half": sb("half", [P, 2 * TT * H]),
        }
        setup_phase(nc, ctx, consts, rows, bias_k)
        prepare_phase(nc, ctx, banks, consts, x, ctx_t, mask, w_cross, scr)
        cross_phase(nc, ctx, banks, consts, scr, ones)
        self_inputs_phase(nc, ctx, banks, consts, x, w_cross, w_self, scr)
        self_phase(nc, ctx, banks, consts, scr, ones)
        expert_phase(nc, ctx, banks, consts, w_self, gate_t, ffn_w, scr, out)


def _tiles(w):
    k = w.shape[0] // P
    return w.reshape(k, P, w.shape[1]).transpose(1, 0, 2)


def kernel(**inputs):
    import numpy as np
    import concourse.bacc as bacc
    from concourse.bass_utils import run_bass_kernel_spmd

    a = {n: np.asarray(v) for n, v in inputs.items()}
    X, F = "L0_xattn_", "L0_ffn_"
    w_cross = np.stack([_tiles(a[X + n].T) for n in ("W_q", "W_k", "W_v", "W_o")], axis=1)
    w_self = np.concatenate([_tiles(a[F + n].T) for n in ("wq", "wk", "wv")]
                            + [_tiles(a[F + "wo"].T[:, ZERO_COLS:])], axis=2)
    rows = np.concatenate([a[X + "b_q"], a[X + "b_v"], a[X + "b_o"], a[F + "n1_w"], a[F + "n2_w"],
                           np.tile(a[F + "qn_w"], H), np.tile(a[F + "kn_w"], H)])
    cut = {"e0_down", "e1_down", "e2_l4", "e3_out"}
    ffn_w = np.concatenate([_tiles(a[F + n].T[:, ZERO_COLS:] if n in cut else a[F + n].T).reshape(P, -1)
                            for n in FFN_W], axis=1)
    arrays = {
        "x": a["x"],
        "ctx_t": a["ctx_1024"].transpose(0, 2, 1),
        "mask": a["mask_Bx1xSxS2_bf1"].reshape(B, S, KEYS).view(np.uint8),
        "w_cross": w_cross,
        "w_self": w_self,
        "rows": np.broadcast_to(rows, (P, rows.size)),
        "bias_k": a[X + "b_k"].reshape(KT, P).T,
        "gate_t": _tiles(a[F + "gate_w"].T),
        "ffn_w": ffn_w,
        "ones": np.ones((3, H * KEYS), dtype=mybir.dt.np(BF16)),
    }
    arrays = {n: np.ascontiguousarray(v) for n, v in arrays.items()}
    nc = bacc.Bacc("TRN2", target_bir_lowering=False, num_devices=1)
    t = {n: nc.dram_tensor(n, v.shape, mybir.dt.from_np(v.dtype), kind="ExternalInput").ap()
         for n, v in arrays.items()}
    out = nc.dram_tensor("out", (B, S, D), F32, kind="ExternalOutput").ap()
    xattn_ffn_kernel(
        nc, t["x"].rearrange("b (t p) d -> b p t d", p=P), t["ctx_t"].rearrange("b (k p) n -> b p k n", p=P),
        t["mask"].rearrange("b (t p) n -> b p t n", p=P), t["w_cross"], t["w_self"], t["rows"], t["bias_k"],
        t["gate_t"], t["ffn_w"], t["ones"].rearrange("r (h n) -> r h n", h=H), out.rearrange("b (t p) d -> b p t d", p=P))
    r = run_bass_kernel_spmd(nc, [arrays], core_ids=[0])
    return r.results[0]["out"]
```

```python
from contextlib import ExitStack

import concourse.bass as bass
from concourse import mybir

F32 = mybir.dt.float32
F32R = mybir.dt.float32r
BF16 = mybir.dt.bfloat16
I32 = mybir.dt.int32
ALU = mybir.AluOpType
ACT = mybir.ActivationFunctionType
AX = mybir.AxisListType

P = 128
B, S, D = 8, 512, 256
KEYS = 1601
H, DK = 16, 16
HG = 4
NG = H // HG
TT = S // P
KT = D // P
NKT = -(-KEYS // P)
HID = 512
HT = HID // P
ZERO_COLS = 64
DOUT = D - ZERO_COLS
PARTS = 96
ROWS = PARTS + 3
VW = DK + 1
BIG = float(2 ** 30)
LN_EPS = 1e-5
RMS_EPS = 1.1920929e-07
FLT_MAX = 3.4028234e38
CHUNKS = []
for _c in range(4):
    _lo = sum(w for _, w in CHUNKS)
    CHUNKS.append((_lo, -(-(KEYS - _lo) // (4 - _c))))
NCH = len(CHUNKS)

Q_BLOCKS = ((0, 2, 4), (1, 5), (3,))
K_BLOCKS = ((0, 1, 3), (2, 5), (4,))

FFN_W = {}
_at = 0
for _name, _kt, _w in (("e0_up", KT, HID), ("e0_down", HT, DOUT),
                       ("e1_w1", KT, HID), ("e1_w2", KT, HID), ("e1_down", HT, DOUT),
                       ("e2_l1", KT, HID), ("e2_l2", HT, HID), ("e2_l3", HT, HID), ("e2_l4", HT, DOUT),
                       ("e3_down", KT, D), ("e3_up", KT, HID), ("e3_out", HT, DOUT)):
    FFN_W[_name] = (_at, _kt, _w)
    _at += _kt * _w


N_M, N_S = 3, 4


def apart(eng, sem):
    eng.sem_inc(sem, 1)


class Ring:

    def __init__(self, eng, banks, sems, uses, b):
        assert uses % len(banks) == 0
        self.eng, self.banks, (self.full, self.free) = eng, banks, sems
        self.base, self.uses, self.n, self.before = b * uses, uses, 0, 0

    def acquire(self):
        self.eng.wait_ge(self.free, self.base + (self.n + 1))
        self.n += 1
        return self.banks[(self.n - 1) % len(self.banks)]

    def take(self):
        self.eng.wait_ge(self.full, self.base + (self.n + 1))
        self.n += 1
        return self.banks[(self.n - 1) % len(self.banks)]

    def wait_released(self, n):
        self.eng.wait_ge(self.free, self.base + (n + len(self.banks)))

    def end(self):
        assert self.n == self.uses, (self.n, self.uses)


def later_ring(eng, banks, sems, uses, first, b):
    turn = first % len(banks)
    ring = Ring(eng, banks[turn:] + banks[:turn], sems, uses, b)
    ring.base, ring.before = b * uses + first, first
    return ring


class Chain:

    def __init__(self, eng, sem, per_batch, b):
        self.eng, self.sem, self.per, self.base, self.n = eng, sem, per_batch, b * per_batch, 0

    def step(self, ins):
        self.n += 1
        ins.then_inc(self.sem, 1)

    def settle(self):
        self.eng.wait_ge(self.sem, self.base + self.n)

    def __call__(self, ins):
        self.step(ins)
        self.settle()

    def end(self):
        assert self.n == self.per, (self.n, self.per)


class Memory:

    def __init__(self, nc, ctx, sems, phase, banks):
        self.nc, self.ctx, self.sems, self.phase = nc, ctx, sems, phase
        self.s_banks, self.m_banks, self.pv = banks[0:N_S], banks[N_S:N_S + N_M], banks[7]

    def sb(self, name, shape, dt=F32):
        return self.ctx.enter_context(self.nc.sbuf_tensor(f"{self.phase}_{name}", shape, dt))

    def sem(self, name):
        return self.sems.enter_context(self.nc.semaphore(f"{self.phase}_{name}"))


def heads(ap):
    return ap.rearrange("p t (h c) -> p t h c", c=DK)


def next_batch(b):
    return (b + 1) % B



def setup_phase(nc, sems, consts, rows, bias_k):
    c = consts
    with ExitStack() as ctx:
        rows_dma, pool_setup, dve_setup = (sems.enter_context(nc.semaphore(n))
                                           for n in ("rows_dma", "pool_setup", "dve_setup"))
        block = ctx.enter_context(nc.Block())

        @block.sync
        def _(sp):
            sp.dma_start(c["row_c"], rows).then_inc(rows_dma, 16)
            sp.dma_start(c["bk"], bias_k).then_inc(rows_dma, 16)
            sp.wait_ge(rows_dma, 32)

        @block.gpsimd
        def _(pool):
            done = [0]

            def once(ins):
                done[0] += 1
                ins.then_inc(pool_setup, 1)
                pool.wait_ge(pool_setup, done[0])

            identf, causal_q, causal_k = c["identf"], c["causal_q"], c["causal_k"]
            once(pool.memset(identf, 0.0))
            once(pool.affine_select(out=identf, in_=identf, compare_op=ALU.not_equal, fill=1.0,
                                    base=0, pattern=[[-1, P]], channel_multiplier=1))
            once(pool.tensor_copy(c["identb"], identf))
            once(pool.memset(causal_q, 0.0))
            once(pool.affine_select(out=causal_q[:, S - P:S], in_=causal_q[:, S - P:S], compare_op=ALU.is_ge,
                                    fill=-BIG, base=0, pattern=[[-1, P]], channel_multiplier=1))
            once(pool.memset(causal_k, 0.0))
            once(pool.affine_select(out=causal_k, in_=causal_k, compare_op=ALU.is_ge,
                                    fill=-BIG, base=0, pattern=[[1, P]], channel_multiplier=-1))
            once(pool.memset(c["half"], -0.5))

        @block.vector
        def _(dve):
            qn = c["row_c"][:, 5 * D:6 * D]
            dve.wait_ge(rows_dma, 32)
            dve.tensor_scalar(qn, qn, DK ** -0.5, None, ALU.mult).then_inc(dve_setup, 1)
            dve.wait_ge(dve_setup, 1)


def cast_part(act, part_of, rest, blocks, part, sems, b):
    cast, left, copied = sems
    if part:
        act.wait_ge(left, b * 2 + part)
    act.activation(part_of(blocks[part][0]), rest, ACT.Copy).then_inc(cast, 1)
    if len(blocks[part]) > 1:
        act.wait_ge(cast, b * 3 + (part + 1))
    for i in blocks[part][1:]:
        act.activation(part_of(i), part_of(blocks[part][0]), ACT.Copy).then_inc(copied, 1)


def subtract_part(eng, part_of, rest, blocks, part, sems, waits_apart, b):
    cast, left, _ = sems
    eng.wait_ge(cast, b * 3 + (part + 1))
    apart(eng, waits_apart)
    eng.tensor_tensor(rest, rest, part_of(blocks[part][0]), ALU.subtract).then_inc(left, 1)


def subtract_parts(eng, part_of, rest, blocks, sems, waits_apart, b):
    for part in range(2):
        subtract_part(eng, part_of, rest, blocks, part, sems, waits_apart, b)


def wait_split(pe, sems, b):
    cast, _, copied = sems
    pe.wait_ge(cast, b * 3 + 3)
    pe.wait_ge(copied, b * 3 + 3)


def prepare_phase(nc, sems, banks, consts, x, ctx_t, mask, w_cross, scr):
    ROW_BANKS = ((0, 0, TT), (1, 0, TT // 2), (1, TT // 2, TT // 2))
    M_FIRST = len(ROW_BANKS) + TT
    M_U, S_U = M_FIRST + NKT + 4, KT * NCH + 4
    K_STORE, CASTS = 16 * 3, 3 * KT
    K_ORDER = ((0, 0), (0, 1), (1, 0), (0, 2), (1, 1), (1, 2))
    with ExitStack() as ctx:
        m = Memory(nc, ctx, sems, "prep", banks)
        sb, sem = m.sb, m.sem
        ident_f, ident_b, half, row_c, bk = (consts[n] for n in ("identf", "identb", "half", "row_c", "bk"))
        bq, bv = row_c[:, 0:D], row_c[:, D:2 * D]
        w = sb("w", [P, 3, KT, D])
        wq, wk, wv = (w[:, i] for i in range(3))
        big_c = sb("big_c", [P, 1])
        x_in, nat, natT = sb("x_in", [P, TT, D]), sb("nat", [P, TT, D]), sb("natT", [P, KT, S])
        q = sb("q", [P, TT, D])
        q_nat = sb("q_nat", [P, TT, H, PARTS], BF16)
        q_stack = sb("q_stack", [PARTS, H, S], BF16)
        ctx_sb = sb("ctx_sb", [P, 2, KT, KEYS])
        kf = sb("kf", [P, KT, KEYS])
        k_part = sb("k_part", [P, KT, 3, KEYS + KEYS % 2], BF16)
        v_aug = sb("v_aug", [P, NG, NKT, HG * VW])
        mask_b = sb("mask_b", [P, TT, KEYS], BF16)
        mask_sum, row_live, mask_any = sb("mask_sum", [P, TT]), sb("row_live", [P, TT]), sb("mask_any", [P, 3])
        masked_i = sb("masked_i", [1, 1], I32)
        stats, mv, ms, rs = sb("stats", [P, TT, 6]), sb("mv", [P, TT, 2]), sb("ms", [P, TT]), sb("rs", [P, TT])

        w_dma, x_dma, mask_dma = sem("w_dma"), sem("x_dma"), sem("mask_dma")
        ctx_dma = [sem(f"ctx{i}_dma") for i in range(2)]
        k_stored = [sem(f"k{t}_stored") for t in range(KT)]
        v_stored, q_stored = sem("v_stored"), sem("q_stored")
        mask_stored, flag_stored = sem("mask_stored"), sem("flag_stored")
        setup = sem("setup")
        s_sems, m_sems = (sem("s_full"), sem("s_free")), (sem("m_full"), sem("m_free"))
        ln_done = sem("ln_done")
        ms_ready, rs_ready = sem("ms_ready"), sem("rs_ready")
        mask_bias = sem("mask_bias")
        live_ready, flag_ready = sem("live_ready"), sem("flag_ready")
        q_ready = sem("q_ready")
        q_split = (sem("q_cast"), sem("q_left"), sem("q_copied"))
        kcast, ksub = sem("kcast"), sem("ksub")
        dve_steps, pool_steps, waits_apart = sem("dve_steps"), sem("pool_steps"), sem("waits_apart")

        def q_part(i):
            return q_nat[:, :, :, i * DK:(i + 1) * DK]

        block = ctx.enter_context(nc.Block())

        @block.sync
        def _(sp):
            sp.dma_start(x_in[:], x[0]).then_inc(x_dma, 16)
            sp.dma_start(w[:], w_cross[:, 0:3]).then_inc(w_dma, 16)
            sp.dma_start(ctx_sb[:, 0], ctx_t[0]).then_inc(ctx_dma[0], 16)
            for stored, n in ((k_stored[0], K_STORE), (k_stored[1], K_STORE), (v_stored, 16), (q_stored, 16), (mask_stored, 16), (flag_stored, 16)):
                sp.sem_inc(stored, n)
            sp.wait_ge(ln_done, 1)
            sp.dma_start(x_in[:], x[1]).then_inc(x_dma, 16)
            with sp.Fori(0, B // 2) as pair:
                for u in range(2):
                    b = pair * 2 + u
                    sp.wait_ge(m_sems[1], b * M_U + (M_FIRST + NKT + 2 - M_U + N_M))
                    apart(sp, waits_apart)
                    sp.dma_start(ctx_sb[:, 1 - u], ctx_t[next_batch(b)]).then_inc(ctx_dma[1 - u], 16)
                    sp.wait_ge(mask_bias, b * TT + TT)
                    sp.dma_start(scr["mask"][b], mask_b[:]).then_inc(mask_stored, 16)
                    sp.wait_ge(flag_ready, b + 1)
                    sp.dma_start(scr["flag"][0:1, bass.ds(b, 1)], masked_i[:]).then_inc(flag_stored, 16)
                    for n, (t, part) in enumerate(K_ORDER):
                        sp.wait_ge(kcast, b * CASTS + (n + 1 + CASTS))
                        apart(sp, waits_apart)
                        sp.dma_start(scr["k"][part, b, t * P:(t + 1) * P, :], k_part[:, t, part, 0:KEYS])\
                            .then_inc(k_stored[t], 16)
                        if n == 1:
                            sp.wait_ge(m_sems[1], b * M_U + (M_FIRST + NKT + N_M))
                            apart(sp, waits_apart)
                            sp.dma_start(scr["v"][b], v_aug[:].rearrange("p g j c -> p g (j c)")).then_inc(v_stored, 16)
                        if n == 3:
                            sp.wait_ge(m_sems[1], b * M_U + (M_FIRST + NKT + 4 + N_M))
                            apart(sp, waits_apart)
                            sp.wait_ge(s_sems[1], b * S_U + (S_U + N_S))
                            sp.dma_start(scr["q"][b], q_stack[:].rearrange("p (g h) n -> p g (h n)", g=NG))\
                                .then_inc(q_stored, 16)
                        if n == 2:
                            sp.wait_ge(ln_done, b + 2)
                            apart(sp, waits_apart)
                            sp.dma_start(x_in[:], x[next_batch(b + 1)]).then_inc(x_dma, 16)
            for stored in k_stored:
                sp.wait_ge(stored, K_STORE * (B + 1))
            for stored in (v_stored, q_stored, mask_stored, flag_stored):
                sp.wait_ge(stored, 16 * (B + 1))

        @block.gpsimd
        def _(pool):
            pool.memset(big_c[:], -BIG).then_inc(setup, 1)
            pool.memset(v_aug[:], 1.0).then_inc(setup, 1)
            pool.dma_start(mask_b[:], mask[0]).then_inc(mask_dma, 16)
            pool.wait_ge(ms_ready, 1)
            pool.tensor_tensor(rs[:], ms[:], half[:, 0:TT], ALU.pow).then_inc(rs_ready, 1)
            with pool.Fori(0, B) as b:
                chain = Chain(pool, pool_steps, 2, b)
                pool.wait_ge(live_ready, b + 1)
                pool.wait_ge(flag_stored, 16 * b + 16)
                apart(pool, waits_apart)
                chain(pool.partition_all_reduce(mask_any[:, 1:2], mask_any[:, 0:1], P, bass.bass_isa.ReduceOp.max))
                apart(pool, waits_apart)
                chain(pool.tensor_scalar(mask_any[:, 2:3], mask_any[:, 1:2], 1.0 / BIG, 1.0, ALU.mult, ALU.min))
                apart(pool, waits_apart)
                pool.tensor_copy(masked_i[:], mask_any[0:1, 2:3]).then_inc(flag_ready, 1)
                subtract_parts(pool, q_part, heads(q[:]), Q_BLOCKS, q_split, waits_apart, b)
                pool.wait_ge(mask_stored, 16 * b + 32)
                apart(pool, waits_apart)
                pool.dma_start(mask_b[:], mask[next_batch(b)]).then_inc(mask_dma, 16)
                pool.wait_ge(ms_ready, b + 2)
                pool.tensor_tensor(rs[:], ms[:], half[:, 0:TT], ALU.pow).then_inc(rs_ready, 1)
                chain.end()

        @block.tensor
        def _(pe):
            mm, tr = pe.matmul, pe.transpose
            pe.wait_ge(w_dma, 16)

            def rows_transposed(mr, b):
                pe.wait_ge(ln_done, b + 1)
                for kt, first, n in ROW_BANKS:
                    bank = mr.acquire()
                    for i in range(n):
                        last = tr(bank[:, i * P:(i + 1) * P], nat[:, first + i, kt * P:(kt + 1) * P], ident_f[:])
                    last.then_inc(m_sems[0], 1)

            def project_q(mr):
                mr.wait_released(mr.n)
                for tt in range(TT):
                    bank = mr.acquire()
                    for kt in range(KT):
                        last = mm(bank[:, 0:D], natT[:, kt, tt * P:(tt + 1) * P], wq[:, kt, :],
                                  start=kt == 0, stop=kt == KT - 1)
                    last.then_inc(m_sems[0], 1)

            mr = Ring(pe, m.m_banks, m_sems, M_U, 0)
            rows_transposed(mr, 0)
            project_q(mr)
            with pe.Fori(0, B // 2) as pair:
                for u in range(2):
                    b = pair * 2 + u
                    sr = Ring(pe, m.s_banks, s_sems, S_U, b)
                    mr = later_ring(pe, m.m_banks, m_sems, M_U, M_FIRST, b)
                    pe.wait_ge(ctx_dma[u], 16 * pair + 16)
                    for t in range(KT):
                        for lo, n in CHUNKS:
                            bank = sr.acquire()
                            for kt in range(KT):
                                last = mm(bank[:, 0:n], wk[:, kt, t * P:(t + 1) * P], ctx_sb[:, u, kt, lo:lo + n],
                                          start=kt == 0, stop=kt == KT - 1)
                            last.then_inc(s_sems[0], 1)
                    for j in range(NKT):
                        r = min(P, KEYS - P * j)
                        bank = mr.acquire()
                        for kt in range(KT):
                            last = mm(bank[0:r, 0:D], ctx_sb[:, u, kt, j * P:j * P + r], wv[:, kt, :],
                                      start=kt == 0, stop=kt == KT - 1)
                        last.then_inc(m_sems[0], 1)
                    wait_split(pe, q_split, b)
                    for n in range(H // 2):
                        ring, full = ((mr, m_sems[0]), (sr, s_sems[0]))[n % 2]
                        bank = ring.acquire().bitcast(BF16)
                        for i in range(2):
                            for tt in range(TT):
                                at = i * S + tt * P
                                last = tr(bank[0:PARTS, at:at + P], q_nat[:, tt, 2 * n + i, :], ident_b[:])
                        last.then_inc(full, 1)
                    rows_transposed(mr, b + 1)
                    project_q(mr)
                    mr.end(), sr.end()

        @block.scalar
        def _(act):
            act.sem_inc(s_sems[1], N_S)
            act.wait_ge(setup, 2)

            def bias_mask(b, tiles=range(TT)):
                act.wait_ge(mask_dma, 16 * b + 16)
                for tt in tiles:
                    act.activation(mask_b[:, tt, :], mask_b[:, tt, :], ACT.Identity, bias=big_c[:], scale=BIG,
                                   accum_out=mask_sum[:, tt:tt + 1]).then_inc(mask_bias, 1)

            act.sem_inc(kcast, CASTS)
            bias_mask(0)
            with act.Fori(0, B) as b:
                sr = Ring(act, m.s_banks, s_sems, S_U, b)

                def keys(t):
                    act.wait_ge(kcast, b * CASTS + (K_ORDER.index((t, 2)) + 1))
                    for lo, n in CHUNKS:
                        bank = sr.take()
                        act.activation(kf[:, t, lo:lo + n], bank[:, 0:n], ACT.Identity, bias=bk[:, t:t + 1])\
                            .then_inc(s_sems[1], 1)

                def key_part(t, part):
                    if part == 0:
                        act.wait_ge(s_sems[1], b * S_U + (NCH * (t + 1) + N_S))
                        act.wait_ge(k_stored[t], b * K_STORE + K_STORE)
                    else:
                        act.wait_ge(ksub, b * (2 * KT) + (2 * t + part))
                    act.activation(k_part[:, t, part, 0:KEYS], kf[:, t, :], ACT.Copy).then_inc(kcast, 1)

                keys(0)
                act.wait_ge(q_ready, b + 1)
                cast_part(act, q_part, heads(q[:]), Q_BLOCKS, 0, q_split, b)
                key_part(0, 0)
                cast_part(act, q_part, heads(q[:]), Q_BLOCKS, 1, q_split, b)
                keys(1)
                cast_part(act, q_part, heads(q[:]), Q_BLOCKS, 2, q_split, b)
                key_part(0, 1)
                key_part(1, 0)
                act.wait_ge(q_stored, 16 * b + 16)
                for n in range(1, H // 2, 2):
                    bank = sr.take().bitcast(BF16)
                    act.activation(q_stack[:, 2 * n:2 * n + 2, :],
                                   bank[0:PARTS, :].rearrange("p (h n) -> p h n", h=2), ACT.Copy).then_inc(s_sems[1], 1)
                key_part(0, 2)
                act.wait_ge(live_ready, b + 1)
                bias_mask(b + 1, range(TT // 2))
                key_part(1, 1)
                bias_mask(b + 1, range(TT // 2, TT))
                key_part(1, 2)
                sr.end()

        @block.vector
        def _(dve):
            dve.wait_ge(setup, 2)
            dve.sem_inc(m_sems[1], N_M)

            def moments(v, b):
                dve.wait_ge(x_dma, 16 * b + 16)
                for tt in range(TT):
                    v.step(dve.bn_stats(stats[:, tt, :], x_in[:, tt, :]))
                v.settle()
                apart(dve, waits_apart)
                for tt in range(TT):
                    v.step(dve.bn_aggr(mv[:, tt, :], stats[:, tt, :]))
                v.settle()
                dve.tensor_scalar(ms[:], mv[:, :, 1], LN_EPS, None, ALU.add).then_inc(ms_ready, 1)

            def normalise(v, b):
                dve.wait_ge(rs_ready, b + 1)
                for tt in range(TT):
                    ins = dve.tensor_scalar(nat[:, tt, :], x_in[:, tt, :], mv[:, tt, 0:1], rs[:, tt:tt + 1],
                                            ALU.subtract, ALU.mult)
                    if tt == TT - 1:
                        ins.then_inc(ln_done, 1)
                    else:
                        v.step(ins)

            def live(v, b):
                dve.wait_ge(mask_bias, b * TT + TT)
                v(dve.tensor_scalar(row_live[:], mask_sum[:], -KEYS * BIG, None, ALU.is_gt))
                dve.tensor_reduce(mask_any[:, 0:1], mask_sum[:], AX.X, ALU.min, negate=True).then_inc(live_ready, 1)

            def queries(mr):
                for kt, first, n in ROW_BANKS:
                    bank = mr.take()
                    dve.tensor_copy(natT[:, kt, first * P:(first + n) * P], bank[:, 0:n * P]).then_inc(m_sems[1], 1)
                for tt in range(TT):
                    bank = mr.take()
                    dve.tensor_tensor(q[:, tt, :], bank[:, 0:D], bq, ALU.add).then_inc(m_sems[1], 1)

            def scale(v, mr):
                mr.wait_released(mr.n)
                for tt in range(TT):
                    ins = dve.tensor_scalar(q[:, tt, :], q[:, tt, :], row_live[:, tt:tt + 1], DK ** -0.5,
                                            ALU.mult, ALU.mult)
                    ins.then_inc(q_ready, 1) if tt == TT - 1 else v.step(ins)

            first = Chain(dve, dve_steps, 15, 0)
            moments(first, 0)
            normalise(first, 0)
            live(first, 0)
            mr = Ring(dve, m.m_banks, m_sems, M_U, 0)
            queries(mr)
            scale(first, mr)
            first.end()
            with dve.Fori(0, B) as b:
                v = Chain(dve, dve_steps, 15, b)
                v.base = b * 15 + 15
                mr = later_ring(dve, m.m_banks, m_sems, M_U, M_FIRST, b)
                moments(v, b + 1)

                def remainder(t, part):
                    dve.wait_ge(kcast, b * CASTS + (K_ORDER.index((t, part)) + 1 + CASTS))
                    dve.tensor_tensor(kf[:, t, :], kf[:, t, :], k_part[:, t, part, 0:KEYS], ALU.subtract)\
                        .then_inc(ksub, 1)

                dve.wait_ge(v_stored, 16 * b + 16)
                for j in range(NKT):
                    r = min(P, KEYS - P * j)
                    bank = mr.take()
                    dve.tensor_tensor(v_aug[0:r, :, j, :].rearrange("p g (h c) -> p g h c", h=HG)[:, :, :, 0:DK],
                                      bank[0:r, 0:D].rearrange("p (g h c) -> p g h c", g=NG, h=HG),
                                      bv[0:r].rearrange("p (g h c) -> p g h c", g=NG, h=HG), ALU.add)\
                        .then_inc(m_sems[1], 1)
                remainder(0, 0)
                remainder(0, 1)
                normalise(v, b + 1)
                dve.wait_ge(q_stored, 16 * b + 16)
                for n in range(0, H // 2, 2):
                    bank = mr.take().bitcast(BF16)
                    dve.tensor_copy(q_stack[:, 2 * n:2 * n + 2, :],
                                    bank[0:PARTS, :].rearrange("p (h n) -> p h n", h=2)).then_inc(m_sems[1], 1)
                remainder(1, 0)
                queries(mr)
                remainder(1, 1)
                dve.wait_ge(q_ready, b + 1)
                dve.wait_ge(flag_ready, b + 1)
                live(v, b + 1)
                scale(v, mr)
                v.end(), mr.end()


PER_STEP = 5
MAXIMA = [("max", hh, tt, c) for tt in range(TT) for hh in range(HG) for c in range(NCH)]
AHEAD = 2 * PER_STEP
NATURAL_AT = 4 * PER_STEP + 3


def cross_side_work(j):
    last = NKT - 3
    if j > last:
        return MAXIMA[PER_STEP * (j - last - 1):PER_STEP * (j - last)]
    work = MAXIMA[AHEAD + PER_STEP * j:AHEAD + PER_STEP * (j + 1)]
    if j == 4:
        work.insert(2, ("natural",))
    return work


def cross_phase(nc, sems, banks, consts, scr, ones):
    G_M, G_S = HG * TT * NCH + 2, NKT * HG + HG - 1
    M_U, S_U = NG * G_M, NG * G_S
    PV_STEPS = NG * NKT
    M_FIRST, S_FIRST = HG * TT * NCH + 1 + AHEAD, HG - 1
    with ExitStack() as ctx:
        m = Memory(nc, ctx, sems, "cross", banks)
        sb, sem, pv = m.sb, m.sem, m.pv
        ident_f, ident_b = consts["identf"], consts["identb"]
        k_stack = sb("k_stack", [ROWS, H, KEYS], BF16)
        q_stack = sb("q_stack", [ROWS, H, S], BF16)
        v_aug = sb("v_aug", [P, NG, NKT, HG, VW])
        mask_max = sb("mask_max", [P, TT, KEYS], BF16)
        mask_exp = sb("mask_exp", [P, TT, KEYS], BF16)
        flags = sb("flags", [1, B], I32)
        probs = sb("probs", [P, 2, HG, S])
        o_t, o_nat = sb("o_t", [P, S]), sb("o_nat", [P, 2, TT, HG, DK])
        junk = sb("junk", [P, 2, S], BF16)
        mx, neg = sb("mx", [P, TT * HG, NCH]), sb("neg", [P, TT * HG])
        neg_nat, rden = sb("neg_nat", [P, TT, HG, 3], BF16), sb("rden", [P, TT, HG])

        kqv_dma = [sem(f"kqv{g}_dma") for g in range(NG)]
        mask_max_dma = [sem(f"mask_max{tt}_dma") for tt in range(TT)]
        mask_exp_dma, flag_dma, ones_dma = sem("mask_exp_dma"), sem("flag_dma"), sem("ones_dma")
        o_stored = [sem(f"o_stored{i}") for i in range(2)]
        s_sems, m_sems = (sem("s_full"), sem("s_free")), (sem("m_full"), sem("m_free"))
        pv_done, pv_copied = sem("pv_done"), sem("pv_copied")
        neg_ready = sem("neg_ready")
        dve_steps, waits_apart = sem("dve_steps"), sem("waits_apart")
        KQV = 16 * (6 + 2)
        block = ctx.enter_context(nc.Block())

        @block.sync
        def _(sp):
            def load_group(b, g):
                rows = slice(g * HG * DK, (g + 1) * HG * DK)
                for part, blocks in enumerate(K_BLOCKS):
                    for blk in blocks:
                        sp.dma_start(k_stack[blk * DK:(blk + 1) * DK, g * HG:(g + 1) * HG, :],
                                     scr["k"][part, b, rows, :].rearrange("(h d) n -> d h n", h=HG))\
                            .then_inc(kqv_dma[g], 16)
                sp.dma_start(q_stack[0:PARTS, g * HG:(g + 1) * HG, :].rearrange("p h n -> p (h n)"),
                             scr["q"][b, :, g, :]).then_inc(kqv_dma[g], 16)
                sp.dma_start(v_aug[:, g].rearrange("p j h c -> p (j h c)"), scr["v"][b, :, g, :])\
                    .then_inc(kqv_dma[g], 16)

            def load_mask_max(b, tt):
                sp.dma_start(mask_max[:, tt, :], scr["mask"][b, :, tt, :]).then_inc(mask_max_dma[tt], 16)

            sp.dma_start(k_stack[PARTS:ROWS, :, :], ones).then_inc(ones_dma, 16)
            sp.dma_start(flags[:], scr["flag"]).then_inc(flag_dma, 16)
            for stored in o_stored:
                sp.sem_inc(stored, 16)
            load_group(0, 0)
            for tt in range(TT):
                load_mask_max(0, tt)
            for g in range(1, NG):
                load_group(0, g)
            sp.dma_start(mask_exp[:], scr["mask"][0]).then_inc(mask_exp_dma, 16)
            with sp.Fori(0, B) as b:
                for g in range(NG):
                    sp.wait_ge(m_sems[1], b * M_U + (g * G_M + NATURAL_AT + M_FIRST + N_M))
                    sp.dma_start(scr["o"][b * NG + g], o_nat[:, g % 2]).then_inc(o_stored[g % 2], 16)
                    if g == NG - 2:
                        for tt in range(TT):
                            sp.wait_ge(m_sems[1], b * M_U + (g * G_M + 1 + (tt + 1) * HG * NCH - AHEAD
                                                             + M_FIRST + N_M))
                            apart(sp, waits_apart)
                            load_mask_max(next_batch(b), tt)
                    sp.wait_ge(pv_done, b * PV_STEPS + ((g + 1) * NKT + 2))
                    apart(sp, waits_apart)
                    load_group(next_batch(b), g)
                sp.dma_start(mask_exp[:], scr["mask"][next_batch(b)]).then_inc(mask_exp_dma, 16)
            sp.wait_ge(m_sems[1], M_U * B + (M_FIRST + 1 + N_M))
            sp.dma_start(scr["o"][B * NG], o_nat[:, 0]).then_inc(o_stored[0], 16)
            sp.wait_ge(o_stored[0], 16 * (B * NG // 2 + 2))
            sp.wait_ge(o_stored[1], 16 * (B * NG // 2 + 1))
            for s in kqv_dma:
                sp.wait_ge(s, KQV * (B + 1))
            for s in mask_max_dma + [mask_exp_dma]:
                sp.wait_ge(s, 16 * (B + 1))

        @block.tensor
        def _(pe):
            mm, tr = pe.matmul, pe.transpose
            pe.wait_ge(ones_dma, 16)
            pe.wait_ge(flag_dma, 16)

            def max_chunk(mr, g, hh, tt, c):
                h, (lo, w) = HG * g + hh, CHUNKS[c]
                bank = mr.acquire()
                mm(bank[:, 0:w], q_stack[0:PARTS, h, tt * P:(tt + 1) * P], k_stack[0:PARTS, h, lo:lo + w],
                   start=True, stop=True).then_inc(m_sems[0], 1)

            def max_rows(sr, mr, groups):
                pe.wait_ge(neg_ready, groups + 1)
                for hh in range(HG):
                    ring, full = (sr, s_sems[0]) if hh else (mr, m_sems[0])
                    bank = ring.acquire().bitcast(BF16)
                    for tt in range(TT):
                        last = tr(bank[PARTS:ROWS, tt * P:(tt + 1) * P], neg_nat[:, tt, hh, :], ident_b)
                    last.then_inc(full, 1)

            def natural(mr, groups):
                pe.wait_ge(pv_copied, groups + 1)
                bank = mr.acquire()
                for tt in range(TT):
                    last = tr(bank[:, tt * P:(tt + 1) * P], o_t[:, tt * P:(tt + 1) * P], ident_f[:])
                last.then_inc(m_sems[0], 1)

            sr, mr = Ring(pe, m.s_banks, s_sems, S_U, 0), Ring(pe, m.m_banks, m_sems, M_U, 0)
            pe.wait_ge(kqv_dma[0], KQV)
            for work in MAXIMA:
                max_chunk(mr, 0, *work[1:])
            max_rows(sr, mr, 0)
            pe.wait_ge(kqv_dma[1], KQV)
            for work in MAXIMA[:AHEAD]:
                max_chunk(mr, 1, *work[1:])
            assert (mr.n, sr.n) == (M_FIRST, S_FIRST)

            def group_of_heads(b, g, sr, mr, masked):
                mr.wait_released(max(mr.n - PER_STEP, 1 - N_M))
                sr.wait_released(sr.n)
                for j in range(NKT):
                    r = min(P, KEYS - P * j)
                    side = cross_side_work(j)
                    maxima_of = (g + (1 if j < NKT - 2 else 2)) % NG
                    if j == NKT - 2:
                        pe.wait_ge(kqv_dma[maxima_of], b * KQV + (KQV * (2 if g + 2 >= NG else 1)))
                    if j == NKT - 1:
                        max_rows(sr, mr, b * NG + g + 1)

                    def beside(n):
                        for work in side[:n]:
                            if work[0] == "max":
                                max_chunk(mr, maxima_of, *work[1:])
                            else:
                                natural(mr, b * NG + g)
                        del side[:n]

                    for hh in range(HG):
                        h = HG * g + hh
                        bank = sr.acquire()
                        if masked:
                            for tt in range(TT):
                                mm(bank[0:r, tt * P:(tt + 1) * P], mask_exp[:, tt, j * P:j * P + r], ident_b[:],
                                   start=tt == 0, stop=False, skip_group_check=True)
                        mm(bank[0:r, :], k_stack[0:ROWS, h, j * P:j * P + r], q_stack[0:ROWS, h, :],
                           start=not masked, stop=True, skip_group_check=masked).then_inc(s_sems[0], 1)
                        beside(1)
                    if j > 0:
                        products(b, g, sr, j - 1, sr.n - HG)
                    beside(len(side))
                products(b, g, sr, NKT - 1, sr.n)

            def products(b, g, sr, j, exps):
                r = min(P, KEYS - P * j)
                sr.wait_released(exps)
                if j == 0:
                    pe.wait_ge(pv_copied, b * NG + g + 1)
                for hh in range(HG):
                    last = mm(pv[32 * hh:32 * hh + VW, :], v_aug[0:r, g, j, hh, :],
                              probs[0:r, (g * NKT + j) % 2, hh, :], start=j == 0, stop=j == NKT - 1)
                last.then_inc(pv_done, 1)

            def heads_of_batch(b, masked):
                sr, mr = later_ring(pe, m.s_banks, s_sems, S_U, S_FIRST, b), later_ring(pe, m.m_banks, m_sems, M_U, M_FIRST, b)
                if masked:
                    pe.wait_ge(mask_exp_dma, 16 * b + 16)
                for g in range(NG):
                    group_of_heads(b, g, sr, mr, masked)
                sr.end(), mr.end()

            with pe.Fori(0, B) as b:
                with pe.If(pe.value_load(flags[0:1, bass.ds(b, 1)])):
                    heads_of_batch(b, True)
                with pe.Else():
                    heads_of_batch(b, False)
            last = later_ring(pe, m.m_banks, m_sems, M_U, M_FIRST, B)
            natural(last, B * NG)

        @block.scalar
        def _(act):
            act.sem_inc(s_sems[1], N_S)
            act.sem_inc(pv_done, 2)
            act.sem_inc(pv_copied, 1)

            def rows_in(sr, g):
                for hh in range(1, HG):
                    bank = sr.take().bitcast(BF16)
                    act.activation(q_stack[PARTS:ROWS, HG * g + hh, :], bank[PARTS:ROWS, 0:S], ACT.Copy)\
                        .then_inc(s_sems[1], 1)

            rows_in(Ring(act, m.s_banks, s_sems, S_U, 0), 0)
            with act.Fori(0, B) as b:
                sr = later_ring(act, m.s_banks, s_sems, S_U, S_FIRST, b)
                for step in range(PV_STEPS):
                    r = min(P, KEYS - P * (step % NKT))
                    if step % NKT == NKT - 1:
                        rows_in(sr, (step // NKT + 1) % NG)
                    act.wait_ge(pv_done, b * PV_STEPS + (step + 1))
                    for hh in range(HG):
                        bank = sr.take()
                        act.activation(probs[0:r, step % 2, hh, :], bank[0:r, :], ACT.Exp).then_inc(s_sems[1], 1)
                sr.end()

        @block.vector
        def _(dve):
            dve.memset(pv, 0.0).then_inc(dve_steps, 1)
            dve.memset(o_t[:], 1.0).then_inc(dve_steps, 1)
            dve.wait_ge(dve_steps, 2)
            dve.sem_inc(m_sems[1], N_M)

            def masked_max(mr, hh, tt, c):
                lo, w = CHUNKS[c]
                mr.wait_released(mr.n - 1)
                bank = mr.take()
                apart(dve, waits_apart)
                dve.tensor_tensor_reduce(junk[:, (mr.n + mr.before) % 2, 0:w], bank[:, 0:w], mask_max[:, tt, lo:lo + w], 1.0,
                                         -FLT_MAX, ALU.add, ALU.max, mx[:, tt * HG + hh, c:c + 1])\
                    .then_inc(m_sems[1], 1)

            def negate(v, mr):
                mr.wait_released(mr.n)
                v(dve.tensor_reduce(neg[:], mx[:], AX.X, ALU.max, negate=True))
                flat = neg_nat[:].rearrange("p t h c -> p (t h) c")
                for part in range(3):
                    ins = dve.tensor_copy(flat[:, :, part], neg[:])
                    if part < 2:
                        v(ins)
                        v(dve.tensor_tensor(neg[:], neg[:], flat[:, :, part], ALU.subtract))
                    else:
                        ins.then_inc(neg_ready, 1)

            def row_in(mr, g):
                bank = mr.take().bitcast(BF16)
                dve.tensor_copy(q_stack[PARTS:ROWS, HG * g, :], bank[PARTS:ROWS, 0:S]).then_inc(m_sems[1], 1)

            def natural(v, mr, slot):
                bank = mr.take().rearrange("p (t h c) -> p t h c", t=TT, h=HG)
                v(dve.reciprocal(rden[:], bank[:, :, :, DK]))
                dve.tensor_tensor(o_nat[:, slot], bank[:, :, :, 0:DK],
                                  rden[:].unsqueeze(3).to_broadcast([P, TT, HG, DK]), ALU.mult).then_inc(m_sems[1], 1)

            first, v = Ring(dve, m.m_banks, m_sems, M_U, 0), Chain(dve, dve_steps, 5, 0)
            v.base = 2
            for work in MAXIMA:
                if first.n % (HG * NCH) == 0:
                    dve.wait_ge(mask_max_dma[work[2]], 16)
                if first.n == 0:
                    lo, w = CHUNKS[0]
                    bank = first.take()
                    dve.tensor_tensor_reduce(junk[:, 1, 0:w], bank[:, 0:w], mask_max[:, 0, lo:lo + w], 1.0,
                                             -FLT_MAX, ALU.add, ALU.max, mx[:, 0, 0:1]).then_inc(m_sems[1], 1)
                else:
                    masked_max(first, *work[1:])
            negate(v, first)
            row_in(first, 0)
            for work in MAXIMA[:AHEAD]:
                masked_max(first, *work[1:])
            v.end()
            with dve.Fori(0, B) as b:
                v, mr = Chain(dve, dve_steps, 6 * NG, b), later_ring(dve, m.m_banks, m_sems, M_U, M_FIRST, b)
                v.base = b * v.per + 7
                for g in range(NG):
                    for j in range(NKT):
                        if j == NKT - 1:
                            row_in(mr, (g + 1) % NG)
                        for work in cross_side_work(j):
                            if work[0] == "max":
                                new_batch = g + (1 if j < NKT - 2 else 2) == NG
                                if new_batch and work[1] == 0 and work[3] == 0:
                                    dve.wait_ge(mask_max_dma[work[2]], 16 * b + 32)
                                masked_max(mr, *work[1:])
                            else:
                                dve.wait_ge(o_stored[g % 2], b * (16 * NG // 2) + 16 * (g // 2 + 1))
                                natural(v, mr, g % 2)
                        if j == NKT - 3:
                            negate(v, mr)
                    dve.wait_ge(pv_done, b * PV_STEPS + ((g + 1) * NKT + 2))
                    dve.tensor_copy(o_t[:], pv).then_inc(pv_copied, 1)
                v.end(), mr.end()
            last = later_ring(dve, m.m_banks, m_sems, M_U, M_FIRST, B)
            bank = last.take().rearrange("p (t h c) -> p t h c", t=TT, h=HG)
            v = Chain(dve, dve_steps, 1, 0)
            v.base = B * 6 * NG + 7
            v(dve.reciprocal(rden[:], bank[:, :, :, DK]))
            dve.wait_ge(o_stored[0], 16 * (B * NG // 2 + 1))
            dve.tensor_tensor(o_nat[:, 0], bank[:, :, :, 0:DK], rden[:].unsqueeze(3).to_broadcast([P, TT, HG, DK]),
                              ALU.mult).then_inc(m_sems[1], 1)


def stack_of_two(eng, bank_of, src, pair, ident_b):
    bank = bank_of.bitcast(BF16)
    for i in range(2):
        for tt in range(TT):
            at = i * S + tt * P
            last = eng.transpose(bank[0:PARTS, at:at + P], src[:, tt, 2 * pair + i, :], ident_b)
    return last


def self_inputs_phase(nc, sems, banks, consts, x, w_cross, w_self, scr):
    BY_DVE = 4
    PAIRS = H // 2
    M_U, S_U = 2 * TT + 2 * PAIRS // BY_DVE, 2 * KT + TT + 2 * (PAIRS - PAIRS // BY_DVE)
    M_FIRST, S_FIRST = 3 * TT, 3 * KT + TT
    INPUTS = 16 * (1 + NG)
    with ExitStack() as ctx:
        m = Memory(nc, ctx, sems, "inputs", banks)
        sb, sem = m.sb, m.sem
        ident_f, ident_b, half, row_c = (consts[n] for n in ("identf", "identb", "half", "row_c"))
        bo, n1w, qkw = row_c[:, 2 * D:3 * D], row_c[:, 3 * D:4 * D], row_c[:, 5 * D:7 * D]
        wo, wqkv = sb("wo", [P, KT, D]), sb("wqkv", [P, KT, 3 * D])
        x_in, o_nat, o_natT = sb("x_in", [P, TT, D]), sb("o_nat", [P, TT, D]), sb("o_natT", [P, KT, S])
        x1, xn = sb("x1", [P, TT, D]), sb("xn", [P, TT, D])
        nat, natT = sb("nat", [P, TT, D]), sb("natT", [P, KT, S])
        qk_slots, squares = sb("qk", [P, 2, TT, 2 * D]), sb("squares", [P, TT, 2 * D])
        vs = sb("vs", [P, NG, TT, HG, VW])
        q_nat, k_nat = sb("q_nat", [P, TT, H, PARTS], BF16), sb("k_nat", [P, TT, H, PARTS], BF16)
        q_stack, k_stack = sb("q_stack", [PARTS, H, S], BF16), sb("k_stack", [PARTS, H, S], BF16)
        junk, stats, mv = sb("junk", [P, TT, D], BF16), sb("stats", [P, TT, 6]), sb("mv", [P, TT, 2])
        sums = sb("sums", [P, TT])
        ln_ms, ln_rs, rms_ms, rms_rs = (sb(n, [P, TT]) for n in ("ln_ms", "ln_rs", "rms_ms", "rms_rs"))
        head_ms, head_rs = sb("head_ms", [P, TT, 2, H]), sb("head_rs", [P, TT, 2, H])

        w_dma, in_dma, setup = sem("w_dma"), sem("in_dma"), sem("setup")
        x1_stored, xn_stored = sem("x1_stored"), sem("xn_stored")
        q_stored, k_stored, v_stored = sem("q_stored"), sem("k_stored"), sem("v_stored")
        s_sems, m_sems = (sem("s_full"), sem("s_free")), (sem("m_full"), sem("m_free"))
        x1_ready, xn_ready, nat_ready = sem("x1_ready"), sem("xn_ready"), sem("nat_ready")
        ln_in, ln_out, rms_in, rms_out, head_in, k_out, q_out = (
            sem(n) for n in ("ln_in", "ln_out", "rms_in", "rms_out", "head_in", "k_out", "q_out"))
        keys_ready, queries_ready = sem("keys_ready"), sem("queries_ready")
        k_split, q_split = ((sem(f"{n}_cast"), sem(f"{n}_left"), sem(f"{n}_copied")) for n in "kq")
        dve_steps, waits_apart = sem("dve_steps"), sem("waits_apart")
        queries, keys = ([heads(qk_slots[:, u, :, lo:lo + D]) for u in range(2)] for lo in (0, D))

        def q_part(i):
            return q_nat[:, :, :, i * DK:(i + 1) * DK]

        def k_part(i):
            return k_nat[:, :, :, i * DK:(i + 1) * DK]
        block = ctx.enter_context(nc.Block())

        @block.sync
        def _(sp):
            def load_inputs(b):
                sp.dma_start(x_in[:], x[b]).then_inc(in_dma, 16)
                for g in range(NG):
                    sp.dma_start(o_nat[:, :, g * HG * DK:(g + 1) * HG * DK],
                                 scr["o"][b * NG + (g + 1)].rearrange("p t h c -> p t (h c)")).then_inc(in_dma, 16)

            def store_x1(b):
                sp.wait_ge(x1_ready, b + 1)
                apart(sp, waits_apart)
                load_inputs(next_batch(b))
                sp.dma_start(scr["x1"][b], x1[:]).then_inc(x1_stored, 16)

            def store_xn(b):
                sp.wait_ge(xn_ready, b + 1)
                apart(sp, waits_apart)
                sp.dma_start(scr["xn"][b], xn[:]).then_inc(xn_stored, 16)

            def store_values(b, uses):
                sp.wait_ge(m_sems[1], uses + N_M)
                apart(sp, waits_apart)
                sp.dma_start(scr["vs"][b], vs[:].rearrange("p g j h c -> p g (j h c)")).then_inc(v_stored, 16)

            load_inputs(0)
            sp.dma_start(wo[:], w_cross[:, 3]).then_inc(w_dma, 16)
            sp.dma_start(wqkv[:], w_self[:, :, 0:3 * D]).then_inc(w_dma, 16)
            for stored in (x1_stored, xn_stored, q_stored, k_stored, v_stored):
                sp.sem_inc(stored, 16)
            store_x1(0)
            store_xn(0)
            store_values(0, 2 * TT)
            store_x1(1)
            with sp.Fori(0, B) as b:
                store_xn(b + 1)
                store_x1(b + 2)
                store_values(b + 1, b * M_U + (M_FIRST + 2 * TT))
                sp.wait_ge(m_sems[1], b * M_U + (M_FIRST + 2 * TT + PAIRS // BY_DVE + N_M))
                apart(sp, waits_apart)
                sp.wait_ge(s_sems[1], b * S_U + (S_FIRST + 2 * KT + TT + PAIRS - PAIRS // BY_DVE + N_S))
                sp.dma_start(scr["ks"][b], k_stack[:].rearrange("p (g h) n -> p g (h n)", g=NG)).then_inc(k_stored, 16)
                sp.wait_ge(m_sems[1], b * M_U + (M_FIRST + M_U + N_M))
                apart(sp, waits_apart)
                sp.wait_ge(s_sems[1], b * S_U + (S_FIRST + S_U + N_S))
                sp.dma_start(scr["qs"][b], q_stack[:].rearrange("p (g h) n -> p g (h n)", g=NG)).then_inc(q_stored, 16)
            for stored, n in ((x1_stored, B + 3), (xn_stored, B + 2), (q_stored, B + 1), (k_stored, B + 1),
                              (v_stored, B + 2)):
                sp.wait_ge(stored, 16 * n)
            sp.wait_ge(in_dma, INPUTS * (B + 3))

        @block.gpsimd
        def _(pool):
            pool.memset(vs[:], 1.0).then_inc(setup, 1)

            def root(b, sem_in, sem_out, ms, rs, exponents):
                pool.wait_ge(sem_in, b + 1)
                pool.tensor_tensor(rs, ms, exponents, ALU.pow).then_inc(sem_out, 1)

            def head_root(b, side, sem_out):
                root(b, head_in, sem_out, head_ms[:, :, side, :], head_rs[:, :, side, :],
                     half[:, 0:TT * H].rearrange("p (t h) -> p t h", t=TT))

            root(0, ln_in, ln_out, ln_ms[:], ln_rs[:], half[:, 0:TT])
            root(0, rms_in, rms_out, rms_ms[:], rms_rs[:], half[:, 0:TT])
            root(1, ln_in, ln_out, ln_ms[:], ln_rs[:], half[:, 0:TT])
            with pool.Fori(0, B // 2) as pair:
                for u in range(2):
                    b = pair * 2 + u
                    head_root(b, 1, k_out)
                    root(b + 1, rms_in, rms_out, rms_ms[:], rms_rs[:], half[:, 0:TT])
                    head_root(b, 0, q_out)
                    root(b + 2, ln_in, ln_out, ln_ms[:], ln_rs[:], half[:, 0:TT])
                    subtract_parts(pool, q_part, queries[u], Q_BLOCKS, q_split, waits_apart, b)

        @block.tensor
        def _(pe):
            mm, tr = pe.matmul, pe.transpose
            pe.wait_ge(w_dma, 32)
            pe.wait_ge(setup, 1)

            def transposed(sr, src):
                for kt in range(KT):
                    bank = sr.acquire()
                    for tt in range(TT):
                        last = tr(bank[:, tt * P:(tt + 1) * P], src[:, tt, kt * P:(kt + 1) * P], ident_f)
                    last.then_inc(s_sems[0], 1)

            def project(ring, full, src, w, width):
                for tt in range(TT):
                    bank = ring.acquire()
                    for kt in range(KT):
                        last = mm(bank[:, 0:width], src[:, kt, tt * P:(tt + 1) * P], w[:, kt, :],
                                  start=kt == 0, stop=kt == KT - 1)
                    last.then_inc(full, 1)

            def attention_transposed(sr, b):
                pe.wait_ge(in_dma, INPUTS * b + INPUTS)
                transposed(sr, o_nat)

            def project_out(sr, mr, copied):
                sr.wait_released(copied)
                project(mr, m_sems[0], o_natT, wo, D)

            def stacks(sr, mr, src):
                for pair in range(PAIRS):
                    ring, full = (sr, s_sems[0]) if pair % BY_DVE else (mr, m_sems[0])
                    stack_of_two(pe, ring.acquire(), src, pair, ident_b).then_inc(full, 1)

            def project_qkv(sr, mr):
                project(sr, s_sems[0], natT, wqkv[:, :, 0:2 * D], 2 * D)
                project(mr, m_sems[0], natT, wqkv[:, :, 2 * D:3 * D], D)

            sr, mr = Ring(pe, m.s_banks, s_sems, S_U, 0), Ring(pe, m.m_banks, m_sems, M_U, 0)
            attention_transposed(sr, 0)
            project_out(sr, mr, sr.n)
            pe.wait_ge(nat_ready, 1)
            transposed(sr, nat)
            sr.wait_released(sr.n)
            project_qkv(sr, mr)
            attention_transposed(sr, 1)
            project_out(sr, mr, sr.n)
            assert (sr.n, mr.n) == (S_FIRST, M_FIRST)
            with pe.Fori(0, B) as b:
                sr = later_ring(pe, m.s_banks, s_sems, S_U, S_FIRST, b)
                mr = later_ring(pe, m.m_banks, m_sems, M_U, M_FIRST, b)
                attention_transposed(sr, b + 2)
                pe.wait_ge(nat_ready, b + 2)
                transposed(sr, nat)
                project_out(sr, mr, KT)
                sr.wait_released(sr.n)
                project_qkv(sr, mr)
                wait_split(pe, k_split, b)
                stacks(sr, mr, k_nat)
                wait_split(pe, q_split, b)
                stacks(sr, mr, q_nat)
                sr.end(), mr.end()

        @block.scalar
        def _(act):
            act.sem_inc(s_sems[1], N_S)

            def copies(sr, dst, n, width=S):
                for i in range(n):
                    bank = sr.take()
                    act.activation(dst[:, i, 0:width], bank[:, 0:width], ACT.Copy).then_inc(s_sems[1], 1)

            def stacks(sr, dst):
                for pair in range(PAIRS):
                    if pair % BY_DVE:
                        bank = sr.take().bitcast(BF16)
                        act.activation(dst[:, 2 * pair:2 * pair + 2, :],
                                       bank[0:PARTS, :].rearrange("p (h n) -> p h n", h=2), ACT.Copy)\
                            .then_inc(s_sems[1], 1)

            sr = Ring(act, m.s_banks, s_sems, S_U, 0)
            copies(sr, o_natT, KT)
            copies(sr, natT, KT)
            copies(sr, qk_slots[:, 0], TT)
            copies(sr, o_natT, KT)
            with act.Fori(0, B // 2) as pair:
                for u in range(2):
                    b = pair * 2 + u
                    sr = later_ring(act, m.s_banks, s_sems, S_U, S_FIRST, b)
                    copies(sr, o_natT, KT)
                    copies(sr, natT, KT)
                    act.wait_ge(keys_ready, b + 1)
                    for part in range(3):
                        cast_part(act, k_part, keys[u], K_BLOCKS, part, k_split, b)
                    copies(sr, qk_slots[:, 1 - u], TT)
                    act.wait_ge(queries_ready, b + 1)
                    for part in range(3):
                        cast_part(act, q_part, queries[u], Q_BLOCKS, part, q_split, b)
                    act.wait_ge(k_stored, 16 * b + 16)
                    stacks(sr, k_stack)
                    act.wait_ge(q_stored, 16 * b + 16)
                    stacks(sr, q_stack)
                    sr.end()

        @block.vector
        def _(dve):
            dve.wait_ge(setup, 1)
            dve.sem_inc(m_sems[1], N_M)

            def rows_x1(v, mr, b):
                dve.wait_ge(in_dma, INPUTS * b + INPUTS)
                for tt in range(TT):
                    v.step(dve.tensor_tensor(x_in[:, tt, :], x_in[:, tt, :], bo, ALU.add))
                dve.wait_ge(x1_stored, 16 * b + 16)
                v.settle()
                for tt in range(TT):
                    bank = mr.take()
                    dve.tensor_tensor(x1[:, tt, :], bank[:, 0:D], x_in[:, tt, :], ALU.add).then_inc(m_sems[1], 1)
                mr.wait_released(mr.n)
                dve.sem_inc(x1_ready, 1)
                for tt in range(TT):
                    v.step(dve.bn_stats(stats[:, tt, :], x1[:, tt, :]))
                v.settle()
                apart(dve, waits_apart)
                for tt in range(TT):
                    v.step(dve.bn_aggr(mv[:, tt, :], stats[:, tt, :]))
                v.settle()
                dve.tensor_scalar(ln_ms[:], mv[:, :, 1], LN_EPS, None, ALU.add).then_inc(ln_in, 1)

            def rows_xn(v, b):
                dve.wait_ge(ln_out, b + 1)
                dve.wait_ge(xn_stored, 16 * b + 16)
                for tt in range(TT):
                    v.step(dve.tensor_scalar(xn[:, tt, :], x1[:, tt, :], mv[:, tt, 0:1], ln_rs[:, tt:tt + 1],
                                             ALU.subtract, ALU.mult))
                v.settle()
                dve.sem_inc(xn_ready, 1)
                for tt in range(TT):
                    v.step(dve.tensor_tensor_reduce(junk[:, tt, :], xn[:, tt, :], xn[:, tt, :], 1.0, 0.0,
                                                    ALU.mult, ALU.add, sums[:, tt:tt + 1]))
                v.settle()
                dve.tensor_scalar(rms_ms[:], sums[:], 1.0 / D, RMS_EPS, ALU.mult, ALU.add).then_inc(rms_in, 1)

            def rows_nat(v, b):
                dve.wait_ge(rms_out, b + 1)
                for tt in range(TT):
                    ins = dve.scalar_tensor_tensor(nat[:, tt, :], xn[:, tt, :], rms_rs[:, tt:tt + 1], n1w,
                                                   ALU.mult, ALU.mult)
                    ins.then_inc(nat_ready, 1) if tt == TT - 1 else v.step(ins)

            def values(mr, b):
                dve.wait_ge(v_stored, 16 * b + 16)
                for tt in range(TT):
                    bank = mr.take()
                    dve.tensor_copy(vs[:, :, tt, :, 0:DK], bank[:, 0:D].rearrange("p (g h c) -> p g h c", g=NG, h=HG))\
                        .then_inc(m_sems[1], 1)

            def stacks(mr, dst):
                for pair in range(0, PAIRS, BY_DVE):
                    bank = mr.take().bitcast(BF16)
                    dve.tensor_copy(dst[:, 2 * pair:2 * pair + 2, :],
                                    bank[0:PARTS, :].rearrange("p (h n) -> p h n", h=2)).then_inc(m_sems[1], 1)

            def head_squares(v, slot, uses):
                qk = qk_slots[:, slot]
                dve.wait_ge(s_sems[1], uses + N_S)
                for tt in range(TT):
                    v.step(dve.tensor_tensor(squares[:, tt, :], qk[:, tt, :], qk[:, tt, :], ALU.mult))
                v.settle()
                flat = head_ms[:].rearrange("p t s h -> p (t s h)")
                v(dve.tensor_reduce(flat, squares[:].rearrange("p t (h c) -> p (t h) c", c=DK), AX.X, ALU.add))
                dve.tensor_scalar(flat, flat, 1.0 / DK, RMS_EPS, ALU.mult, ALU.add).then_inc(head_in, 1)

            def head_norm(v, slot, side, ready):
                lo = D * side
                for tt in range(TT):
                    view = qk_slots[:, slot, tt, lo:lo + D].rearrange("p (h c) -> p h c", c=DK)
                    v.step(dve.tensor_tensor(view, view, head_rs[:, tt, side, :].unsqueeze(2).to_broadcast([P, H, DK]),
                                             ALU.mult))
                v.settle()
                for tt in range(TT):
                    row = qk_slots[:, slot, tt, lo:lo + D]
                    ins = dve.tensor_tensor(row, row, qkw[:, lo:lo + D], ALU.mult)
                    ins.then_inc(ready, 1) if tt == TT - 1 else v.step(ins)

            v, mr = Chain(dve, dve_steps, 40, 0), Ring(dve, m.m_banks, m_sems, M_U, 0)
            rows_x1(v, mr, 0)
            rows_xn(v, 0)
            rows_nat(v, 0)
            values(mr, 0)
            head_squares(v, 0, 2 * KT + TT)
            rows_x1(v, mr, 1)
            v.end()
            with dve.Fori(0, B // 2) as pair:
                for u in range(2):
                    b = pair * 2 + u
                    v, mr = Chain(dve, dve_steps, 42, b), later_ring(dve, m.m_banks, m_sems, M_U, M_FIRST, b)
                    v.base = b * v.per + 40
                    rows_xn(v, b + 1)
                    rows_nat(v, b + 1)
                    dve.wait_ge(k_out, b + 1)
                    head_norm(v, u, 1, keys_ready)
                    rows_x1(v, mr, b + 2)
                    subtract_parts(dve, k_part, keys[u], K_BLOCKS, k_split, waits_apart, b)
                    dve.wait_ge(q_out, b + 1)
                    head_norm(v, u, 0, queries_ready)
                    values(mr, b + 1)
                    head_squares(v, 1 - u, b * S_U + (S_FIRST + 2 * KT + TT))
                    dve.wait_ge(k_stored, 16 * b + 16)
                    stacks(mr, k_stack)
                    dve.wait_ge(q_stored, 16 * b + 16)
                    stacks(mr, q_stack)
                    v.end(), mr.end()


SELF_MAXIMA = [("max", hh, tt) for tt in range(TT) for hh in range(HG)]
SELF_AHEAD = 6


def self_side_work(j):
    if j >= 2:
        return SELF_MAXIMA[3 * (j - 2):3 * (j - 1)]
    work = SELF_MAXIMA[SELF_AHEAD + 5 * j:SELF_AHEAD + 5 * (j + 1)]
    if j == 0:
        work.insert(3, ("natural",))
    return work


def self_phase(nc, sems, banks, consts, scr, ones):
    G_M, G_S = HG * TT + 2, HG * TT + HG - 1
    M_U, S_U = NG * G_M, NG * G_S
    M_FIRST, S_FIRST = HG * TT + 1 + SELF_AHEAD, HG - 1
    PV_STEPS = NG * TT
    with ExitStack() as ctx:
        m = Memory(nc, ctx, sems, "self", banks)
        sb, sem, pv = m.sb, m.sem, m.pv
        ident_f, ident_b, causal_q, causal_k = (consts[n] for n in ("identf", "identb", "causal_q", "causal_k"))
        k_stack = sb("k_stack", [ROWS, H, S], BF16)
        q_stack = sb("q_stack", [ROWS, H, S], BF16)
        vs = sb("vs", [P, NG, TT, HG, VW])
        probs = sb("probs", [P, 2, HG, S])
        o_t, o_nat = sb("o_t", [P, S]), sb("o_nat", [P, 2, TT, HG, DK])
        junk = sb("junk", [P, 2, S], BF16)
        mx, neg = sb("mx", [P, TT * HG]), sb("neg", [P, TT * HG])
        neg_nat, rden = sb("neg_nat", [P, TT, HG, 3], BF16), sb("rden", [P, TT, HG])

        kqv_dma = [sem(f"kqv{g}_dma") for g in range(NG)]
        ones_dma = sem("ones_dma")
        o_stored = [sem(f"o_stored{i}") for i in range(2)]
        s_sems, m_sems = (sem("s_full"), sem("s_free")), (sem("m_full"), sem("m_free"))
        pv_done, pv_copied = sem("pv_done"), sem("pv_copied")
        neg_ready = sem("neg_ready")
        dve_steps, waits_apart = sem("dve_steps"), sem("waits_apart")
        KQV = 16 * 3
        NATURAL = 4
        block = ctx.enter_context(nc.Block())

        @block.sync
        def _(sp):
            def load_group(b, g):
                hs = slice(g * HG, (g + 1) * HG)
                for stack, name in ((k_stack, "ks"), (q_stack, "qs")):
                    sp.dma_start(stack[0:PARTS, hs, :].rearrange("p h n -> p (h n)"), scr[name][b, :, g, :])\
                        .then_inc(kqv_dma[g], 16)
                sp.dma_start(vs[:, g].rearrange("p j h c -> p (j h c)"), scr["vs"][b, :, g, :])\
                    .then_inc(kqv_dma[g], 16)

            sp.dma_start(k_stack[PARTS:ROWS, :, :], ones[:, :, 0:S]).then_inc(ones_dma, 16)
            for stored in o_stored:
                sp.sem_inc(stored, 16)
            for g in range(NG):
                load_group(0, g)
            with sp.Fori(0, B) as b:
                for g in range(NG):
                    sp.wait_ge(m_sems[1], b * M_U + (g * G_M + NATURAL + M_FIRST + N_M))
                    sp.dma_start(scr["os"][b * NG + g], o_nat[:, g % 2]).then_inc(o_stored[g % 2], 16)
                    sp.wait_ge(pv_done, b * PV_STEPS + ((g + 1) * TT + 2))
                    apart(sp, waits_apart)
                    load_group(next_batch(b), g)
            sp.wait_ge(m_sems[1], M_U * B + (M_FIRST + 1 + N_M))
            sp.dma_start(scr["os"][B * NG], o_nat[:, 0]).then_inc(o_stored[0], 16)
            sp.wait_ge(o_stored[0], 16 * (B * NG // 2 + 2))
            sp.wait_ge(o_stored[1], 16 * (B * NG // 2 + 1))
            for s in kqv_dma:
                sp.wait_ge(s, KQV * (B + 1))

        @block.tensor
        def _(pe):
            mm, tr = pe.matmul, pe.transpose
            pe.wait_ge(ones_dma, 16)

            def max_tile(mr, g, hh, tt):
                h, w = HG * g + hh, P * (tt + 1)
                bank = mr.acquire()
                mm(bank[:, 0:w], q_stack[0:PARTS, h, tt * P:(tt + 1) * P], k_stack[0:PARTS, h, 0:w],
                   start=True, stop=True).then_inc(m_sems[0], 1)

            def max_rows(sr, mr, groups):
                pe.wait_ge(neg_ready, groups + 1)
                for hh in range(HG):
                    ring, full = (sr, s_sems[0]) if hh else (mr, m_sems[0])
                    bank = ring.acquire().bitcast(BF16)
                    for tt in range(TT):
                        last = tr(bank[PARTS:ROWS, tt * P:(tt + 1) * P], neg_nat[:, tt, hh, :], ident_b)
                    last.then_inc(full, 1)

            def natural(mr, groups):
                pe.wait_ge(pv_copied, groups + 1)
                bank = mr.acquire()
                for tt in range(TT):
                    last = tr(bank[:, tt * P:(tt + 1) * P], o_t[:, tt * P:(tt + 1) * P], ident_f)
                last.then_inc(m_sems[0], 1)

            sr, mr = Ring(pe, m.s_banks, s_sems, S_U, 0), Ring(pe, m.m_banks, m_sems, M_U, 0)
            pe.wait_ge(kqv_dma[0], KQV)
            for work in SELF_MAXIMA:
                max_tile(mr, 0, *work[1:])
            max_rows(sr, mr, 0)
            pe.wait_ge(kqv_dma[1], KQV)
            for work in SELF_MAXIMA[:SELF_AHEAD]:
                max_tile(mr, 1, *work[1:])
            assert (mr.n, sr.n) == (M_FIRST, S_FIRST)

            def products(b, g, sr, j, exps):
                sr.wait_released(exps)
                if j == 0:
                    pe.wait_ge(pv_copied, b * NG + g + 1)
                for hh in range(HG):
                    last = mm(pv[32 * hh:32 * hh + VW, P * j:S], vs[:, g, j, hh, :],
                              probs[:, j % 2, hh, 0:S - P * j], start=j == 0, stop=j == TT - 1)
                last.then_inc(pv_done, 1)

            with pe.Fori(0, B) as b:
                sr = later_ring(pe, m.s_banks, s_sems, S_U, S_FIRST, b)
                mr = later_ring(pe, m.m_banks, m_sems, M_U, M_FIRST, b)
                for g in range(NG):
                    mr.wait_released(max(mr.n - SELF_AHEAD // 2, 1 - N_M))
                    sr.wait_released(sr.n)
                    for j in range(TT):
                        maxima_of = (g + (1 if j < 2 else 2)) % NG
                        if j == 2:
                            pe.wait_ge(kqv_dma[maxima_of], b * KQV + (KQV * (2 if g + 2 >= NG else 1)))
                        if j == TT - 1:
                            max_rows(sr, mr, b * NG + g + 1)
                        lo, side = P * j, self_side_work(j)

                        def beside(n):
                            for work in side[:n]:
                                if work[0] == "max":
                                    max_tile(mr, maxima_of, *work[1:])
                                else:
                                    natural(mr, b * NG + g)
                            del side[:n]

                        for hh in range(HG):
                            h = HG * g + hh
                            bank = sr.acquire()
                            mm(bank[:, 0:S - lo], k_stack[0:ROWS, h, lo:lo + P], q_stack[0:ROWS, h, lo:S],
                               start=True, stop=False)
                            mm(bank[:, 0:P], ident_b, causal_k, start=False, stop=True).then_inc(s_sems[0], 1)
                            beside(1)
                        exps = sr.n
                        if j > 0:
                            products(b, g, sr, j - 1, exps - HG)
                        beside(len(side))
                    products(b, g, sr, TT - 1, exps)
                sr.end(), mr.end()
            natural(later_ring(pe, m.m_banks, m_sems, M_U, M_FIRST, B), B * NG)

        @block.scalar
        def _(act):
            act.sem_inc(s_sems[1], N_S)
            act.sem_inc(pv_done, 2)
            act.sem_inc(pv_copied, 1)

            def rows_in(sr, g):
                for hh in range(1, HG):
                    bank = sr.take().bitcast(BF16)
                    act.activation(q_stack[PARTS:ROWS, HG * g + hh, :], bank[PARTS:ROWS, 0:S], ACT.Copy)\
                        .then_inc(s_sems[1], 1)

            rows_in(Ring(act, m.s_banks, s_sems, S_U, 0), 0)
            with act.Fori(0, B) as b:
                sr = later_ring(act, m.s_banks, s_sems, S_U, S_FIRST, b)
                for g in range(NG):
                    for j in range(TT):
                        if j == TT - 1:
                            rows_in(sr, (g + 1) % NG)
                        act.wait_ge(pv_done, b * PV_STEPS + (g * TT + j + 1))
                        for hh in range(HG):
                            bank = sr.take()
                            act.activation(probs[:, j % 2, hh, 0:S - P * j], bank[:, 0:S - P * j], ACT.Exp)\
                                .then_inc(s_sems[1], 1)
                sr.end()

        @block.vector
        def _(dve):
            dve.memset(pv, 0.0).then_inc(dve_steps, 1)
            dve.memset(o_t[:], 1.0).then_inc(dve_steps, 1)
            dve.wait_ge(dve_steps, 2)
            dve.sem_inc(m_sems[1], N_M)

            def masked_max(mr, hh, tt):
                w = P * (tt + 1)
                mr.wait_released(max(mr.n - 1, 1 - N_M))
                bank = mr.take()
                apart(dve, waits_apart)
                dve.tensor_tensor_reduce(junk[:, (mr.n + mr.before) % 2, 0:w], bank[:, 0:w], causal_q[:, S - w:S], 1.0,
                                         -FLT_MAX, ALU.add, ALU.max, mx[:, tt * HG + hh:tt * HG + hh + 1])\
                    .then_inc(m_sems[1], 1)

            def negate(v, mr):
                mr.wait_released(mr.n)
                v(dve.tensor_scalar(neg[:], mx[:], -1.0, None, ALU.mult))
                flat = neg_nat[:].rearrange("p t h c -> p (t h) c")
                for part in range(3):
                    ins = dve.tensor_copy(flat[:, :, part], neg[:])
                    if part < 2:
                        v(ins)
                        v(dve.tensor_tensor(neg[:], neg[:], flat[:, :, part], ALU.subtract))
                    else:
                        ins.then_inc(neg_ready, 1)

            def row_in(mr, g):
                bank = mr.take().bitcast(BF16)
                dve.tensor_copy(q_stack[PARTS:ROWS, HG * g, :], bank[PARTS:ROWS, 0:S]).then_inc(m_sems[1], 1)

            def natural(v, mr, slot):
                bank = mr.take().rearrange("p (t h c) -> p t h c", t=TT, h=HG)
                v(dve.reciprocal(rden[:], bank[:, :, :, DK]))
                dve.tensor_tensor(o_nat[:, slot], bank[:, :, :, 0:DK],
                                  rden[:].unsqueeze(3).to_broadcast([P, TT, HG, DK]), ALU.mult).then_inc(m_sems[1], 1)

            v, mr = Chain(dve, dve_steps, 5, 0), Ring(dve, m.m_banks, m_sems, M_U, 0)
            v.base = 2
            for work in SELF_MAXIMA:
                masked_max(mr, *work[1:])
            negate(v, mr)
            row_in(mr, 0)
            for work in SELF_MAXIMA[:SELF_AHEAD]:
                masked_max(mr, *work[1:])
            v.end()
            with dve.Fori(0, B) as b:
                v, mr = Chain(dve, dve_steps, 6 * NG, b), later_ring(dve, m.m_banks, m_sems, M_U, M_FIRST, b)
                v.base = b * v.per + 7
                for g in range(NG):
                    for j in range(TT):
                        if j == TT - 1:
                            row_in(mr, (g + 1) % NG)
                        for work in self_side_work(j):
                            if work[0] == "max":
                                masked_max(mr, *work[1:])
                            else:
                                dve.wait_ge(o_stored[g % 2], b * (16 * NG // 2) + 16 * (g // 2 + 1))
                                natural(v, mr, g % 2)
                        if j == 1:
                            negate(v, mr)
                    dve.wait_ge(pv_done, b * PV_STEPS + ((g + 1) * TT + 2))
                    dve.tensor_copy(o_t[:], pv).then_inc(pv_copied, 1)
                v.end(), mr.end()
            mr = later_ring(dve, m.m_banks, m_sems, M_U, M_FIRST, B)
            v = Chain(dve, dve_steps, 1, 0)
            v.base = B * 6 * NG + 7
            dve.wait_ge(o_stored[0], 16 * (B * NG // 2 + 1))
            natural(v, mr, 0)


SPLIT_W = {}
_at = 0
for _name in ("e0_up", "e1_w1", "e1_w2", "e2_l1", "e2_l2", "e3_down", "e2_l3", "e3_up"):
    SPLIT_W[_name] = (int(_name[1]), _at)
    _at += FFN_W[_name][1] * FFN_W[_name][2]
SPLIT_WORDS = _at
STAGE_AT = {"e0_up": 2048, "e1_w1": 0, "e1_w2": 1024, "e2_l1": 2048, "e2_l2": 0, "e3_down": 2048, "e2_l3": 0,
            "e3_up": 2048}
STAGE_WORDS = 3072
DOWN_AT = {name: i * HT * DOUT for i, name in enumerate(("e0_down", "e1_down", "e2_l4", "e3_out"))}


def expert_phase(nc, sems, banks, consts, w_self, gate_t, ffn_w, scr, out):
    M_FRONT, S_FRONT = KT + TT + 1, KT
    M_U, S_U = M_FRONT + HT + 4 * TT, S_FRONT + 2 * HT + 3 * HT + KT + HT
    S_SILU, S_L1, S_L2, S_E3, S_ROWS = HT, 2 * HT, 3 * HT, 4 * HT, 5 * HT + KT
    SPLITS = 2 * HT + 2 * KT
    INPUTS = 16 * (2 + NG)
    with ExitStack() as ctx:
        m = Memory(nc, ctx, sems, "expert", banks)
        sb, sem = m.sb, m.sem
        ident_f, half, row_c = (consts[n] for n in ("identf", "half", "row_c"))
        n2w = row_c[:, 4 * D:5 * D]
        down_w, stage = sb("down_w", [P, 4 * HT * DOUT]), sb("stage", [P, STAGE_WORDS])
        wo, gate_w = sb("wo", [P, KT, DOUT]), sb("gate_w", [P, KT, 4])
        o_nat, o_natT = sb("o_nat", [P, TT, D]), sb("o_natT", [P, KT, S])
        x1, x2 = sb("x1", [P, TT, D]), sb("x2", [P, TT, D])
        nat, natT = sb("nat", [P, TT, D]), sb("natT", [P, KT, S])
        acc, lg = sb("acc", [P, 2, TT, D]), sb("lg", [P, 2, TT, 4])
        h0, h1 = sb("h0", [P, HT, S])[:], sb("h1", [P, HT, S])[:]
        h2 = o_natT[:]
        w_hi, w_lo = sb("w_hi", [P, SPLIT_WORDS], F32R), sb("w_lo", [P, SPLIT_WORDS], F32R)
        h0_hi, h0_lo, h1_hi, h1_lo, h2_hi, h2_lo, natT_hi, natT_lo = (
            sb(f"{n}_{part}", [P, t, S], F32R)[:]
            for n, t in (("h0", HT), ("h1", HT), ("h2", KT), ("natT", KT)) for part in ("hi", "lo"))
        junk = nat[:].bitcast(BF16)
        sums = sb("sums", [P, TT])
        rms_ms, rms_rs = sb("rms_ms", [P, TT]), sb("rms_rs", [P, TT])
        lt, rank, l1 = sb("lt", [P, TT, 4]), sb("rank", [P, TT, 4]), sb("l1", [P, TT])

        w_dma, in_dma = sem("w_dma"), sem("in_dma")
        layer_dma = {name: sem(f"{name}_dma") for name in SPLIT_W}
        down_dma = sem("down_dma")
        out_stored = [sem(f"out_stored{i}") for i in range(2)]
        s_sems, m_sems = (sem("s_full"), sem("s_free")), (sem("m_full"), sem("m_free"))
        rms_in, rms_out = sem("rms_in"), sem("rms_out")
        nat_ready = sem("nat_ready")
        gate_in, gate_exp = sem("gate_in"), sem("gate_exp")
        out_ready = sem("out_ready")
        w_cast, w_split = sem("w_cast"), sem("w_split")
        tile_split = sem("tile_split")
        dve_steps, waits_apart = sem("dve_steps"), sem("waits_apart")
        first, *others = SPLIT_W
        block = ctx.enter_context(nc.Block())

        @block.sync
        def _(sp):
            def load_inputs(b):
                for g in range(NG):
                    sp.dma_start(o_nat[:, :, g * HG * DK:(g + 1) * HG * DK],
                                 scr["os"][b * NG + (g + 1)].rearrange("p t h c -> p t (h c)")).then_inc(in_dma, 16)
                sp.dma_start(x2[:], scr["xn"][b]).then_inc(in_dma, 16)
                sp.dma_start(x1[:], scr["x1"][b]).then_inc(in_dma, 16)

            load_inputs(0)
            sp.dma_start(wo[:], w_self[:, :, 3 * D:3 * D + DOUT]).then_inc(w_dma, 16)
            sp.dma_start(gate_w[:], gate_t).then_inc(w_dma, 16)
            for stored in out_stored:
                sp.sem_inc(stored, 16)
            for n, name in enumerate(SPLIT_W):
                at, kts, w = FFN_W[name]
                before = [i for i, other in enumerate(list(SPLIT_W)[:n])
                          if STAGE_AT[other] < STAGE_AT[name] + kts * w
                          and STAGE_AT[name] < STAGE_AT[other] + FFN_W[other][1] * FFN_W[other][2]]
                if before:
                    sp.wait_ge(w_split, before[-1] + 1)
                sp.dma_start(stage[:, STAGE_AT[name]:STAGE_AT[name] + kts * w], ffn_w[:, at:at + kts * w])\
                    .then_inc(layer_dma[name], 16)
                if n == 2:
                    for down, at_down in DOWN_AT.items():
                        at, kts, w = FFN_W[down]
                        sp.dma_start(down_w[:, at_down:at_down + kts * w], ffn_w[:, at:at + kts * w])\
                            .then_inc(down_dma, 16)
            with sp.Fori(0, B // 2) as pair:
                for u in range(2):
                    b = pair * 2 + u
                    sp.wait_ge(nat_ready, b + 1)
                    apart(sp, waits_apart)
                    load_inputs(next_batch(b))
                    sp.wait_ge(out_ready, b + 1)
                    sp.dma_start(out[b], acc[:, u]).then_inc(out_stored[u], 16)
            for stored in out_stored:
                sp.wait_ge(stored, 16 * (B // 2 + 1))
            sp.wait_ge(in_dma, INPUTS * (B + 1))

        @block.gpsimd
        def _(pool):
            def root(b):
                pool.wait_ge(rms_in, b + 1)
                pool.tensor_tensor(rms_rs[:], rms_ms[:], half[:, 0:TT], ALU.pow).then_inc(rms_out, 1)

            root(0)
            with pool.Fori(0, B) as b:
                root(b + 1)

        @block.tensor
        def _(pe):
            mm, tr = pe.matmul, pe.transpose
            pe.wait_ge(w_dma, 32)

            def transposed(ring, full, src):
                for kt in range(KT):
                    bank = ring.acquire()
                    for tt in range(TT):
                        last = tr(bank[:, tt * P:(tt + 1) * P], src[:, tt, kt * P:(kt + 1) * P], ident_f)
                    last.then_inc(full, 1)

            def attention_transposed(mr, b):
                pe.wait_ge(in_dma, INPUTS * b + INPUTS)
                transposed(mr, m_sems[0], o_nat)

            def project_out(mr):
                mr.wait_released(mr.n)
                for tt in range(TT):
                    bank = mr.acquire()
                    for kt in range(KT):
                        last = mm(bank[:, 0:DOUT], o_natT[:, kt, tt * P:(tt + 1) * P], wo[:, kt, :],
                                  start=kt == 0, stop=kt == KT - 1)
                    last.then_inc(m_sems[0], 1)

            def rows_transposed(sr, b):
                pe.wait_ge(nat_ready, b + 1)
                transposed(sr, s_sems[0], nat)

            def gates(mr):
                bank = mr.acquire()
                for tt in range(TT):
                    for kt in range(KT):
                        last = mm(bank[:, 4 * tt:4 * tt + 4], natT[:, kt, tt * P:(tt + 1) * P], gate_w[:, kt, :],
                                  start=kt == 0, stop=kt == KT - 1)
                last.then_inc(m_sems[0], 1)

            def layer(name, hi, lo, ring, full):
                _, kts, w = FFN_W[name]
                at_hi = SPLIT_W[name][1]
                pe.wait_ge(w_split, list(SPLIT_W).index(name) + 1)
                for t in range(w // P):
                    bank = ring.acquire()
                    for kt in range(kts):
                        at_kt = kt * w + t * P
                        high = w_hi[:, at_hi + at_kt:at_hi + at_kt + P]
                        low = w_lo[:, at_hi + at_kt:at_hi + at_kt + P]
                        mm(bank[:, :], high, hi[:, kt, :], start=kt == 0, stop=False)
                        mm(bank[:, :], high, lo[:, kt, :], start=False, stop=False)
                        last = mm(bank[:, :], low, hi[:, kt, :], start=False, stop=kt == kts - 1)
                    last.then_inc(full, 1)

            def down(name, src, mr):
                at, (_, kts, w) = DOWN_AT[name], FFN_W[name]
                for tt in range(TT):
                    bank = mr.acquire()
                    for kt in range(kts):
                        last = mm(bank[:, 0:w], src[:, kt, tt * P:(tt + 1) * P], down_w[:, at + kt * w:at + (kt + 1) * w],
                                  start=kt == 0, stop=kt == kts - 1)
                    last.then_inc(m_sems[0], 1)

            sr, mr = Ring(pe, m.s_banks, s_sems, S_U, 0), Ring(pe, m.m_banks, m_sems, M_U, 0)
            attention_transposed(mr, 0)
            project_out(mr)
            rows_transposed(sr, 0)
            sr.wait_released(sr.n)
            gates(mr)
            assert (sr.n, mr.n) == (S_FRONT, M_FRONT)
            with pe.Fori(0, B) as b:
                sr = later_ring(pe, m.s_banks, s_sems, S_U, S_FRONT, b)
                mr = later_ring(pe, m.m_banks, m_sems, M_U, M_FRONT, b)
                pe.wait_ge(tile_split, b * SPLITS + KT)
                layer("e0_up", natT_hi, natT_lo, sr, s_sems[0])
                layer("e1_w1", natT_hi, natT_lo, sr, s_sems[0])
                layer("e1_w2", natT_hi, natT_lo, mr, m_sems[0])
                h1_done = mr.n
                sr.wait_released(HT)
                pe.wait_ge(down_dma, 16 * 4)
                down("e0_down", h0, mr)
                attention_transposed(mr, b + 1)
                layer("e2_l1", natT_hi, natT_lo, sr, s_sems[0])
                project_out(mr)
                mr.wait_released(h1_done)
                down("e1_down", h1, mr)
                pe.wait_ge(tile_split, b * SPLITS + (KT + HT))
                layer("e2_l2", h0_hi, h0_lo, sr, s_sems[0])
                layer("e3_down", natT_hi, natT_lo, sr, s_sems[0])
                pe.wait_ge(tile_split, b * SPLITS + (KT + 2 * HT))
                layer("e2_l3", h1_hi, h1_lo, sr, s_sems[0])
                h0_done = sr.n
                rows_transposed(sr, b + 1)
                natT_done = sr.n
                pe.wait_ge(tile_split, b * SPLITS + (2 * KT + 2 * HT))
                layer("e3_up", h2_hi, h2_lo, sr, s_sems[0])
                sr.wait_released(h0_done)
                down("e2_l4", h0, mr)
                sr.wait_released(natT_done)
                gates(mr)
                sr.wait_released(sr.n)
                down("e3_out", h1, mr)
                sr.end(), mr.end()

        @block.scalar
        def _(act):
            act.sem_inc(s_sems[1], N_S)

            def empty(sr, dst, tiles, func):
                for t in range(tiles):
                    bank = sr.take()
                    act.activation(dst[:, t, :], bank[:, 0:S], func).then_inc(s_sems[1], 1)

            def exp_gates(slot, b):
                act.wait_ge(gate_in, b + 1)
                act.activation(lg[:, slot], lg[:, slot], ACT.Exp).then_inc(gate_exp, 1)

            def cast_weights(name):
                (_, kts, w), at, at_hi = FFN_W[name], STAGE_AT[name], SPLIT_W[name][1]
                act.wait_ge(layer_dma[name], 16)
                act.activation(w_hi[:, at_hi:at_hi + kts * w], stage[:, at:at + kts * w], ACT.Copy).then_inc(w_cast, 1)

            cast_weights(first)
            empty(Ring(act, m.s_banks, s_sems, S_U, 0), natT, KT, ACT.Copy)
            exp_gates(0, 0)
            for name in others:
                cast_weights(name)
            with act.Fori(0, B // 2) as pair:
                for u in range(2):
                    b = pair * 2 + u
                    sr = later_ring(act, m.s_banks, s_sems, S_U, S_FRONT, b)
                    empty(sr, h0, HT, ACT.Gelu)
                    empty(sr, h1, HT, ACT.Silu)
                    empty(sr, h0, HT, ACT.Gelu)
                    empty(sr, h1, HT, ACT.Gelu)
                    empty(sr, h2, KT, ACT.Gelu)
                    empty(sr, h0, HT, ACT.Gelu)
                    empty(sr, natT, KT, ACT.Copy)
                    empty(sr, h1, HT, ACT.Gelu)
                    exp_gates(1 - u, b + 1)
                    sr.end()

        @block.vector
        def _(dve):
            dve.sem_inc(m_sems[1], N_M)

            def attention_transposed(mr):
                for kt in range(KT):
                    bank = mr.take()
                    dve.tensor_copy(o_natT[:, kt, :], bank).then_inc(m_sems[1], 1)

            def rows_x2(v, mr, slot, b, stored):
                dve.wait_ge(in_dma, INPUTS * b + INPUTS)
                for tt in range(TT):
                    bank = mr.take()
                    dve.tensor_tensor(x2[:, tt, ZERO_COLS:D], bank[:, 0:DOUT], x2[:, tt, ZERO_COLS:D], ALU.add)\
                        .then_inc(m_sems[1], 1)
                mr.wait_released(mr.n)
                for tt in range(TT):
                    v.step(dve.tensor_tensor_reduce(junk[:, tt, 0:D], x2[:, tt, :], x2[:, tt, :], 1.0, 0.0,
                                                    ALU.mult, ALU.add, sums[:, tt:tt + 1]))
                v.settle()
                dve.tensor_scalar(rms_ms[:], sums[:], 1.0 / D, RMS_EPS, ALU.mult, ALU.add).then_inc(rms_in, 1)
                dve.wait_ge(out_stored[slot], stored)
                for tt in range(TT):
                    v.step(dve.tensor_tensor(acc[:, slot, tt, :], x1[:, tt, :], x2[:, tt, :], ALU.add))
                v.settle()

            def rows_nat(v, b):
                dve.wait_ge(rms_out, b + 1)
                for tt in range(TT):
                    ins = dve.scalar_tensor_tensor(nat[:, tt, :], x2[:, tt, :], rms_rs[:, tt:tt + 1], n2w,
                                                   ALU.mult, ALU.mult)
                    ins.then_inc(nat_ready, 1) if tt == TT - 1 else v.step(ins)

            def logits(v, mr, slot):
                g = lg[:, slot]
                bank = mr.take()
                dve.tensor_scalar(g, bank[:, 0:4 * TT].rearrange("p (t e) -> p t e", e=4), FLT_MAX, -FLT_MAX,
                                  ALU.min, ALU.max).then_inc(m_sems[1], 1)
                mr.wait_released(mr.n)
                v(dve.tensor_reduce(l1[:], g, AX.X, ALU.max))
                dve.tensor_tensor(g, g, l1[:].unsqueeze(2).to_broadcast([P, TT, 4]), ALU.subtract).then_inc(gate_in, 1)

            def weights(v, slot, b):
                g = lg[:, slot]
                dve.wait_ge(gate_exp, b + 1)
                v(dve.tensor_reduce(l1[:], g, AX.X, ALU.add))
                v(dve.reciprocal(l1[:], l1[:]))
                v(dve.tensor_tensor(g, g, l1[:].unsqueeze(2).to_broadcast([P, TT, 4]), ALU.mult))
                v(dve.memset(rank[:], 0.0))
                for e in range(4):
                    if e > 0:
                        v.step(dve.tensor_tensor(lt[:, :, 0:e], g[:, :, e:e + 1].to_broadcast([P, TT, e]),
                                                 g[:, :, 0:e], ALU.is_gt))
                    if e < 3:
                        v.step(dve.tensor_tensor(lt[:, :, e + 1:4], g[:, :, e:e + 1].to_broadcast([P, TT, 3 - e]),
                                                 g[:, :, e + 1:4], ALU.is_ge))
                    v.settle()
                    if e > 0:
                        v.step(dve.tensor_tensor(rank[:, :, 0:e], rank[:, :, 0:e], lt[:, :, 0:e], ALU.add))
                    if e < 3:
                        v.step(dve.tensor_tensor(rank[:, :, e + 1:4], rank[:, :, e + 1:4], lt[:, :, e + 1:4], ALU.add))
                    v.settle()
                v(dve.tensor_scalar(rank[:], rank[:], 2.0, None, ALU.is_lt))
                v(dve.tensor_tensor(g, g, rank[:], ALU.mult))
                v(dve.tensor_reduce(l1[:], g, AX.X, ALU.add))
                v(dve.tensor_scalar(l1[:], l1[:], 1e-8, None, ALU.add))
                v(dve.reciprocal(l1[:], l1[:]))
                v(dve.tensor_tensor(g, g, l1[:].unsqueeze(2).to_broadcast([P, TT, 4]), ALU.mult))

            def down(mr, slot, e):
                for tt in range(TT):
                    bank = mr.take()
                    mr.wait_released(mr.n - TT)
                    dve.scalar_tensor_tensor(acc[:, slot, tt, ZERO_COLS:D], bank[:, 0:DOUT], lg[:, slot, tt, e:e + 1],
                                             acc[:, slot, tt, ZERO_COLS:D], ALU.mult, ALU.add).then_inc(m_sems[1], 1)

            def split_weights(name):
                (_, kts, w), at, at_hi = FFN_W[name], STAGE_AT[name], SPLIT_W[name][1]
                span = slice(at_hi, at_hi + kts * w)
                dve.wait_ge(w_cast, list(SPLIT_W).index(name) + 1)
                dve.tensor_tensor(w_lo[:, span], stage[:, at:at + kts * w], w_hi[:, span].bitcast(F32), ALU.subtract)\
                    .then_inc(w_split, 1)

            def split_tiles(v, src, hi, lo, tiles, uses):
                for t in range(tiles):
                    dve.wait_ge(s_sems[1], uses + (t + 1 + N_S))
                    v.step(dve.tensor_copy(hi[:, t, :], src[:, t, :]))
                v.settle()
                for t in range(tiles):
                    dve.tensor_tensor(lo[:, t, :], src[:, t, :], hi[:, t, :].bitcast(F32), ALU.subtract)\
                        .then_inc(tile_split, 1)

            v, mr = Chain(dve, dve_steps, 36, 0), Ring(dve, m.m_banks, m_sems, M_U, 0)
            attention_transposed(mr)
            rows_x2(v, mr, 0, 0, 16)
            rows_nat(v, 0)
            logits(v, mr, 0)
            split_tiles(v, natT, natT_hi, natT_lo, KT, 0)
            split_weights(first)
            weights(v, 0, 0)
            for name in others:
                split_weights(name)
            v.end()
            with dve.Fori(0, B // 2) as pair:
                for u in range(2):
                    b = pair * 2 + u
                    v, mr = Chain(dve, dve_steps, 46, b), later_ring(dve, m.m_banks, m_sems, M_U, M_FRONT, b)
                    v.base = b * 46 + 36
                    for t in range(HT):
                        bank = mr.take()
                        dve.wait_ge(s_sems[1], b * S_U + (S_FRONT + S_SILU + t + 1 + N_S))
                        dve.tensor_tensor(h1[:, t, :], bank, h1[:, t, :], ALU.mult).then_inc(m_sems[1], 1)
                    down(mr, u, 0)
                    attention_transposed(mr)
                    split_tiles(v, h0, h0_hi, h0_lo, HT, b * S_U + (S_FRONT + S_L1))
                    rows_x2(v, mr, 1 - u, b + 1, pair * 16 + (16 + 16 * u))
                    rows_nat(v, b + 1)
                    down(mr, u, 1)
                    split_tiles(v, h1, h1_hi, h1_lo, HT, b * S_U + (S_FRONT + S_L2))
                    split_tiles(v, h2, h2_hi, h2_lo, KT, b * S_U + (S_FRONT + S_E3))
                    split_tiles(v, natT, natT_hi, natT_lo, KT, b * S_U + (S_FRONT + S_ROWS))
                    down(mr, u, 2)
                    logits(v, mr, 1 - u)
                    down(mr, u, 3)
                    mr.wait_released(mr.n)
                    dve.sem_inc(out_ready, 1)
                    weights(v, 1 - u, b + 1)
                    v.end(), mr.end()


def xattn_ffn_kernel(nc, x, ctx_t, mask, w_cross, w_self, rows, bias_k, gate_t, ffn_w, ones, out):
    def scratch(name, shape, dt=F32):
        return nc.dram_tensor(f"scratch_{name}", shape, dt).ap()

    scr = {
        "k": scratch("k", (3, B, D, KEYS), BF16), "q": scratch("q", (B, PARTS, NG, HG * S), BF16),
        "v": scratch("v", (B, P, NG, NKT * HG * VW)),
        "mask": scratch("mask", (B, P, TT, KEYS), BF16), "flag": scratch("flag", (1, B), I32),
        "o": scratch("o", (B * NG + 1, P, TT, HG, DK)),
        "x1": scratch("x1", (B + 2, P, TT, D)), "xn": scratch("xn", (B + 1, P, TT, D)),
        "qs": scratch("qs", (B, PARTS, NG, HG * S), BF16), "ks": scratch("ks", (B, PARTS, NG, HG * S), BF16),
        "vs": scratch("vs", (B + 1, P, NG, TT * HG * VW)),
        "os": scratch("os", (B * NG + 1, P, TT, HG, DK)),
    }
    with ExitStack() as ctx:
        banks = [ctx.enter_context(nc.psum_tensor(f"bank{i}", [P, 512], F32))[:] for i in range(8)]

        def sb(name, shape, dt=F32):
            return ctx.enter_context(nc.sbuf_tensor(name, shape, dt))[:]

        consts = {
            "row_c": sb("row_c", [P, 7 * D]), "bk": sb("bk", [P, KT]),
            "identf": sb("identf", [P, P]), "identb": sb("identb", [P, P], BF16),
            "causal_q": sb("causal_q", [P, S], BF16),
            "causal_k": sb("causal_k", [P, P], BF16),
            "half": sb("half", [P, 2 * TT * H]),
        }
        setup_phase(nc, ctx, consts, rows, bias_k)
        prepare_phase(nc, ctx, banks, consts, x, ctx_t, mask, w_cross, scr)
        cross_phase(nc, ctx, banks, consts, scr, ones)
        self_inputs_phase(nc, ctx, banks, consts, x, w_cross, w_self, scr)
        self_phase(nc, ctx, banks, consts, scr, ones)
        expert_phase(nc, ctx, banks, consts, w_self, gate_t, ffn_w, scr, out)


def _tiles(w):
    k = w.shape[0] // P
    return w.reshape(k, P, w.shape[1]).transpose(1, 0, 2)


def kernel(**inputs):
    import numpy as np
    import concourse.bacc as bacc
    from concourse.bass_utils import run_bass_kernel_spmd

    a = {n: np.asarray(v) for n, v in inputs.items()}
    X, F = "L0_xattn_", "L0_ffn_"
    w_cross = np.stack([_tiles(a[X + n].T) for n in ("W_q", "W_k", "W_v", "W_o")], axis=1)
    w_self = np.concatenate([_tiles(a[F + n].T) for n in ("wq", "wk", "wv")]
                            + [_tiles(a[F + "wo"].T[:, ZERO_COLS:])], axis=2)
    rows = np.concatenate([a[X + "b_q"], a[X + "b_v"], a[X + "b_o"], a[F + "n1_w"], a[F + "n2_w"],
                           np.tile(a[F + "qn_w"], H), np.tile(a[F + "kn_w"], H)])
    cut = {"e0_down", "e1_down", "e2_l4", "e3_out"}
    ffn_w = np.concatenate([_tiles(a[F + n].T[:, ZERO_COLS:] if n in cut else a[F + n].T).reshape(P, -1)
                            for n in FFN_W], axis=1)
    arrays = {
        "x": a["x"],
        "ctx_t": a["ctx_1024"].transpose(0, 2, 1),
        "mask": a["mask_Bx1xSxS2_bf1"].reshape(B, S, KEYS).view(np.uint8),
        "w_cross": w_cross,
        "w_self": w_self,
        "rows": np.broadcast_to(rows, (P, rows.size)),
        "bias_k": a[X + "b_k"].reshape(KT, P).T,
        "gate_t": _tiles(a[F + "gate_w"].T),
        "ffn_w": ffn_w,
        "ones": np.ones((3, H * KEYS), dtype=mybir.dt.np(BF16)),
    }
    arrays = {n: np.ascontiguousarray(v) for n, v in arrays.items()}
    nc = bacc.Bacc("TRN2", target_bir_lowering=False, num_devices=1)
    t = {n: nc.dram_tensor(n, v.shape, mybir.dt.from_np(v.dtype), kind="ExternalInput").ap()
         for n, v in arrays.items()}
    out = nc.dram_tensor("out", (B, S, D), F32, kind="ExternalOutput").ap()
    xattn_ffn_kernel(
        nc, t["x"].rearrange("b (t p) d -> b p t d", p=P), t["ctx_t"].rearrange("b (k p) n -> b p k n", p=P),
        t["mask"].rearrange("b (t p) n -> b p t n", p=P), t["w_cross"], t["w_self"], t["rows"], t["bias_k"],
        t["gate_t"], t["ffn_w"], t["ones"].rearrange("r (h n) -> r h n", h=H), out.rearrange("b (t p) d -> b p t d", p=P))
    r = run_bass_kernel_spmd(nc, [arrays], core_ids=[0])
    return r.results[0]["out"]
```
